# Optimizing a Trainium2 kernel written in Bass

```python
import numpy as np
import jax
import jax.numpy as jnp

def _softmax(x, axis=-1):
    return jax.nn.softmax(x, axis=axis)

def _gelu(x):
    return jax.nn.gelu(x, approximate=True)

def _silu(x):
    return jax.nn.silu(x)

def _sigmoid(x):
    return jax.nn.sigmoid(x)

def _layernorm(x, axis=-1, eps=1e-05):
    m = jnp.mean(x, axis=axis, keepdims=True)
    v = jnp.var(x, axis=axis, keepdims=True)
    return (x - m) / jnp.sqrt(v + eps)

def _scatter_add(tgt, idx, src, axis=0):
    return tgt.at[idx].add(src)

def _segment_sum(src, seg, n):
    return jax.ops.segment_sum(src, seg, n)
kernel_name = 'mk_decoder_preln_d1_seqx_r4_ddf99a'

def setup_inputs(seed: int=0):
    np.random.seed(seed)
    _w = jnp.asarray

    def _rec_inputs():
        import jax
        import jax.numpy as jnp
        _rk = jax.random.key(seed)
        x = -0.0002928 + 1 * jax.random.normal(jax.random.fold_in(_rk, 1), (16, 256, 256), jnp.float32)
        _lenS = 256 - jax.random.randint(jax.random.fold_in(_rk, 7), (16,), 0, max(1, 256 // 4) + 1, jnp.int32)
        _lenS2 = 256 - jax.random.randint(jax.random.fold_in(_rk, 8), (16,), 0, max(1, 256 // 4) + 1, jnp.int32)
        _ctx_1024P = jax.random.normal(jax.random.fold_in(_rk, 11), (16, 16, 256), jnp.float32)
        _ctx_1024c = jax.random.dirichlet(jax.random.fold_in(_rk, 511), 0.3 * jnp.ones((16,), jnp.float32), (16, 256))
        _ctx_1024t = jnp.einsum('bsk,bkd->bsd', _ctx_1024c, _ctx_1024P)
        _ctx_1024t = _ctx_1024t * jax.lax.rsqrt(jnp.mean(jnp.square(_ctx_1024t)) + 1e-12) * 0.953939
        ctx_1024 = -1.39393e-06 + 0.999914 * (_ctx_1024t + 0.3 * jax.random.normal(jax.random.fold_in(_rk, 611), (16, 256, 256), jnp.float32))
        return (x, ctx_1024)
    x, ctx_1024 = _rec_inputs()

    def _L0_attn_setup():
        import jax, jax.numpy as jnp
        import numpy as np
        N_HEADS = 16
        ROPE_THETA = 10000.0

        def _rope_tables(T, d, dtype=jnp.float32):
            inv = 1.0 / ROPE_THETA ** (jnp.arange(0, d, 2, dtype=dtype) / d)
            t = jnp.arange(T, dtype=dtype)
            freqs = jnp.outer(t, inv)
            return (jnp.cos(freqs), jnp.sin(freqs))

        def _apply_rope(x, cos, sin):
            x_even = x[..., ::2]
            x_odd = x[..., 1::2]
            cos = cos[None, None]
            sin = sin[None, None]
            rot_even = x_even * cos - x_odd * sin
            rot_odd = x_odd * cos + x_even * sin
            out = jnp.stack([rot_even, rot_odd], axis=-1)
            return out.reshape(x.shape)
        key = jax.random.key(seed)
        k1, k2, k3 = jax.random.split(key, 3)
        B, T, C = (1, 1024, 256)
        x = jax.random.normal(k1, (B, T, C), dtype=jnp.float32)
        w_qkv = jax.random.normal(k2, (C, 3 * C), dtype=jnp.float32) * (1.0 / np.sqrt(C))
        w_out = jax.random.normal(k3, (C, C), dtype=jnp.float32) * (1.0 / np.sqrt(C))
        return {'x': x, 'w_qkv': w_qkv, 'w_out': w_out}
    _L0_attn_all = _L0_attn_setup()
    _L0_attn_in = {k: v for k, v in _L0_attn_all.items() if k in ('w_qkv', 'w_out')}
    del _L0_attn_all

    def _L0_xattn_setup():
        import jax, jax.numpy as jnp
        import numpy as np
        B, S, H, NH = (2, 512, 256, 4)
        DH = H // NH
        EPS = 1e-06

        def _parallel_stabilized(qh, kh, vh, ig, fg):
            log_fg = jax.nn.log_sigmoid(fg)
            cs = jnp.cumsum(log_fg, axis=2)
            ltr = jnp.tril(jnp.ones((qh.shape[2], qh.shape[2]), dtype=bool))
            log_fg_mat = jnp.where(ltr, cs - jnp.swapaxes(cs, 2, 3), -jnp.inf)
            log_D = log_fg_mat + jnp.swapaxes(ig, 2, 3)
            max_log_D = jnp.max(log_D, axis=-1, keepdims=True)
            D = jnp.exp(log_D - max_log_D)
            qk = jnp.einsum('bhsd,bhtd->bhst', qh, kh) / jnp.sqrt(jnp.float32(DH))
            C = qk * D
            normalizer = jnp.maximum(jnp.abs(jnp.sum(C, axis=-1, keepdims=True)), jnp.exp(-max_log_D))
            return jnp.einsum('bhst,bhtd->bhsd', C / (normalizer + EPS), vh)
        key = jax.random.key(seed)
        ks = jax.random.split(key, 6)
        q = jax.random.normal(ks[0], (B, S, H), dtype=jnp.float32)
        k = jax.random.normal(ks[1], (B, S, H), dtype=jnp.float32)
        v = jax.random.normal(ks[2], (B, S, H), dtype=jnp.float32)
        igate_kernel = jax.random.normal(ks[3], (3 * H, NH), dtype=jnp.float32) * 0.02
        fgate_kernel = jax.random.normal(ks[4], (3 * H, NH), dtype=jnp.float32) * 0.02
        igate_bias = jax.random.normal(ks[5], (NH,), dtype=jnp.float32) * 0.1
        fgate_bias = jnp.linspace(3.0, 6.0, NH, dtype=jnp.float32)
        outnorm_scale = jnp.ones((H,), dtype=jnp.float32)
        return {'q': q, 'k': k, 'v': v, 'igate_kernel': igate_kernel, 'igate_bias': igate_bias, 'fgate_kernel': fgate_kernel, 'fgate_bias': fgate_bias, 'outnorm_scale': outnorm_scale}
    _L0_xattn_all = _L0_xattn_setup()
    _L0_xattn_in = {k: v for k, v in _L0_xattn_all.items() if k in ('igate_kernel', 'igate_bias', 'fgate_kernel', 'fgate_bias', 'outnorm_scale')}
    del _L0_xattn_all

    def _L0_ffn_setup():
        import jax, jax.numpy as jnp
        import numpy as np
        TOP_K = 2
        key = jax.random.key(seed)
        ks = jax.random.split(key, 8)
        B, S, D = (2, 512, 256)
        N_r, N_s = (16, 2)
        u = jax.random.normal(ks[0], (B, S, D), dtype=jnp.float32)
        centroids = jax.random.normal(ks[1], (N_r, D), dtype=jnp.float32)
        expert_biases = jnp.zeros((N_r,), dtype=jnp.float32)
        Wr = jax.random.normal(ks[2], (N_r, D, D), dtype=jnp.float32) * (1.0 / np.sqrt(D))
        br = jax.random.normal(ks[3], (N_r, D), dtype=jnp.float32) * 0.01
        Ws = jax.random.normal(ks[4], (N_s, D, D), dtype=jnp.float32) * (1.0 / np.sqrt(D))
        bs = jax.random.normal(ks[5], (N_s, D), dtype=jnp.float32) * 0.01
        return {'u': u, 'centroids': centroids, 'expert_biases': expert_biases, 'Wr': Wr, 'br': br, 'Ws': Ws, 'bs': bs}
    _L0_ffn_all = _L0_ffn_setup()
    _L0_ffn_in = {k: v for k, v in _L0_ffn_all.items() if k in ('centroids', 'expert_biases', 'Wr', 'br', 'Ws', 'bs')}
    del _L0_ffn_all
    return {'x': x, 'ctx_1024': ctx_1024, 'L0_attn_w_qkv': _L0_attn_in['w_qkv'], 'L0_attn_w_out': _L0_attn_in['w_out'], 'L0_xattn_igate_kernel': _L0_xattn_in['igate_kernel'], 'L0_xattn_igate_bias': _L0_xattn_in['igate_bias'], 'L0_xattn_fgate_kernel': _L0_xattn_in['fgate_kernel'], 'L0_xattn_fgate_bias': _L0_xattn_in['fgate_bias'], 'L0_xattn_outnorm_scale': _L0_xattn_in['outnorm_scale'], 'L0_ffn_centroids': _L0_ffn_in['centroids'], 'L0_ffn_expert_biases': _L0_ffn_in['expert_biases'], 'L0_ffn_Wr': _L0_ffn_in['Wr'], 'L0_ffn_br': _L0_ffn_in['br'], 'L0_ffn_Ws': _L0_ffn_in['Ws'], 'L0_ffn_bs': _L0_ffn_in['bs']}

def reference(x, ctx_1024, L0_attn_w_qkv, L0_attn_w_out, L0_xattn_igate_kernel, L0_xattn_igate_bias, L0_xattn_fgate_kernel, L0_xattn_fgate_bias, L0_xattn_outnorm_scale, L0_ffn_centroids, L0_ffn_expert_biases, L0_ffn_Wr, L0_ffn_br, L0_ffn_Ws, L0_ffn_bs):
    import jax
    import jax.numpy as jnp

    def _L0_attn_ref(x, w_qkv, w_out):
        import jax, jax.numpy as jnp
        import numpy as np
        N_HEADS = 16
        ROPE_THETA = 10000.0

        def _rope_tables(T, d, dtype=jnp.float32):
            inv = 1.0 / ROPE_THETA ** (jnp.arange(0, d, 2, dtype=dtype) / d)
            t = jnp.arange(T, dtype=dtype)
            freqs = jnp.outer(t, inv)
            return (jnp.cos(freqs), jnp.sin(freqs))

        def _apply_rope(x, cos, sin):
            x_even = x[..., ::2]
            x_odd = x[..., 1::2]
            cos = cos[None, None]
            sin = sin[None, None]
            rot_even = x_even * cos - x_odd * sin
            rot_odd = x_odd * cos + x_even * sin
            out = jnp.stack([rot_even, rot_odd], axis=-1)
            return out.reshape(x.shape)
        B, T, C = x.shape
        H = N_HEADS
        D = C // H
        qkv = x @ w_qkv
        q, k, v = jnp.split(qkv, 3, axis=-1)
        to_heads = lambda t_: t_.reshape(B, T, H, D).transpose(0, 2, 1, 3)
        q, k, v = (to_heads(q), to_heads(k), to_heads(v))
        cos, sin = _rope_tables(T, D, x.dtype)
        q = _apply_rope(q, cos, sin)
        k = _apply_rope(k, cos, sin)
        scale = 1.0 / np.sqrt(D)
        att = jnp.einsum('bhtd,bhsd->bhts', q, k) * scale
        causal_mask = jnp.triu(jnp.ones((T, T), dtype=bool), 1)
        att = jnp.where(causal_mask[None, None], -jnp.inf, att)
        att = jax.nn.softmax(att, axis=-1)
        o = jnp.einsum('bhts,bhsd->bhtd', att, v)
        o = o.transpose(0, 2, 1, 3).reshape(B, T, C)
        return o @ w_out

    def _L0_xattn_ref(q, k, v, igate_kernel, igate_bias, fgate_kernel, fgate_bias, outnorm_scale):
        import jax, jax.numpy as jnp
        import numpy as np
        B, S, H, NH = (2, 512, 256, 4)
        DH = H // NH
        EPS = 1e-06

        def _parallel_stabilized(qh, kh, vh, ig, fg):
            log_fg = jax.nn.log_sigmoid(fg)
            cs = jnp.cumsum(log_fg, axis=2)
            ltr = jnp.tril(jnp.ones((qh.shape[2], qh.shape[2]), dtype=bool))
            log_fg_mat = jnp.where(ltr, cs - jnp.swapaxes(cs, 2, 3), -jnp.inf)
            log_D = log_fg_mat + jnp.swapaxes(ig, 2, 3)
            max_log_D = jnp.max(log_D, axis=-1, keepdims=True)
            D = jnp.exp(log_D - max_log_D)
            qk = jnp.einsum('bhsd,bhtd->bhst', qh, kh) / jnp.sqrt(jnp.float32(DH))
            C = qk * D
            normalizer = jnp.maximum(jnp.abs(jnp.sum(C, axis=-1, keepdims=True)), jnp.exp(-max_log_D))
            return jnp.einsum('bhst,bhtd->bhsd', C / (normalizer + EPS), vh)
        Bq, Sq, Hq = q.shape
        x = jnp.concatenate([q, k, v], axis=-1)
        ig = x @ igate_kernel + igate_bias
        fg = x @ fgate_kernel + fgate_bias
        ig = jnp.transpose(ig, (0, 2, 1))[..., None]
        fg = jnp.transpose(fg, (0, 2, 1))[..., None]
        qh = jnp.transpose(q.reshape(Bq, Sq, NH, DH), (0, 2, 1, 3))
        kh = jnp.transpose(k.reshape(Bq, Sq, NH, DH), (0, 2, 1, 3))
        vh = jnp.transpose(v.reshape(Bq, Sq, NH, DH), (0, 2, 1, 3))
        h = _parallel_stabilized(qh, kh, vh, ig, fg)
        mean = jnp.mean(h, axis=-1, keepdims=True)
        var = jnp.mean((h - mean) ** 2, axis=-1, keepdims=True)
        h_norm = (h - mean) * jax.lax.rsqrt(var + 1e-05)
        h_norm = h_norm * outnorm_scale.reshape(1, NH, 1, DH)
        out = jnp.transpose(h_norm, (0, 2, 1, 3)).reshape(Bq, Sq, Hq)
        return out

    def _L0_ffn_ref(u, centroids, expert_biases, Wr, br, Ws, bs):
        import jax, jax.numpy as jnp
        import numpy as np
        TOP_K = 2
        N_r = centroids.shape[0]
        N_s = Ws.shape[0]
        raw_scores = jnp.einsum('bsd,ed->bse', u, centroids)
        s = jax.nn.softmax(raw_scores + expert_biases, axis=-1)
        topk_vals, topk_idx = jax.lax.top_k(s, TOP_K)
        g_topk = jnp.sum(jax.nn.one_hot(topk_idx, N_r, dtype=s.dtype) * topk_vals[..., None], axis=-2)
        xe = jnp.einsum('bsd,eod->bseo', u, Wr) + br
        routed = jnp.einsum('bse,bseo->bso', g_topk, xe)
        shared = (jnp.einsum('bsd,eod->bso', u, Ws) + jnp.sum(bs, axis=0)) / N_s
        return u + routed + shared
    x = x + _L0_attn_ref(_layernorm(x, axis=-1), L0_attn_w_qkv, L0_attn_w_out)
    x = x + _L0_xattn_ref(_layernorm(x, axis=-1), ctx_1024, ctx_1024, L0_xattn_igate_kernel, L0_xattn_igate_bias, L0_xattn_fgate_kernel, L0_xattn_fgate_bias, L0_xattn_outnorm_scale)
    x = x + _L0_ffn_ref(_layernorm(x, axis=-1), L0_ffn_centroids, L0_ffn_expert_biases, L0_ffn_Wr, L0_ffn_br, L0_ffn_Ws, L0_ffn_bs)
    return x

_drawn_inputs = setup_inputs


def setup_inputs(seed=0):
    import zlib

    import numpy as np

    out = dict(_drawn_inputs(seed))
    spreads = {'L0_xattn_outnorm_scale': (1.0, 0.2), 'L0_ffn_expert_biases': (0.0, 0.8)}
    factors = {'L0_xattn_igate_bias': 64.0, 'L0_ffn_br': 8.0, 'L0_ffn_bs': 25.107}
    for name, (base, spread) in spreads.items():
        noise = np.random.default_rng([zlib.crc32(name.encode()), seed]).standard_normal(out[name].shape)
        drawn = base * np.exp(spread * noise) if base else spread * noise
        out[name] = jnp.asarray(drawn.astype(out[name].dtype))
    for name, factor in factors.items():
        out[name] = (out[name] * factor).astype(out[name].dtype)
    return out
```

```python
import concourse.bass as bass
from concourse import mybir
from contextlib import ExitStack
from collections import namedtuple

B, T, C = 16, 256, 256
NT = T // 128
CH = C // 128
NHA, DA = 16, C // 16
NP = NHA // 2
NHX, DX = 4, C // 4
NE, NS = 16, 2
TILES = B * NT
WS = 64.0
NEG = -1e30
PB = 4
JOBS = 6

Seq = namedtuple("Seq", "n half par")
Step = namedtuple("Step", "P Q R")


def decoder_layer(nc, x, ctx, w_qkv, w_out, igk, igb, fgk, fgb, onorm, centT, ebias, WrT, br, WsT, bs, rope_cos, rope_sin, out):
    f32, f16, bf16, u32 = mybir.dt.float32, mybir.dt.float16, mybir.dt.bfloat16, mybir.dt.uint32
    ALU, ACT, AX = mybir.AluOpType, mybir.ActivationFunctionType, mybir.AxisListType

    stack = ExitStack()
    with stack:
        def sb(name, shape, dt=f32):
            return stack.enter_context(nc.sbuf_tensor(name, shape, dt))

        def sem(name):
            return stack.enter_context(nc.semaphore(name))

        ident = sb("ident", [128, 128])
        ident16 = sb("ident16", [128, 128], f16)
        identb = sb("identb", [128, 128], bf16)
        causal = sb("causal", [128, 2, 128], bf16)
        zero_row = sb("zero_row", [NHX, T])
        headsel = sb("headsel", [NHX, NHX, 128])
        mhalf = sb("mhalf", [128, 8])
        iota16 = sb("iota16", [128, NE])
        cos_t = sb("cos_t", [128, NT, DA])
        sin_t = sb("sin_t", [128, NT, DA])
        wstage = sb("wstage", [128, CH, 3 * C])
        wostage = sb("wostage", [128, CH, C])
        wqkv_h = sb("wqkv_h", [128, CH, 3 * C], f16)
        wqkv_l = sb("wqkv_l", [128, CH, 3 * C], f16)
        wo_h = sb("wo_h", [128, CH, C], f16)
        wo_l = sb("wo_l", [128, CH, C], f16)
        gstage = sb("gstage", [128, 2, 3 * CH, NHX])
        gsum = sb("gsum", [128, 2 * CH, 36])
        gw_h = sb("gw_h", [128, 2 * CH, 36], f16)
        gw_l = sb("gw_l", [128, 2 * CH, 36], f16)
        gbias = sb("gbias", [36, 1])
        onorm_bc = sb("onorm_bc", [128, C])
        cent32 = sb("cent32", [128, CH, NE])
        cent_h = sb("cent_h", [128, CH, NE], f16)
        cent_l = sb("cent_l", [128, CH, NE], f16)
        ebias_bc = sb("ebias_bc", [128, NE])
        ball = sb("ball", [NE + NS, C])
        estage = sb("estage", [128, 2, CH, C])
        ew_h = sb("ew_h", [128, CH, NE + 1, C], f16)
        ew_l = sb("ew_l", [128, CH, NE + 1, C], f16)

        xin = [sb(f"xin{i}", [128, NT, C]) for i in range(2)]
        p_stats = sb("p_stats", [128, NT, 6])
        p_mv = sb("p_mv", [128, NT, 2])
        p_ve = sb("p_ve", [128, NT])
        p_rs = sb("p_rs", [128, NT])
        p_xn_t = sb("p_xn_t", [128, NT, C])
        xT_h = sb("xT_h", [128, CH, T], f16)
        xT_l = sb("xT_l", [128, CH, T], f16)
        rope_a = sb("rope_a", [128, 2 * C])
        rope_b = sb("rope_b", [128, 2 * C])
        rot = sb("rot", [128, 2, NHA, DA])
        qst = [sb(f"qst{i}", [128, NT, NHA, 64], f16) for i in range(2)]
        kst = sb("kst", [128, NT, NHA, 64], f16)
        qT = [sb(f"qT{i}", [128, NP, T], f16) for i in range(2)]
        kT = [sb(f"kT{i}", [128, NP, T], f16) for i in range(2)]
        v17 = [sb(f"v17_{i}", [128, NT, NHA, DA + 1]) for i in range(2)]

        xres = [sb(f"xres{i}", [128, NT, C]) for i in range(2)]
        qmT = sb("qmT", [128, NP, T], f16)
        probs = [sb(f"probs{j}", [128, 1024]) for j in range(PB)]
        rec = sb("rec", [128, NT, NHA])
        o_n = sb("o_n", [128, NT, C])
        oT_h = sb("oT_h", [128, NT, CH, 128], f16)
        oT_l = sb("oT_l", [128, NT, CH, 128], f16)
        x1 = [sb(f"x1_{i}", [128, NT, C]) for i in range(2)]

        ctx_t = [sb(f"ctx{i}", [128, NT, C]) for i in range(2)]
        ctx65 = [sb(f"ctx65_{i}", [128, NT, NHX, DX + 1]) for i in range(2)]
        r_stats = sb("r_stats", [128, NT, 6])
        r_mv = sb("r_mv", [128, NT, 2])
        r_ve = sb("r_ve", [128, NT])
        r_rs = sb("r_rs", [128, NT])
        r_xn_t = sb("r_xn_t", [128, NT, C])
        tr_h = sb("tr_h", [128, 2, CH, T], f16)
        tr_l = sb("tr_l", [128, 2, CH, T], f16)
        fg = sb("fg", [NHX, T])
        fg_a = sb("fg_a", [NHX, T])
        fg_e = fg_l = fg_a
        ig = sb("ig", [NHX, T])
        lsig = fg
        cs = sb("cs", [NHX, T])
        am = sb("am", [36, T])
        cmax = sb("cmax", [NHX, T])
        acol = sb("acol", [128, NT, NHX])
        emd = sb("emd", [128, NT, NHX])
        E_t = wstage[:].rearrange("p c n -> p (c n)").rearrange("p (h q) -> p h q", h=NHX)
        C_t = sb("C_t", [128, NHX, 3 * 128])
        nrm = sb("nrm", [128, NT, NHX])
        nre = sb("nre", [128, NT, NHX])
        nrr = sb("nrr", [128, NT, NHX])
        hh = sb("hh", [128, NT, NHX, DX])
        h_stats = sb("h_stats", [128, NT * NHX, 6])
        h_mv = sb("h_mv", [128, NT * NHX, 2])
        h_ve = sb("h_ve", [128, NT * NHX])
        h_rs = sb("h_rs", [128, NT * NHX])
        hc = sb("hc", [128, NT * NHX, DX])
        hn = hc
        hs = wostage
        x2 = sb("x2", [128, TILES, C])

        f_stats = sb("f_stats", [128, 6])
        f_mv = sb("f_mv", [128, 2])
        f_ve = sb("f_ve", [128, 1])
        f_rs = sb("f_rs", [128, 1])
        u_t = p_xn_t[:, 0]
        xu = [xin[1][:, i] for i in range(2)]
        uT_h = [xT_h[:, :, bass.ts(i, 128)] for i in range(2)]
        uT_l = [xT_l[:, :, bass.ts(i, 128)] for i in range(2)]
        lg = sb("lg", [128, NE])
        lgs = sb("lgs", [128, NE])
        mx8 = sb("mx8", [128, 8])
        ex = sb("ex", [128, NE])
        exsum = sb("exsum", [128, 1])
        exrec = sb("exrec", [128, 1])
        sm = sb("sm", [128, NE])
        top8 = sb("top8", [128, 8])
        idx8 = sb("idx8", [128, 8], u32)
        idxf = sb("idxf", [128, 2])
        g1 = sb("g1", [128, NE])
        g2 = sb("g2", [128, NE])
        gate = sb("gate", [128, NE + NS])
        gsc = [sb(f"gsc{i}", [128, NE]) for i in range(2)]
        gT = [sb(f"gT{i}", [NE + NS, 128]) for i in range(2)]
        accA = rope_a[:].rearrange("p (a c) -> p a c", a=2)
        accB = rope_b[:].rearrange("p (a c) -> p a c", a=2)
        fin = [xin[0][:, i] for i in range(2)]

        ring = [stack.enter_context(nc.psum_tensor(f"ring{i}", [128, 1024], f32)) for i in range(2)]
        proj = stack.enter_context(nc.psum_tensor("proj", [128, 512], f32))
        tp = stack.enter_context(nc.psum_tensor("tp", [128, 512], f32))
        obank = stack.enter_context(nc.psum_tensor("obank", [128, 512], f32))
        rbank = stack.enter_context(nc.psum_tensor("rbank", [128, 512], f32))
        tp16 = tp[:, :].bitcast(f16).rearrange("p (a q) -> p a q", a=NP)

        w_in, pool_ready, w_hi, w_lo, g_sum, zeros_in = map(sem, ("w_in", "pool_ready", "w_hi", "w_lo", "g_sum", "zeros_in"))
        misc_in, dve_held, pe_held, pool_held = map(sem, ("misc_in", "dve_held", "pe_held", "pool_held"))
        x_in, xres_in, ctx_in = ([sem(f"{n}{i}") for i in range(2)] for n in ("x_in", "xres_in", "ctx_in"))
        names = ("p_var p_rstd p_xn p_xT p_xh p_xl p_qk p_roped p_rot p_hi p_lo p_tr p_te p_vp p_vev dve_p pool_p "
                 "s_done m_done q_rt q_rte t_done e_done k_done av_done n_done o_t o_h o_l w_done x1_done dve_q "
                 "c_cp r_var r_rstd r_xn r_tr r_th r_tl r_g r_ga r_sc r_at r_ac r_mb r_e r_em r_qk r_c r_h r_hn "
                 "r_gv r_gr r_n x2_done dve_r act_r pool_r").split()
        (p_var, p_rstd, p_xn, p_xT, p_xh, p_xl, p_qk, p_roped, p_rot, p_hi, p_lo, p_tr, p_te, p_vp, p_vev, dve_p, pool_p,
         s_done, m_done, q_rt, q_rte, t_done, e_done, k_done, av_done, n_done, o_t, o_h, o_l, w_done, x1_done, dve_q,
         c_cp, r_var, r_rstd, r_xn, r_tr, r_th, r_tl, r_g, r_ga, r_sc, r_at, r_ac, r_mb, r_e, r_em, r_qk, r_c, r_h, r_hn,
         r_gv, r_gr, r_n, x2_done, dve_r, act_r, pool_r) = map(sem, names)
        e_in = [sem("e_in0"), sem("e_in1")]
        e_ws, e_hi, e_lo = map(sem, ("e_ws", "e_hi", "e_lo"))
        (f_var, f_rstd, f_u, f_xu, f_ut, f_uh, f_ul, f_lg, f_sh, f_ex, f_g, f_gt, f_gte, f_base, f_pair, f_comb, f_fin,
         f_baseread, dve_f, pool_f) = map(sem, "f_var f_rstd f_u f_xu f_ut f_uh f_ul f_lg f_sh f_ex f_g f_gt f_gte f_base f_pair f_comb f_fin f_baseread dve_f pool_f".split())
        out_sent = [sem("out_sent0"), sem("out_sent1")]

        def wait(eng, s, value):
            if not isinstance(value, int) or value > 0:
                eng.wait_ge(s, value)

        def held(eng, s):
            eng.sem_inc(s, 1)

        def step(i):
            return Step(*(Seq(i - d, (i - d) // 2, (i - d) % 2) if 0 <= i - d < B else None for d in range(3)))

        PEEL, STEPS = 4, B + 2

        def pipeline(body, engine):
            for i in range(PEEL):
                body(step(i))
            with engine.Fori(PEEL // 2, B // 2) as it:
                for u in range(2):
                    body(Step(*(Seq(it * 2 + (u - d), it + (u - d) // 2, (u - d) % 2) for d in range(3))))
            for i in range(B, STEPS):
                body(step(i))

        RING = [("s0", "Q", m_done, 6, 1), ("s1", "Q", m_done, 6, 2), ("tr", "R", r_tl, 1, 1), ("s2", "Q", m_done, 6, 3),
                ("t0", "Q", e_done, 6, 1), ("s3", "Q", m_done, 6, 4), ("t1", "Q", e_done, 6, 2), ("s4", "Q", m_done, 6, 5),
                ("s5", "Q", m_done, 6, 6), ("mb", "R", r_e, 1, 1), ("t2", "Q", e_done, 6, 3), ("qk0", "R", r_c, 2, 1),
                ("t3", "Q", e_done, 6, 4), ("qk1", "R", r_c, 2, 2), ("t4", "Q", e_done, 6, 5), ("t5", "Q", e_done, 6, 6)]
        RINGPOS = {u[0]: n % 2 for n, u in enumerate(RING)}
        USES = {
            "ring0": RING[0::2], "ring1": RING[1::2],
            "tp": [("xT", "P", p_xl, 1, 1), ("reT0", "Q", q_rte, 2, 1), ("tq0", "P", p_te, 4, 1), ("tk0", "P", p_te, 4, 2),
                   ("reT1", "Q", q_rte, 2, 2), ("oT0", "Q", o_l, 2, 1), ("tq1", "P", p_te, 4, 3), ("tk1", "P", p_te, 4, 4),
                   ("oT1", "Q", o_l, 2, 2)],
            "proj": [("qk0", "P", p_roped, 2, 1), ("v0", "P", p_vev, 2, 1), ("qk1", "P", p_roped, 2, 2), ("v1", "P", p_vev, 2, 2),
                     ("w0", "Q", x1_done, 2, 1), ("w1", "Q", x1_done, 2, 2)],
            "obank": [("o0", "Q", n_done, 2, 1), ("o1", "Q", n_done, 2, 2)],
            "rbank": [("gates", "R", r_ga, 1, 1), ("aT", "R", r_ac, 1, 1), ("h0", "R", r_hn, 2, 1), ("h1", "R", r_hn, 2, 2)],
        }

        def bank_free(pe, bank, name, st):
            uses = USES[bank]
            at = [u[0] for u in uses].index(name)
            for back in range(1, len(uses) + 1):
                _, stream, s, per, count = uses[(at - back) % len(uses)]
                seq, ago = getattr_stream(st, stream), int(at - back < 0)
                if seq is None:
                    if ago == 0:
                        continue
                    seq = getattr_stream(st, stream, True)
                    if seq is None:
                        continue
                n = seq.n - ago
                if isinstance(n, int) and not 0 <= n < B:
                    continue
                wait(pe, s, n * per + count)
                return

        def getattr_stream(st, stream, beyond=False):
            d = "PQR".index(stream)
            if st[d] is not None or not beyond:
                return st[d]
            for k in range(3):
                if st[k] is not None:
                    n = st[k].n + k - d
                    return Seq(n, n // 2, n % 2)
            return None

        block = stack.enter_context(nc.Block())

        x_v = x.rearrange("b (t p) c -> b p t c", p=128)
        ctx_v = ctx.rearrange("b (t p) c -> b p t c", p=128)
        out_v = out.rearrange("b (t p) c -> (b t) p c", p=128)
        EXPERTS = NE + NS

        @block.sync
        def _(sp):
            sp.dma_start(xin[0][:], x_v[0]).then_inc(x_in[0], 16)
            sp.dma_start(wstage[:], w_qkv.rearrange("(c p) n -> p c n", p=128)).then_inc(w_in, 16)
            sp.dma_start(cos_t[:], rope_cos).then_inc(w_in, 16)
            sp.dma_start(sin_t[:], rope_sin).then_inc(w_in, 16)
            sp.dma_start(wostage[:], w_out.rearrange("(c p) n -> p c n", p=128)).then_inc(w_in, 16)
            sp.dma_start(gstage[:, 0], igk.rearrange("(c p) n -> p c n", p=128)).then_inc(w_in, 16)
            sp.dma_start(gstage[:, 1], fgk.rearrange("(c p) n -> p c n", p=128)).then_inc(w_in, 16)
            sp.dma_start(cent32[:], centT.rearrange("(c p) n -> p c n", p=128)).then_inc(w_in, 16)
            sp.wait_ge(zeros_in, 1)
            sp.dma_start(gbias[0:NHX, :], igb.rearrange("(h a) -> h a", a=1)).then_inc(misc_in, 16)
            sp.dma_start(gbias[32:32 + NHX, :], fgb.rearrange("(h a) -> h a", a=1)).then_inc(misc_in, 16)
            sp.dma_start(onorm_bc[:], onorm.partition_broadcast(128)).then_inc(misc_in, 16)
            sp.dma_start(ebias_bc[:], ebias.partition_broadcast(128)).then_inc(misc_in, 16)
            sp.dma_start(ball[0:NE, :], br).then_inc(misc_in, 16)
            sp.dma_start(ball[NE:NE + NS, :], bs).then_inc(misc_in, 16)

            def expert(k):
                if k >= 2:
                    sp.wait_ge(e_lo, k - 1)
                src = WrT[:, k] if k < NE else WsT[:, k - NE]
                sp.dma_start(estage[:, k % 2], src.rearrange("(c p) o -> p c o", p=128)).then_inc(e_in[k % 2], 16)

            sent = [0]

            def body(st):
                if st.P is not None:
                    b = st.P
                    if not (isinstance(b.n, int) and b.n == 0):
                        wait(sp, p_xn, b.n - 1)
                        sp.dma_start(xin[b.par][:], x_v[b.n]).then_inc(x_in[b.par], 16)
                    wait(sp, x1_done, 2 * (b.n - 1))
                    sp.dma_start(xres[b.par][:], x_v[b.n]).then_inc(xres_in[b.par], 16)
                    wait(sp, r_tr, b.n - 1)
                    wait(sp, c_cp, b.n - 1)
                    sp.dma_start(ctx_t[b.par][:], ctx_v[b.n]).then_inc(ctx_in[b.par], 16)
                if (st.P or st.R) and isinstance((st.P or st.R).n, int):
                    for _ in range(6):
                        if sent[0] < EXPERTS:
                            expert(sent[0])
                            sent[0] += 1

            pipeline(body, nc.sync)
            while sent[0] < EXPERTS:
                expert(sent[0])
                sent[0] += 1

            with nc.sync.Fori(0, TILES // 2) as it:
                for u in range(2):
                    sp.wait_ge(f_fin, it * 2 + (u + 1))
                    sp.dma_start(out_v[it * 2 + u], fin[u]).then_inc(out_sent[u], 16)
            for u in range(2):
                sp.wait_ge(out_sent[u], 16 * (TILES // 2))

        @block.gpsimd
        def _(pool):
            g = nc.gpsimd
            chain = {}

            def link(ins, s, seq, per, key):
                chain[key] = chain.get(key, 0) % per + 1
                ins.then_inc(s, 1)
                pool.wait_ge(s, seq.n * per + chain[key])

            g.memset(ident[:], 0.0)
            g.memset(gsum[:], 0.0)
            g.memset(gbias[:], 0.0).then_inc(zeros_in, 1)
            pool.wait_ge(zeros_in, 1)
            g.affine_select(out=ident[:], in_=ident[:], compare_op=ALU.not_equal, fill=1.0, base=0,
                            pattern=[[-1, 128]], channel_multiplier=1).then_inc(zeros_in, 1)
            g.memset(causal[:], 0.0)
            g.memset(headsel[:], 1.0)
            g.memset(mhalf[:], -0.5)
            g.memset(am[:], 0.0)
            g.memset(zero_row[:], 0.0)
            g.memset(gate[:], 0.5)
            g.memset(kst[:], 0.0)
            for i in range(2):
                g.memset(qst[i][:], 0.0)
                g.memset(v17[i][:], 1.0)
                g.memset(ctx65[i][:], 1.0)
            g.iota(iota16[:], pattern=[[1, NE]], base=0, channel_multiplier=0,
                   allow_small_or_imprecise_dtypes=True).then_inc(zeros_in, 1)
            pool.wait_ge(zeros_in, 3)
            g.memset(kst[:, :, :, 3 * DA:3 * DA + 1], 1.0)
            g.tensor_copy(ident16[:], ident[:])
            g.tensor_copy(identb[:], ident[:])
            g.affine_select(out=causal[:], in_=causal[:], compare_op=ALU.is_ge, fill=NEG, base=0,
                            pattern=[[0, 2], [-1, 128]], channel_multiplier=1)
            g.affine_select(out=headsel[:], in_=headsel[:], compare_op=ALU.is_equal, fill=0.0, base=0,
                            pattern=[[-1, NHX], [0, 128]], channel_multiplier=1).then_inc(pool_ready, 1)

            def rstd(dst, ve, var, n, eps, ready, value, linked, done):
                pool.wait_ge(ready, value)
                held(pool, pool_held)
                linked(g.tensor_scalar(ve, var, eps, None, ALU.add))
                g.tensor_tensor(dst, ve, mhalf[:, 0:n], ALU.pow).then_inc(done, 1)

            def p_rstd_step(b):
                rstd(p_rs[:], p_ve[:], p_mv[:, :, 1], NT, 1e-5, p_var, b.n + 1,
                     lambda i: link(i, pool_p, b, 1, "p"), p_rstd)

            def r_rstd_step(b):
                rstd(r_rs[:], r_ve[:], r_mv[:, :, 1], NT, 1e-5, r_var, b.n + 1,
                     lambda i: link(i, pool_r, b, 3, "r"), r_rstd)

            def p_hi_copy(b, t):
                pool.wait_ge(p_rot, 2 * b.n + t + 1)
                wait(pool, q_rt, 2 * (b.n - 2) + t + 1)
                wait(pool, p_tr, 4 * (b.n - 1) + 2 * t + 2)
                held(pool, pool_held)
                q_to = qst[b.par][:, t].rearrange("p h (a s) -> p h a s", a=2)[:, :, :, 0:DA]
                k_to = kst[:, t, :, 0:2 * DA].rearrange("p h (a s) -> p h a s", a=2)
                g.tensor_copy(q_to, rot[:, 0].unsqueeze(2).broadcast_to([128, NHA, 2, DA]))
                g.tensor_copy(k_to, rot[:, 1].unsqueeze(2).broadcast_to([128, NHA, 2, DA])).then_inc(p_hi, 1)

            def mask_probs(b, j):
                pool.wait_ge(e_done, JOBS * b.n + j + 1)
                held(pool, pool_held)
                if j < 2:
                    view = probs[j % PB][:, :].rearrange("p (a q) -> p a q", q=128)
                    pattern = [[0, 8], [1, 128]]
                else:
                    view = probs[j % PB][:, :].rearrange("p (a k q) -> p a k q", k=2, q=128)[:, :, 1, :]
                    pattern = [[0, 4], [1, 128]]
                g.affine_select(out=view, in_=view, compare_op=ALU.is_ge, fill=0.0, base=0, pattern=pattern,
                                channel_multiplier=-1).then_inc(k_done, 1)

            def ctx_copy(b):
                pool.wait_ge(ctx_in[b.par], 16 * (b.half + 1))
                wait(pool, r_h, 2 * (b.n - 1))
                held(pool, pool_held)
                for t in range(NT):
                    last = g.tensor_copy(ctx65[b.par][:, t, :, 0:DX], ctx_t[b.par][:, t].rearrange("p (h d) -> p h d", h=NHX))
                last.then_inc(c_cp, 1)

            def mask_E(b):
                pool.wait_ge(r_e, b.n + 1)
                held(pool, pool_held)
                for k in (0, 2):
                    view = E_t[:, :, bass.ts(k, 128)]
                    last = g.affine_select(out=view, in_=view, compare_op=ALU.is_ge, fill=0.0, base=0,
                                           pattern=[[0, NHX], [1, 128]], channel_multiplier=-1)
                last.then_inc(r_em, 1)

            def h_rstd_step(b):
                rstd(h_rs[:], h_ve[:], h_mv[:, :, 1], NT * NHX, 1e-5, r_gv, b.n + 1,
                     lambda i: link(i, pool_r, b, 3, "r"), r_gr)

            def finish_r(b):
                pool.wait_ge(r_n, b.n + 1)
                link(g.tensor_tensor(hs[:], hn[:].rearrange("p (t h) d -> p t (h d)", t=NT),
                                     onorm_bc[:].unsqueeze(1).broadcast_to([128, NT, C]), ALU.mult), pool_r, b, 3, "r")
                g.tensor_tensor(x2[:, bass.ts(b.n, NT), :], hs[:], x1[b.par][:], ALU.add).then_inc(x2_done, 1)

            split = [0]

            def split_expert(k):
                if k == NE:
                    return split_shared()
                pool.wait_ge(e_in[k % 2], 16 * (k // 2 + 1))
                w, hi, lo = estage[:, k % 2], ew_h[:, :, k], ew_l[:, :, k]
                g.tensor_scalar(w, w, WS, None, ALU.mult).then_inc(e_ws, 1)
                pool.wait_ge(e_ws, k + 1)
                g.tensor_copy(hi, w).then_inc(e_hi, 1)
                pool.wait_ge(e_hi, k + 1)
                g.tensor_tensor(lo, w, hi, ALU.subtract).then_inc(e_lo, 1)

            def split_shared():
                for i in range(2):
                    pool.wait_ge(e_in[i], 16 * (NE // 2 + 1))
                w, hi, lo = estage[:, 0], ew_h[:, :, NE], ew_l[:, :, NE]
                g.tensor_tensor(w, w, estage[:, 1], ALU.add).then_inc(e_ws, 1)
                pool.wait_ge(e_ws, NE + 1)
                g.tensor_scalar(w, w, WS, None, ALU.mult).then_inc(e_ws, 1)
                pool.wait_ge(e_ws, NE + 2)
                g.tensor_copy(hi, w).then_inc(e_hi, 1)
                pool.wait_ge(e_hi, NE + 1)
                g.tensor_tensor(lo, w, hi, ALU.subtract).then_inc(e_lo, 1)

            def some_experts(count):
                for _ in range(count):
                    if split[0] <= NE:
                        split_expert(split[0])
                        split[0] += 1

            pool.wait_ge(misc_in, 96)

            def body(st):
                P, Q, R = st
                peeled = isinstance((P or R).n, int)
                if P: p_rstd_step(P)
                if R:
                    r_rstd_step(R)
                    ctx_copy(R)
                if P: p_hi_copy(P, 0)
                if Q: mask_probs(Q, 0)
                if Q: mask_probs(Q, 1)
                if peeled: some_experts(2)
                if R: mask_E(R)
                if P: p_hi_copy(P, 1)
                if peeled: some_experts(2)
                for j in range(2, JOBS):
                    if Q: mask_probs(Q, j)
                if R:
                    h_rstd_step(R)
                    finish_r(R)
                if peeled: some_experts(2)

            pipeline(body, nc.gpsimd)
            some_experts(EXPERTS)

            def f_rstd_step(n):
                rstd(f_rs[:], f_ve[:], f_mv[:, 1:2], 1, 1e-5, f_var, n + 1,
                     lambda i: (i.then_inc(pool_f, 1), pool.wait_ge(pool_f, n + 1)), f_rstd)

            f_rstd_step(0)
            with nc.gpsimd.Fori(0, TILES // 2 - 1) as it:
                for u in range(2):
                    f_rstd_step(it * 2 + (u + 1))
            f_rstd_step(TILES - 1)

        @block.scalar
        def _(act):
            a = nc.scalar
            a.preload_act_table_set("natural_log_exp_and_others")
            chain = {}

            def link(ins, seq):
                chain["r"] = chain.get("r", 0) % 3 + 1
                ins.then_inc(act_r, 1)
                act.wait_ge(act_r, 3 * seq.n + chain["r"])

            act.wait_ge(w_in, 112)
            act.wait_ge(g_sum, 2)
            for c in range(CH):
                a.activation(wqkv_h[:, c], wstage[:, c], ACT.Copy, scale=WS)
            a.activation(wo_h[:], wostage[:], ACT.Copy, scale=WS)
            a.activation(gw_h[:], gsum[:], ACT.Copy, scale=WS)
            a.activation(cent_h[:], cent32[:], ACT.Copy, scale=WS).then_inc(w_hi, 1)

            def xT_hi(b):
                act.wait_ge(p_xT, b.n + 1)
                wait(act, p_vp, 2 * b.n)
                a.activation(xT_h[:].rearrange("p c q -> p (c q)"), tp[:], ACT.Copy).then_inc(p_xh, 1)

            def transposed(b, n):
                t, is_k = divmod(n, 2)
                act.wait_ge(p_tr, 4 * b.n + n + 1)
                wait(act, t_done if is_k else s_done, JOBS * (b.n - 1))
                dst = (kT if is_k else qT)[b.par]
                a.activation(dst[:, :, bass.ts(t, 128)], tp16, ACT.Copy).then_inc(p_te, 1)

            def v_out(b, t):
                act.wait_ge(p_vp, 2 * b.n + t + 1)
                wait(act, av_done, JOBS * (b.n - 1))
                a.activation(v17[b.par][:, t, :, 0:DA], proj[:, 0:C].rearrange("p (h d) -> p h d", h=NHA), ACT.Copy,
                             scale=1.0 / WS).then_inc(p_vev, 1)

            def retransposed(b, t):
                act.wait_ge(q_rt, 2 * b.n + t + 1)
                wait(act, t_done, JOBS * (b.n - 1) + (2 if t == 0 else JOBS))
                a.activation(qmT[:, :, bass.ts(t, 128)], tp16, ACT.Copy).then_inc(q_rte, 1)

            def exp_job(b, j):
                act.wait_ge(t_done, JOBS * b.n + j + 1)
                wait(act, av_done, JOBS * b.n + j - PB + 1 if j >= PB else JOBS * (b.n - 1) + (j + PB if j + PB < JOBS else j) + 1)
                a.activation(probs[j % PB][:], ring[RINGPOS[f"t{j}"]][:], ACT.Exp, scale=DA ** -0.5).then_inc(e_done, 1)

            def oT_hi(b, t):
                act.wait_ge(o_t, 2 * b.n + t + 1)
                wait(act, w_done, 2 * (b.n - 1) + t + 1)
                a.activation(oT_h[:, t].rearrange("p c q -> p (c q)"), tp[:, 0:C], ACT.Copy).then_inc(o_h, 1)

            def tr_hi(b):
                act.wait_ge(r_tr, b.n + 1)
                wait(act, r_qk, 2 * b.n)
                a.activation(tr_h[:].rearrange("p s c q -> p (s c q)"), ring[RINGPOS["tr"]][:], ACT.Copy).then_inc(r_th, 1)

            def gate_acts(b):
                act.wait_ge(r_g, b.n + 1)
                wait(act, r_sc, b.n)
                link(a.activation(fg[:], rbank[32:32 + NHX, 0:T], ACT.Identity, scale=1.0 / WS, bias=gbias[32:32 + NHX, :]), b)
                a.activation(ig[:], rbank[0:NHX, 0:T], ACT.Identity, scale=1.0 / WS, bias=gbias[0:NHX, :])
                link(a.activation(fg_a[:], fg[:], ACT.Abs), b)
                link(a.activation(fg_e[:], fg_a[:], ACT.Exp, scale=-1.0), b)
                a.activation(fg_l[:], fg_e[:], ACT.Ln, bias=1.0).then_inc(r_ga, 1)

            def columns(b):
                act.wait_ge(r_at, b.n + 1)
                cols = rbank[:, 256:256 + NT * 36].rearrange("p (t n) -> p t n", t=NT)
                a.activation(acol[:], cols[:, :, 0:NHX], ACT.Copy)
                a.activation(emd[:], cols[:, :, 32:32 + NHX], ACT.Exp, scale=-1.0).then_inc(r_ac, 1)

            def decay(b):
                act.wait_ge(r_ac, b.n + 1)
                act.wait_ge(r_mb, b.n + 1)
                wait(act, r_c, 2 * b.n)
                mb = ring[RINGPOS["mb"]][:].rearrange("p (h q) -> p h q", h=NHX)
                for h in range(NHX):
                    a.activation(E_t[:, h, 0:T], mb[:, h, :], ACT.Exp, scale=-1.0, bias=acol[:, 0, h:h + 1])
                    last = a.activation(E_t[:, h, T:T + 128], mb[:, h, 128:T], ACT.Exp, scale=-1.0, bias=acol[:, 1, h:h + 1])
                last.then_inc(r_e, 1)

            act.wait_ge(misc_in, 96)

            def body(st):
                P, Q, R = st
                if P: xT_hi(P)
                if R: tr_hi(R)
                if Q: retransposed(Q, 0)
                if Q: exp_job(Q, 0)
                if R: gate_acts(R)
                if Q: exp_job(Q, 1)
                if P: v_out(P, 0)
                if P: transposed(P, 0)
                if R: columns(R)
                if R: decay(R)
                if P: transposed(P, 1)
                if Q: retransposed(Q, 1)
                if Q: exp_job(Q, 2)
                if Q: exp_job(Q, 3)
                if Q: oT_hi(Q, 0)
                if P: v_out(P, 1)
                if Q: exp_job(Q, 4)
                if Q: exp_job(Q, 5)
                if P: transposed(P, 2)
                if P: transposed(P, 3)
                if Q: oT_hi(Q, 1)

            pipeline(body, nc.scalar)

            def prep(n, p):
                act.wait_ge(f_ut, n + 1)
                wait(act, f_base, n - 1)
                a.activation(uT_h[p], tp[:, 0:C].rearrange("p (c q) -> p c q", c=CH), ACT.Copy).then_inc(f_uh, 1)
                act.wait_ge(f_sh, n + 1)
                a.activation(ex[:], lgs[:], ACT.Exp, accum_out=exsum[:]).then_inc(f_ex, 1)
                act.wait_ge(f_gt, n + 1)
                a.activation(gT[p][:], rbank[0:NE + NS, 128:256], ACT.Copy).then_inc(f_gte, 1)

            for n in range(2):
                prep(n, n)
            with nc.scalar.Fori(1, TILES // 2) as it:
                for u in range(2):
                    prep(it * 2 + u, u)

        @block.vector
        def _(dve):
            v = nc.vector
            chain = {}

            def link(ins, s, seq, per, key):
                chain[key] = chain.get(key, 0) % per + 1
                ins.then_inc(s, 1)
                dve.wait_ge(s, seq.n * per + chain[key])

            dve.wait_ge(w_in, 112)
            dve.wait_ge(zeros_in, 2)
            for k, col in ((0, 0), (1, 32)):
                v.tensor_copy(gsum[:, 0:CH, col:col + NHX], gstage[:, k, 0:CH])
                v.tensor_tensor(gsum[:, CH:2 * CH, col:col + NHX], gstage[:, k, CH:2 * CH], gstage[:, k, 2 * CH:3 * CH],
                                ALU.add).then_inc(g_sum, 1)
            dve.wait_ge(g_sum, 2)
            dve.wait_ge(w_hi, 1)
            for lo, w, hi in ((wqkv_l, wstage, wqkv_h), (wo_l, wostage, wo_h), (gw_l, gsum, gw_h), (cent_l, cent32, cent_h)):
                last = v.scalar_tensor_tensor(lo[:].rearrange("p c n -> p (c n)"), w[:].rearrange("p c n -> p (c n)"), WS,
                                              hi[:].rearrange("p c n -> p (c n)"), ALU.mult, ALU.subtract)
            last.then_inc(w_lo, 1)
            dve.wait_ge(misc_in, 96)
            v.tensor_scalar(ball[:], ball[:], 2.0 * WS, None, ALU.mult).then_inc(w_lo, 1)

            def ln_stats(src, stats, mv, s, seq, per, key, done):
                for t in range(NT):
                    ins = v.bn_stats(stats[:, t], src[:, t])
                link(ins, s, seq, per, key)
                held(dve, dve_held)
                for t in range(NT):
                    ins = v.bn_aggr(mv[:, t], stats[:, t])
                ins.then_inc(done, 1)

            def p_stats_step(b):
                dve.wait_ge(x_in[b.par], 16 * (b.half + 1))
                ln_stats(xin[b.par], p_stats, p_mv, dve_p, b, 3, "p", p_var)

            def normalize(dst, src, mv, rs, done):
                for t in range(NT):
                    last = v.tensor_scalar(dst[:, t], src[:, t], mv[:, t, 0:1], rs[:, t:t + 1], ALU.subtract, ALU.mult)
                last.then_inc(done, 1)

            def p_norm(b):
                dve.wait_ge(p_rstd, b.n + 1)
                wait(dve, p_xT, b.n)
                normalize(p_xn_t, xin[b.par], p_mv, p_rs, p_xn)

            def p_xlo(b):
                dve.wait_ge(p_xh, b.n + 1)
                v.tensor_tensor(xT_l[:].rearrange("p c q -> p (c q)"), tp[:], xT_h[:].rearrange("p c q -> p (c q)"),
                                ALU.subtract).then_inc(p_xl, 1)

            def p_rope(b, t):
                dve.wait_ge(p_qk, 2 * b.n + t + 1)
                qk = proj[:].rearrange("p (h i two) -> p h i two", h=2 * NHA, two=2)

                def table(tab):
                    return tab[:, t].rearrange("p (i two) -> p i two", two=2).unsqueeze(1).broadcast_to([128, 2 * NHA, DA // 2, 2])

                shape = "p (h i two) -> p h i two"
                v.tensor_tensor(rope_a[:].rearrange(shape, h=2 * NHA, two=2), qk, table(cos_t), ALU.mult)
                v.tensor_tensor(rope_b[:].rearrange(shape, h=2 * NHA, two=2), qk[:, :, :, ::-1], table(sin_t),
                                ALU.mult).then_inc(p_roped, 1)
                dve.wait_ge(p_roped, 2 * b.n + t + 1)
                v.tensor_tensor(rot[:].rearrange("p s h d -> p (s h d)"), rope_a[:], rope_b[:], ALU.add).then_inc(p_rot, 1)

            def p_low(b, t):
                dve.wait_ge(p_hi, 2 * b.n + t + 1)
                v.tensor_tensor(qst[b.par][:, t, :, DA:2 * DA], rot[:, 0], qst[b.par][:, t, :, 0:DA], ALU.subtract)
                v.tensor_tensor(kst[:, t, :, 2 * DA:3 * DA], rot[:, 1], kst[:, t, :, 0:DA], ALU.subtract).then_inc(p_lo, 1)

            def max_job(b, j):
                dve.wait_ge(s_done, JOBS * b.n + j + 1)
                src = ring[RINGPOS[f"s{j}"]]
                if j < 2:
                    t, pairs, keys = 0, slice(4 * j, 4 * j + 4), 128
                else:
                    t, pairs, keys = 1, slice(2 * (j - 2), 2 * (j - 2) + 2), T
                to = qst[b.par][:, t].rearrange("p (k r) s -> p r k s", r=2)[:, :, pairs, 3 * DA]
                v.tensor_reduce(to, src[:].rearrange("p (r k q) -> p r k q", r=2, q=keys), axis=AX.X, op=ALU.max,
                                negate=True).then_inc(m_done, 1)

            def o_norm(b, t):
                dve.wait_ge(av_done, JOBS * b.n + (2 if t == 0 else JOBS))
                wait(dve, o_t, 2 * (b.n - 1) + t + 1)
                o = obank[:, 0:NHA * (DA + 1)].rearrange("p (h d) -> p h d", h=NHA)
                link(v.reciprocal(rec[:, t], o[:, :, DA]), dve_q, b, 2, "q")
                v.tensor_tensor(o_n[:, t].rearrange("p (h d) -> p h d", h=NHA), o[:, :, 0:DA],
                                rec[:, t].unsqueeze(2).broadcast_to([128, NHA, DA]), ALU.mult).then_inc(n_done, 1)

            def oT_lo(b, t):
                dve.wait_ge(o_h, 2 * b.n + t + 1)
                v.tensor_tensor(oT_l[:, t].rearrange("p c q -> p (c q)"), tp[:, 0:C], oT_h[:, t].rearrange("p c q -> p (c q)"),
                                ALU.subtract).then_inc(o_l, 1)

            def residual(b, t):
                if t == 0:
                    dve.wait_ge(xres_in[b.par], 16 * (b.half + 1))
                    wait(dve, x2_done, b.n - 1)
                dve.wait_ge(w_done, 2 * b.n + t + 1)
                v.scalar_tensor_tensor(x1[b.par][:, t], proj[:, 0:C], 1.0 / WS, xres[b.par][:, t], ALU.mult,
                                       ALU.add).then_inc(x1_done, 1)

            def r_stats_step(b):
                dve.wait_ge(x1_done, 2 * b.n + 2)
                ln_stats(x1[b.par], r_stats, r_mv, dve_r, b, KR, "r", r_var)

            def r_norm(b):
                dve.wait_ge(r_rstd, b.n + 1)
                wait(dve, r_tr, b.n)
                normalize(r_xn_t, x1[b.par], r_mv, r_rs, r_xn)

            def tr_lo(b):
                dve.wait_ge(r_th, b.n + 1)
                v.tensor_tensor(tr_l[:].rearrange("p s c q -> p (s c q)"), ring[RINGPOS["tr"]][:],
                                tr_h[:].rearrange("p s c q -> p (s c q)"), ALU.subtract).then_inc(r_tl, 1)

            def scans(b):
                dve.wait_ge(r_ga, b.n + 1)
                wait(dve, r_mb, b.n)
                link(v.scalar_tensor_tensor(lsig[:], fg[:], 0.0, fg_l[:], ALU.min, ALU.subtract), dve_r, b, KR, "r")
                link(v.tensor_tensor_scan(cs[:], lsig[:], zero_row[:], 0.0, ALU.add, ALU.add), dve_r, b, KR, "r")
                link(v.tensor_tensor(am[0:NHX, :], ig[:], cs[:], ALU.subtract), dve_r, b, KR, "r")
                link(v.tensor_tensor_scan(cmax[:], am[0:NHX, :], am[0:NHX, :], -3e38, ALU.max, ALU.max), dve_r, b, KR, "r")
                v.tensor_tensor(am[32:32 + NHX, :], cs[:], cmax[:], ALU.add).then_inc(r_sc, 1)

            def weigh(b, c):
                if c == 0:
                    dve.wait_ge(r_em, b.n + 1)
                    wait(dve, r_h, 2 * b.n)
                dve.wait_ge(r_qk, 2 * b.n + c + 1)
                src = ring[RINGPOS[f"qk{c}"]][:].rearrange("p (r q) -> p r q", r=2)[:, :, 0:384]
                v.scalar_tensor_tensor(C_t[:, 2 * c:2 * c + 2], src, DX ** -0.5, E_t[:, 2 * c:2 * c + 2], ALU.mult,
                                       ALU.mult).then_inc(r_c, 1)

            def h_scale(b, t):
                dve.wait_ge(r_h, 2 * b.n + t + 1)
                H = rbank[:, 0:NHX * (DX + 1)].rearrange("p (h d) -> p h d", h=NHX)
                link(v.scalar_tensor_tensor(nre[:, t], H[:, :, DX], -1.0, emd[:, t], ALU.mult, ALU.max), dve_r, b, KR, "r")
                link(v.tensor_tensor(nrm[:, t], H[:, :, DX], nre[:, t], ALU.max), dve_r, b, KR, "r")
                link(v.tensor_scalar(nre[:, t], nrm[:, t], 1e-6, None, ALU.add), dve_r, b, KR, "r")
                link(v.reciprocal(nrr[:, t], nre[:, t]), dve_r, b, KR, "r")
                v.tensor_tensor(hh[:, t], H[:, :, 0:DX], nrr[:, t].unsqueeze(2).broadcast_to([128, NHX, DX]),
                                ALU.mult).then_inc(r_hn, 1)

            def h_norm(b):
                dve.wait_ge(r_hn, 2 * b.n + 2)
                for k in range(NT * NHX):
                    ins = v.bn_stats(h_stats[:, k], hh[:, k // NHX, k % NHX])
                link(ins, dve_r, b, KR, "r")
                held(dve, dve_held)
                for k in range(NT * NHX):
                    ins = v.bn_aggr(h_mv[:, k], h_stats[:, k])
                ins.then_inc(r_gv, 1)
                dve.wait_ge(r_gv, b.n + 1)
                link(v.tensor_tensor(hc[:], hh[:].rearrange("p t h d -> p (t h) d"),
                                     h_mv[:, :, 0:1].broadcast_to([128, NT * NHX, DX]), ALU.subtract), dve_r, b, KR, "r")
                dve.wait_ge(r_gr, b.n + 1)
                wait(dve, x2_done, b.n)
                v.tensor_tensor(hn[:], hc[:], h_rs[:].unsqueeze(2).broadcast_to([128, NT * NHX, DX]), ALU.mult).then_inc(r_n, 1)

            KR = 1 + 4 + 8 + 2

            def body(st):
                P, Q, R = st
                chain["p"] = 0
                if P: ln_p(P)
                if R: r_stats_step(R)
                if Q: max_job(Q, 0)
                if P: p_norm(P)
                if R: r_norm(R)
                if Q: max_job(Q, 1)
                if P: p_xlo(P)
                if Q: max_job(Q, 2)
                if R: tr_lo(R)
                if P: p_rope(P, 0)
                if Q: max_job(Q, 3)
                if P: p_low(P, 0)
                if Q: max_job(Q, 4)
                if R: scans(R)
                if Q: o_norm(Q, 0)
                if Q: max_job(Q, 5)
                if P: p_rope(P, 1)
                if R: weigh(R, 0)
                if Q: oT_lo(Q, 0)
                if R: weigh(R, 1)
                if P: p_low(P, 1)
                if Q: residual(Q, 0)
                if R: h_scale(R, 0)
                if R: h_scale(R, 1)
                if R: h_norm(R)
                if Q: o_norm(Q, 1)
                if Q: oT_lo(Q, 1)
                if Q: residual(Q, 1)

            def ln_p(b):
                dve.wait_ge(x_in[b.par], 16 * (b.half + 1))
                ln_stats(xin[b.par], p_stats, p_mv, dve_p, b, 1, "p", p_var)

            pipeline(body, nc.vector)

            KF = 10

            def flink(ins, n):
                chain["f"] = chain.get("f", 0) % KF + 1
                ins.then_inc(dve_f, 1)
                dve.wait_ge(dve_f, n * KF + chain["f"])

            def prep_a(n, p):
                if isinstance(n, int) and n == 0:
                    dve.wait_ge(x2_done, B)
                xt = x2[:, bass.ds(n, 1), :].rearrange("p a c -> p (a c)")
                flink(v.bn_stats(f_stats[:], xt), n)
                held(dve, dve_held)
                v.bn_aggr(f_mv[:], f_stats[:]).then_inc(f_var, 1)

            def prep_b(n, p):
                xt = x2[:, bass.ds(n, 1), :].rearrange("p a c -> p (a c)")
                dve.wait_ge(f_rstd, n + 1)
                wait(dve, f_ut, n)
                v.tensor_scalar(u_t, xt, f_mv[:, 0:1], f_rs[:], ALU.subtract, ALU.mult).then_inc(f_u, 1)
                dve.wait_ge(f_u, n + 1)
                v.tensor_tensor(xu[p], u_t, xt, ALU.add).then_inc(f_xu, 1)

            def prep_c(n, p):
                dve.wait_ge(f_uh, n + 1)
                v.tensor_tensor(uT_l[p], tp[:, 0:C].rearrange("p (c q) -> p c q", c=CH), uT_h[p],
                                ALU.subtract).then_inc(f_ul, 1)

            def prep_d(n, p):
                dve.wait_ge(f_lg, n + 1)
                flink(v.scalar_tensor_tensor(lg[:], rbank[:, 0:NE], 1.0 / WS, ebias_bc[:], ALU.mult, ALU.add), n)
                held(dve, dve_held)
                flink(v.max(mx8[:], lg[:]), n)
                v.tensor_scalar(lgs[:], lg[:], mx8[:, 0:1], None, ALU.subtract).then_inc(f_sh, 1)

            def prep_e(n, p):
                dve.wait_ge(f_ex, n + 1)
                flink(v.reciprocal(exrec[:], exsum[:]), n)
                flink(v.tensor_scalar(sm[:], ex[:], exrec[:], None, ALU.mult), n)
                held(dve, dve_held)
                flink(v.max(top8[:], sm[:]), n)
                held(dve, dve_held)
                flink(v.max_index(idx8[:], top8[:], sm[:]), n)
                flink(v.tensor_copy(idxf[:], idx8[:, 0:2]), n)
                v.tensor_scalar(g1[:], iota16[:], idxf[:, 0:1], top8[:, 0:1], ALU.is_equal, ALU.mult)
                flink(v.tensor_scalar(g2[:], iota16[:], idxf[:, 1:2], top8[:, 1:2], ALU.is_equal, ALU.mult), n)
                wait(dve, f_gt, n)
                flink(v.tensor_tensor(gate[:, 0:NE], g1[:], g2[:], ALU.add), n)
                v.tensor_scalar(gsc[p][:], gate[:, 0:NE], 1.0 / WS, None, ALU.mult).then_inc(f_g, 1)

            def start(n, p):
                dve.wait_ge(f_base, n + 1)
                dve.wait_ge(f_g, n + 1)
                dve.wait_ge(f_xu, n + 1)
                wait(dve, f_fin, n)
                bank = (proj, obank)[p]
                v.scalar_tensor_tensor(accA[:, 0], bank[:, 0:C], 0.5 / WS, xu[p], ALU.mult, ALU.add).then_inc(f_baseread, 1)

            def combine(n, p, k):
                dve.wait_ge(f_pair, 8 * n + k + 1)
                if k == 0:
                    dve.wait_ge(f_baseread, n + 1)
                else:
                    dve.wait_ge(f_comb, 8 * n + k)
                src = ring[(k // 2) % 2][:, bass.ts(k % 2, 512)].rearrange("p (e c) -> p e c", e=2)
                now, nxt = k % 2, (k + 1) % 2
                v.scalar_tensor_tensor(accA[:, nxt], src[:, 0], gsc[p][:, 2 * k:2 * k + 1], accA[:, now], ALU.mult, ALU.add)
                if k == 0:
                    v.tensor_scalar(accB[:, nxt], src[:, 1], gsc[p][:, 1:2], None, ALU.mult).then_inc(f_comb, 1)
                else:
                    v.scalar_tensor_tensor(accB[:, nxt], src[:, 1], gsc[p][:, 2 * k + 1:2 * k + 2], accB[:, now], ALU.mult,
                                           ALU.add).then_inc(f_comb, 1)

            def close(n, p):
                dve.wait_ge(f_comb, 8 * n + 8)
                return v.tensor_tensor(fin[p], accA[:, 0], accB[:, 0], ALU.add)

            def tile(n, p, half, following):
                start(n, p)
                for k in range(8):
                    combine(n, p, k)
                    if following:
                        m, q = n + 1, 1 - p
                        if k == 0: prep_a(m, q)
                        if k == 1: prep_b(m, q)
                        if k == 3: prep_c(m, q)
                        if k == 5: prep_d(m, q)
                        if k == 6: prep_e(m, q)
                if not isinstance(half, int) or half > 0:
                    dve.wait_ge(out_sent[p], half * 16)
                close(n, p).then_inc(f_fin, 1)

            prep_a(0, 0)
            prep_b(0, 0)
            prep_c(0, 0)
            prep_d(0, 0)
            prep_e(0, 0)
            for n in range(2):
                tile(n, n, 0, True)
            with nc.vector.Fori(1, TILES // 2 - 1) as it:
                for u in range(2):
                    tile(it * 2 + u, u, it, True)
            tile(TILES - 2, 0, TILES // 2 - 1, True)
            tile(TILES - 1, 1, TILES // 2 - 1, False)

        @block.tensor
        def _(pe):
            m = nc.tensor

            def split_product(dst, pieces, skip=False):
                for k, (lhsT, rhs) in enumerate(pieces):
                    last = m.matmul(dst, lhsT, rhs, start=k == 0, stop=k == len(pieces) - 1)
                return last

            def xT(b):
                pe.wait_ge(p_xn, b.n + 1)
                for c in range(CH):
                    for t in range(NT):
                        last = m.transpose(tp[:, bass.ds(c * T + t * 128, 128)], p_xn_t[:, t, bass.ts(c, 128)], ident[:])
                last.then_inc(p_xT, 1)

            def project(b, t, cols, done):
                if t == 0:
                    pe.wait_ge(p_xl, b.n + 1)
                q = bass.ts(t, 128)
                pieces = []
                for c in range(CH):
                    pieces += [(xT_h[:, c, q], wqkv_h[:, c, cols]), (xT_h[:, c, q], wqkv_l[:, c, cols]),
                               (xT_l[:, c, q], wqkv_h[:, c, cols])]
                split_product(proj[:, 0:cols.stop - cols.start], pieces).then_inc(done, 1)

            def transpose_heads(src, t, done):
                for k in range(NP):
                    last = m.transpose(tp16[:, k], src[:, t, 2 * k:2 * k + 2].rearrange("p r s -> p (r s)"), ident16[:])
                last.then_inc(done, 1)

            def scores(b, j):
                bank_free(pe, f"ring{RINGPOS[f's{j}']}", f"s{j}", cur[0])
                if j in (0, 2):
                    pe.wait_ge(p_te, 4 * b.n + (2 if j == 0 else 4))
                if j < 2:
                    t, pairs, keys, per = 0, range(4 * j, 4 * j + 4), 128, 4
                else:
                    t, pairs, keys, per = 1, range(2 * (j - 2), 2 * (j - 2) + 2), T, 2
                out4 = ring[RINGPOS[f"s{j}"]][:].rearrange("p (r k q) -> p r k q", r=2, q=keys)
                for r in range(2):
                    for h2 in range(0, per, 2):
                        m.matmul(out4[:, r, h2:h2 + 2, keys - 128:keys], identb[:], causal[:], start=h2 == 0, stop=False,
                                 skip_group_check=True)
                for k, pair in enumerate(pairs):
                    for r in range(2):
                        rows = slice(64 * r, 64 * r + 3 * DA)
                        last = m.matmul(out4[:, r, k], qT[b.par][rows, pair, bass.ts(t, 128)], kT[b.par][rows, pair, 0:keys],
                                        start=False, stop=True, skip_group_check=True)
                last.then_inc(s_done, 1)

            def reT(b, t):
                pe.wait_ge(m_done, JOBS * b.n + (2 if t == 0 else JOBS))
                transpose_heads(qst[b.par], t, q_rt)

            def scoresT(b, j):
                bank_free(pe, f"ring{RINGPOS[f't{j}']}", f"t{j}", cur[0])
                if j in (0, 2):
                    pe.wait_ge(q_rte, 2 * b.n + (1 if j == 0 else 2))
                if j < 2:
                    out4 = ring[RINGPOS[f"t{j}"]][:].rearrange("p (r k a q) -> p r k a q", r=2, k=4, a=1)
                    t, pairs = 0, range(4 * j, 4 * j + 4)
                else:
                    out4 = ring[RINGPOS[f"t{j}"]][:].rearrange("p (r k a q) -> p r k a q", r=2, k=2, a=2)
                    t, pairs = 1, range(2 * (j - 2), 2 * (j - 2) + 2)
                for k, pair in enumerate(pairs):
                    for kt in range(t + 1):
                        for r in range(2):
                            rows = slice(64 * r, 64 * r + 64)
                            last = m.matmul(out4[:, r, k, kt], kT[b.par][rows, pair, bass.ts(kt, 128)],
                                            qmT[rows, pair, bass.ts(t, 128)], start=True, stop=True)
                last.then_inc(t_done, 1)

            def values(b, j):
                if j in (0, 2):
                    bank_free(pe, "obank", f"o{j // 2}", cur[0])
                    pe.wait_ge(p_vev, 2 * b.n + (1 if j == 0 else 2))
                pe.wait_ge(k_done, JOBS * b.n + j + 1)
                o = obank[:, 0:NHA * (DA + 1)].rearrange("p (h d) -> p h d", h=NHA)
                t = 0 if j < 2 else 1
                pairs = range(4 * j, 4 * j + 4) if j < 2 else range(2 * (j - 2), 2 * (j - 2) + 2)
                pr = probs[j % PB][:].rearrange("p (r k a q) -> p r k a q", r=2, k=len(pairs), q=128)
                for r in range(2):
                    for k, pair in enumerate(pairs):
                        head = 2 * pair + r
                        for kt in range(t + 1):
                            last = m.matmul(o[:, head], pr[:, r, k, kt], v17[b.par][:, kt, head], start=kt == 0, stop=kt == t)
                last.then_inc(av_done, 1)

            def oT(b, t):
                pe.wait_ge(n_done, 2 * b.n + t + 1)
                for c in range(CH):
                    last = m.transpose(tp[:, bass.ts(c, 128)], o_n[:, t, bass.ts(c, 128)], ident[:])
                last.then_inc(o_t, 1)

            def project_out(b, t):
                pe.wait_ge(o_l, 2 * b.n + t + 1)
                pieces = []
                for c in range(CH):
                    pieces += [(oT_h[:, t, c], wo_h[:, c]), (oT_h[:, t, c], wo_l[:, c]), (oT_l[:, t, c], wo_h[:, c])]
                split_product(proj[:, 0:C], pieces).then_inc(w_done, 1)

            def tr(b):
                bank_free(pe, f"ring{RINGPOS['tr']}", "tr", cur[0])
                pe.wait_ge(ctx_in[b.par], 16 * (b.half + 1))
                pe.wait_ge(r_xn, b.n + 1)
                to = ring[RINGPOS["tr"]][:].rearrange("p (s c q) -> p s c q", s=2, c=CH)
                for s, src in ((0, ctx_t[b.par]), (1, r_xn_t)):
                    for c in range(CH):
                        for t in range(NT):
                            last = m.transpose(to[:, s, c, bass.ts(t, 128)], src[:, t, bass.ts(c, 128)], ident[:])
                last.then_inc(r_tr, 1)

            def gates(b):
                bank_free(pe, "rbank", "gates", cur[0])
                pe.wait_ge(r_tl, b.n + 1)
                pieces = []
                for s, w0 in ((1, 0), (0, CH)):
                    for c in range(CH):
                        pieces += [(gw_h[:, w0 + c], tr_h[:, s, c]), (gw_h[:, w0 + c], tr_l[:, s, c]), (gw_l[:, w0 + c], tr_h[:, s, c])]
                split_product(rbank[0:36, 0:T], pieces).then_inc(r_g, 1)

            def aT(b):
                bank_free(pe, "rbank", "aT", cur[0])
                pe.wait_ge(r_sc, b.n + 1)
                held(pe, pe_held)
                for t in range(NT):
                    last = m.transpose(rbank[:, 256 + 36 * t:256 + 36 * t + 36], am[:, bass.ts(t, 128)], ident[0:36, 0:36])
                last.then_inc(r_at, 1)

            def mb(b):
                bank_free(pe, f"ring{RINGPOS['mb']}", "mb", cur[0])
                to = ring[RINGPOS["mb"]][:].rearrange("p (h q) -> p h q", h=NHX)
                for h in range(NHX):
                    last = m.matmul(to[:, h], headsel[:, h], cmax[:], start=True, stop=True)
                last.then_inc(r_mb, 1)

            def xqk(b, c):
                bank_free(pe, f"ring{RINGPOS[f'qk{c}']}", f"qk{c}", cur[0])
                to = ring[RINGPOS[f"qk{c}"]][:].rearrange("p (r q) -> p r q", r=2)
                for kt in range(NT):
                    for n, (kp, xp) in enumerate(((tr_h, tr_h), (tr_l, tr_h), (tr_h, tr_l))):
                        for r in range(2):
                            rows = slice(64 * r, 64 * r + 64)
                            dst = to[:, r, 0:T] if kt == 0 else to[:, r, T:T + 128]
                            last = m.matmul(dst, kp[rows, 0, c, bass.ts(kt, 128)], xp[rows, 1, c, kt * 128:T], start=n == 0, stop=n == 2)
                last.then_inc(r_qk, 1)

            def xvalues(b, t):
                bank_free(pe, "rbank", f"h{t}", cur[0])
                if t == 0:
                    pe.wait_ge(r_c, 2 * b.n + 2)
                    pe.wait_ge(c_cp, b.n + 1)
                H = rbank[:, 0:NHX * (DX + 1)].rearrange("p (h d) -> p h d", h=NHX)
                for h in range(NHX):
                    for kt in range(t + 1):
                        cols = slice(128 * t, 128 * t + 128) if kt == 0 else slice(256, 384)
                        last = m.matmul(H[:, h], C_t[:, h, cols], ctx65[b.par][:, kt, h], start=kt == 0, stop=kt == t)
                last.then_inc(r_h, 1)

            cur = [None]
            pe.wait_ge(pool_ready, 1)
            pe.wait_ge(w_lo, 2)

            def tp_use(name, st, fn, *args):
                bank_free(pe, "tp", name, st)
                fn(*args)

            def proj_use(name, st, fn, *args):
                bank_free(pe, "proj", name, st)
                fn(*args)

            def heads_of(b, t, is_k):
                if not is_k:
                    pe.wait_ge(p_lo, 2 * b.n + t + 1)
                transpose_heads(kst if is_k else qst[b.par], t, p_tr)

            QK, V = slice(0, 2 * C), slice(2 * C, 3 * C)

            def body(st):
                P, Q, R = st
                cur[0] = st
                if Q: scores(Q, 0)
                if Q: scores(Q, 1)
                if P: tp_use("xT", st, xT, P)
                if R: tr(R)
                if Q: scores(Q, 2)
                if Q: tp_use("reT0", st, reT, Q, 0)
                if P: proj_use("qk0", st, project, P, 0, QK, p_qk)
                if Q: scoresT(Q, 0)
                if Q: scores(Q, 3)
                if R: gates(R)
                if Q: scoresT(Q, 1)
                if Q: scores(Q, 4)
                if P: proj_use("v0", st, project, P, 0, V, p_vp)
                if Q: values(Q, 0)
                if Q: values(Q, 1)
                if Q: scores(Q, 5)
                if P: tp_use("tq0", st, heads_of, P, 0, False)
                if P: proj_use("qk1", st, project, P, 1, QK, p_qk)
                if R: aT(R)
                if R: mb(R)
                if P: tp_use("tk0", st, heads_of, P, 0, True)
                if Q: tp_use("reT1", st, reT, Q, 1)
                if Q: scoresT(Q, 2)
                if R: xqk(R, 0)
                if Q: scoresT(Q, 3)
                if Q: tp_use("oT0", st, oT, Q, 0)
                if P: proj_use("v1", st, project, P, 1, V, p_vp)
                if R: xqk(R, 1)
                if Q: scoresT(Q, 4)
                if Q: values(Q, 2)
                if Q: scoresT(Q, 5)
                if Q: values(Q, 3)
                if Q: proj_use("w0", st, project_out, Q, 0)
                if P: tp_use("tq1", st, heads_of, P, 1, False)
                if R: xvalues(R, 0)
                if Q: values(Q, 4)
                if P: tp_use("tk1", st, heads_of, P, 1, True)
                if R: xvalues(R, 1)
                if Q: values(Q, 5)
                if Q: tp_use("oT1", st, oT, Q, 1)
                if Q: proj_use("w1", st, project_out, Q, 1)

            pipeline(body, nc.tensor)

            pe.wait_ge(e_lo, NE + 1)
            pe.wait_ge(x2_done, B)

            def prep_a(n, p):
                pe.wait_ge(f_u, n + 1)
                wait(pe, f_ul, n)
                for c in range(CH):
                    last = m.transpose(tp[:, bass.ts(c, 128)], u_t[:, bass.ts(c, 128)], ident[:])
                last.then_inc(f_ut, 1)

            def products(lhs, rhs_h, rhs_l, c_order=range(CH)):
                h, l = lhs
                return [x for c in c_order for x in ((h[:, c], rhs_h(c)), (h[:, c], rhs_l(c)), (l[:, c], rhs_h(c)))]

            def prep_b(n, p):
                pe.wait_ge(f_ul, n + 1)
                wait(pe, f_gte, n)
                split_product(rbank[:, 0:NE], products((uT_h[p], uT_l[p]), lambda c: cent_h[:, c], lambda c: cent_l[:, c])).then_inc(f_lg, 1)

            def prep_c(n, p):
                pe.wait_ge(f_g, n + 1)
                m.transpose(rbank[0:NE + NS, 128:256], gate[:], ident[:]).then_inc(f_gt, 1)

            def base(n, p):
                pe.wait_ge(f_gte, n + 1)
                wait(pe, f_baseread, n - 1)
                pieces = products((uT_h[p], uT_l[p]), lambda c: ew_h[:, c, NE], lambda c: ew_l[:, c, NE])
                split_product((proj, obank)[p][:, 0:C], pieces + [(gT[p][:], ball[:])]).then_inc(f_base, 1)

            def pair(n, p, k):
                wait(pe, f_comb, 8 * n + k - 3)
                pieces = products((uT_h[p], uT_l[p]), lambda c: ew_h[:, c, 2 * k:2 * k + 2].rearrange("p e o -> p (e o)"),
                                  lambda c: ew_l[:, c, 2 * k:2 * k + 2].rearrange("p e o -> p (e o)"))
                split_product(ring[(k // 2) % 2][:, bass.ts(k % 2, 512)], pieces).then_inc(f_pair, 1)

            def tile(n, p, following):
                for k in range(8):
                    pair(n, p, k)
                    if k == 0:
                        base(n, p)
                    if following:
                        if k == 2: prep_a(n + 1, 1 - p)
                        if k == 4: prep_b(n + 1, 1 - p)
                        if k == 7: prep_c(n + 1, 1 - p)

            prep_a(0, 0)
            prep_b(0, 0)
            prep_c(0, 0)
            for n in range(2):
                tile(n, n, True)
            with nc.tensor.Fori(1, TILES // 2 - 1) as it:
                for u in range(2):
                    tile(it * 2 + u, u, True)
            tile(TILES - 2, 0, True)
            tile(TILES - 1, 1, False)


def kernel(**inputs):
    import numpy as np
    import concourse.bacc as bacc
    from concourse.bass_utils import run_bass_kernel_spmd as run

    def lay(a):
        return np.ascontiguousarray(a)

    inv = 1.0 / 10000.0 ** (np.arange(0, DA, 2, dtype=np.float32) / DA)
    ang = np.outer(np.arange(T, dtype=np.float32), inv.astype(np.float32)).astype(np.float32)
    cos = np.repeat(np.cos(ang), 2, axis=1) / WS
    sin = np.repeat(np.sin(ang), 2, axis=1) / WS * np.tile([-1.0, 1.0], DA // 2)
    def tiles(a):
        return lay(a.astype(np.float32).reshape(NT, 128, DA).transpose(1, 0, 2))

    arrays = {
        "x": lay(inputs["x"]), "ctx": lay(inputs["ctx_1024"]), "w_qkv": lay(inputs["L0_attn_w_qkv"]),
        "w_out": lay(inputs["L0_attn_w_out"]), "igk": lay(inputs["L0_xattn_igate_kernel"]),
        "igb": lay(inputs["L0_xattn_igate_bias"]), "fgk": lay(inputs["L0_xattn_fgate_kernel"]),
        "fgb": lay(inputs["L0_xattn_fgate_bias"]), "onorm": lay(inputs["L0_xattn_outnorm_scale"]),
        "centT": lay(np.asarray(inputs["L0_ffn_centroids"]).T), "ebias": lay(inputs["L0_ffn_expert_biases"]),
        "WrT": lay(np.asarray(inputs["L0_ffn_Wr"]).transpose(2, 0, 1)), "br": lay(inputs["L0_ffn_br"]),
        "WsT": lay(np.asarray(inputs["L0_ffn_Ws"]).transpose(2, 0, 1)), "bs": lay(inputs["L0_ffn_bs"]),
        "rope_cos": tiles(cos), "rope_sin": tiles(sin),
    }
    nc = bacc.Bacc("TRN2", target_bir_lowering=False, num_devices=1)
    args = [nc.dram_tensor(f"in_{k}", a.shape, mybir.dt.from_np(a.dtype), kind="ExternalInput").ap() for k, a in arrays.items()]
    args.append(nc.dram_tensor("out_y", (B, T, C), mybir.dt.float32, kind="ExternalOutput").ap())
    decoder_layer(nc, *args)
    r = run(nc, [{f"in_{k}": a for k, a in arrays.items()}], core_ids=[0])
    return r.results[0]["out_y"]
```

```python
import concourse.bass as bass
from concourse import mybir
from contextlib import ExitStack
from collections import namedtuple

B, T, C = 16, 256, 256
NT = T // 128
CH = C // 128
NHA, DA = 16, C // 16
NP = NHA // 2
NHX, DX = 4, C // 4
NE, NS = 16, 2
WS = 64.0
NEG = -1e30
PB = 3
JOBS = 6

Seq = namedtuple("Seq", "n half par")
LAGS = 6


def decoder_layer(nc, x, ctx, w_qkv, w_out, igk, igb, fgk, fgb, onorm, centT, ebias, WrT, br, WsT, bs, rope_cos, rope_sin, out):
    f32, f16, bf16, u32 = mybir.dt.float32, mybir.dt.float16, mybir.dt.bfloat16, mybir.dt.uint32
    ALU, ACT, AX = mybir.AluOpType, mybir.ActivationFunctionType, mybir.AxisListType

    stack = ExitStack()
    with stack:
        def sb(name, shape, dt=f32):
            return stack.enter_context(nc.sbuf_tensor(name, shape, dt))

        EB = 4

        def sem(name):
            return stack.enter_context(nc.semaphore(name))

        ident = sb("ident", [128, 128])
        ident16 = sb("ident16", [128, 128], f16)
        identb = sb("identb", [128, 128], bf16)
        causal = sb("causal", [128, 2, 128], bf16)
        zero_row = sb("zero_row", [NHX, T])
        headsel = sb("headsel", [64 + NHX, NHX, 128], bf16)
        mhalf = sb("mhalf", [128, 8])
        iota16 = sb("iota16", [128, NE])
        cos_t = sb("cos_t", [128, NT, DA])
        sin_t = sb("sin_t", [128, NT, DA])
        wstage = sb("wstage", [128, CH, 3 * C])
        wostage = sb("wostage", [128, CH, C])
        wqkv_h = sb("wqkv_h", [128, CH, 3 * C], f16)
        wqkv_l = sb("wqkv_l", [128, CH, 3 * C], f16)
        wo_h = sb("wo_h", [128, CH, C], f16)
        wo_l = sb("wo_l", [128, CH, C], f16)
        gstage = sb("gstage", [128, 2, 3 * CH, NHX])
        gsum = sb("gsum", [128, 2 * CH, 36])
        gw_h = sb("gw_h", [128, 2 * CH, 36], f16)
        gw_l = sb("gw_l", [128, 2 * CH, 36], f16)
        gbias = sb("gbias", [36, 1])
        onorm_bc = sb("onorm_bc", [128, C])
        cent32 = sb("cent32", [128, CH, NE])
        cent_h = sb("cent_h", [128, CH, NE], f16)
        cent_l = sb("cent_l", [128, CH, NE], f16)
        ebias_bc = sb("ebias_bc", [128, NE])
        ball = sb("ball", [NE + NS, C])
        estage = sb("estage", [128, EB, CH, C])
        ew_h = sb("ew_h", [128, CH, NE + 1, C], f16)
        ew_l = sb("ew_l", [128, CH, NE + 1, C], f16)

        xin = [sb(f"xin{i}", [128, NT, C]) for i in range(2)]
        p_stats = sb("p_stats", [128, NT, 6])
        p_mv = sb("p_mv", [128, NT, 2])
        p_ve = sb("p_ve", [128, NT])
        p_rs = sb("p_rs", [128, NT])
        p_xn_t = sb("p_xn_t", [128, NT, C])
        xT_h = sb("xT_h", [128, CH, T], f16)
        xT_l = sb("xT_l", [128, CH, T], f16)
        rope_a = sb("rope_a", [128, 2 * C])
        rope_b = sb("rope_b", [128, 2 * C])
        rot = sb("rot", [128, 2, NHA, DA])
        qst = [sb(f"qst{i}", [128, NT, NHA, 64], f16) for i in range(2)]
        kst = sb("kst", [128, NT, NHA, 64], f16)
        qT = [sb(f"qT{i}", [128, NP, T], f16) for i in range(2)]
        kT = [sb(f"kT{i}", [128, NP, T], f16) for i in range(2)]
        v17_h = [sb(f"v17_h{i}", [128, NT, NHA, DA + 1], f16) for i in range(2)]
        v17_l = [sb(f"v17_l{i}", [128, NT, NHA, DA + 1], f16) for i in range(2)]

        xres = [sb(f"xres{i}", [128, NT, C]) for i in range(2)]
        qmT = sb("qmT", [128, NP, T], f16)
        probs = [sb(f"probs{i}", [128, 1024]) for i in range(2)]
        probs_h = [sb(f"probs_h{i}", [128, 1024], f16) for i in range(PB)]
        probs_l = [sb(f"probs_l{i}", [128, 1024], f16) for i in range(PB)]
        rec = sb("rec", [128, NT, NHA])
        o_n = sb("o_n", [128, NT, C])
        oT_h = sb("oT_h", [128, NT, CH, 128], f16)
        oT_l = sb("oT_l", [128, NT, CH, 128], f16)
        x1 = [sb(f"x1_{i}", [128, NT, C]) for i in range(2)]

        ctx_t = [sb(f"ctx{i}", [128, NT, C]) for i in range(2)]
        ctx65 = [sb(f"ctx65_{i}", [128, NT, NHX, DX + 1]) for i in range(2)]
        r_stats = sb("r_stats", [128, NT, 6])
        r_mv = sb("r_mv", [128, NT, 2])
        r_ve = sb("r_ve", [128, NT])
        r_rs = sb("r_rs", [128, NT])
        r_xn_t = sb("r_xn_t", [128, NT, C])
        tr_h = sb("tr_h", [128, 2, CH, T], f16)
        tr_l = sb("tr_l", [128, 2, CH, T], f16)
        fg = sb("fg", [NHX, T])
        fg_a = sb("fg_a", [NHX, T])
        fg_e = fg_l = fg_a
        ig = sb("ig", [NHX, T])
        lsig = fg
        cs = sb("cs", [NHX, T])
        am = sb("am", [36, T])
        cmax = sb("cmax", [NHX, T])
        cmax_r = sb("cmax_r", [NHX, T])
        cmax3 = sb("cmax3", [64 + NHX, T], bf16)
        acol = sb("acol", [128, NT, NHX])
        emd = sb("emd", [128, NT, NHX])
        E_t = wstage[:].rearrange("p c n -> p (c n)").rearrange("p (h q) -> p h q", h=NHX)
        C_t = sb("C_t", [128, NHX, 3 * 128])
        nrm = sb("nrm", [128, NT, NHX])
        nre = sb("nre", [128, NT, NHX])
        nrr = sb("nrr", [128, NT, NHX])
        hh = sb("hh", [128, NT, NHX, DX])
        h_stats = sb("h_stats", [128, NT * NHX, 6])
        h_mv = sb("h_mv", [128, NT * NHX, 2])
        h_ve = sb("h_ve", [128, NT * NHX])
        h_rs = sb("h_rs", [128, NT * NHX])
        hc = sb("hc", [128, NT * NHX, DX])
        hn = hc
        hs = wostage
        x2 = sb("x2", [128, NT, C])

        f_stats = sb("f_stats", [128, NT, 6])
        f_mv = sb("f_mv", [128, NT, 2])
        f_ve = sb("f_ve", [128, NT])
        f_rs = sb("f_rs", [128, NT])
        u_t = sb("u_t", [128, NT, C])
        xu = [sb(f"xu{i}", [128, NT, C]) for i in range(2)]
        uT_h = [sb(f"uT_h{i}", [128, CH, T], f16) for i in range(2)]
        uT_l = [sb(f"uT_l{i}", [128, CH, T], f16) for i in range(2)]
        lg = sb("lg", [128, NT, NE])
        lgs = sb("lgs", [128, NT, NE])
        mx8 = sb("mx8", [128, NT, 8])
        ex = sb("ex", [128, NT, NE])
        exsum = sb("exsum", [128, NT])
        exrec = sb("exrec", [128, NT])
        sm = sb("sm", [128, NT, NE])
        top8 = sb("top8", [128, NT, 8])
        idx8 = sb("idx8", [128, NT, 8], u32)
        idxf = sb("idxf", [128, NT, 2])
        g1 = sb("g1", [128, NT, NE])
        g2 = sb("g2", [128, NT, NE])
        gate = sb("gate", [128, NT, NE + NS])
        gsc = [sb(f"gsc{i}", [128, NT, NE]) for i in range(2)]
        gT = sb("gT", [NE + NS, NT, 128])
        acc = sb("acc", [128, NT, 2, C])
        fin = [sb(f"fin{i}", [128, NT, C]) for i in range(2)]

        ring = [stack.enter_context(nc.psum_tensor(f"ring{i}", [128, 1024], f32)) for i in range(2)]
        proj = stack.enter_context(nc.psum_tensor("proj", [128, 512], f32))
        tp = stack.enter_context(nc.psum_tensor("tp", [128, 512], f32))
        obank = stack.enter_context(nc.psum_tensor("obank", [128, 512], f32))
        rbank = stack.enter_context(nc.psum_tensor("rbank", [128, 512], f32))
        tp16 = tp[:, :].bitcast(f16).rearrange("p (a q) -> p a q", a=NP)

        w_in, pool_ready, w_hi, w_lo, g_sum, zeros_in = map(sem, ("w_in", "pool_ready", "w_hi", "w_lo", "g_sum", "zeros_in"))
        misc_in, dve_held, pe_held, pool_held, dve_g, pool_g = map(sem, ("misc_in", "dve_held", "pe_held", "pool_held", "dve_g", "pool_g"))
        x_in, xres_in, ctx_in = ([sem(f"{n}{i}") for i in range(2)] for n in ("x_in", "xres_in", "ctx_in"))
        names = ("p_var p_rstd p_xn p_xT p_xh p_xl p_qk p_roped p_rot p_hi p_lo p_tr p_te p_vp p_vh p_vev dve_p pool_p "
                 "s_done m_done q_rt q_rte t_done e_done k_done ph_done pl_done av_done n_done o_t o_h o_l w_done x1_done dve_q "
                 "c_cp r_var r_rstd r_xn r_tr r_th r_tl r_g r_ga r_sc r_c3 r_at r_ac r_mb r_e r_em r_qk r_c r_h r_hn "
                 "r_gv r_gr r_n x2_done dve_r act_r pool_r").split()
        (p_var, p_rstd, p_xn, p_xT, p_xh, p_xl, p_qk, p_roped, p_rot, p_hi, p_lo, p_tr, p_te, p_vp, p_vh, p_vev, dve_p, pool_p,
         s_done, m_done, q_rt, q_rte, t_done, e_done, k_done, ph_done, pl_done, av_done, n_done, o_t, o_h, o_l, w_done, x1_done, dve_q,
         c_cp, r_var, r_rstd, r_xn, r_tr, r_th, r_tl, r_g, r_ga, r_sc, r_c3, r_at, r_ac, r_mb, r_e, r_em, r_qk, r_c, r_h, r_hn,
         r_gv, r_gr, r_n, x2_done, dve_r, act_r, pool_r) = map(sem, names)
        e_in = [sem(f"e_in{i}") for i in range(EB)]
        e_sum, e_hi, e_lo = map(sem, ("e_sum", "e_hi", "e_lo"))
        (f_var, f_rstd, f_u, f_xu, f_ut, f_uh, f_ul, f_rt, f_lg, f_sh, f_ex, f_g, f_gt, f_gte, f_base, f_quad, f_comb, f_fin,
         f_baseread, dve_f, pool_f) = map(sem, ("f_var f_rstd f_u f_xu f_ut f_uh f_ul f_rt f_lg f_sh f_ex f_g f_gt f_gte "
                                                "f_base f_quad f_comb f_fin f_baseread dve_f pool_f").split())
        out_sent = [sem("out_sent0"), sem("out_sent1")]

        def wait(eng, s, value):
            if not isinstance(value, int) or value > 0:
                eng.wait_ge(s, value)

        def held(eng, s):
            eng.sem_inc(s, 1)

        def pipeline(body, engine, lags=LAGS, peel=6):
            def step(i):
                return [Seq(i - d, (i - d) // 2, (i - d) % 2) if 0 <= i - d < B else None for d in range(lags)]

            for i in range(peel):
                body(step(i))
            with engine.Fori(peel // 2, B // 2) as it:
                for u in range(2):
                    body([Seq(it * 2 + (u - d), it + (u - d) // 2, (u - d) % 2) for d in range(lags)])
            for i in range(B, B + lags - 1):
                body(step(i))

        USES = {
            "ring0": [(f"c{q}", 5, f_comb, 32, 4 * q + 4) for q in range(8)],
            "ring1": [("s2", 1, m_done, 6, 3), ("t5", 2, e_done, 6, 6), ("s3", 1, m_done, 6, 4), ("tr", 3, r_tl, 1, 1),
                      ("s4", 1, m_done, 6, 5), ("t0", 1, e_done, 6, 1), ("s5", 1, m_done, 6, 6), ("t1", 1, e_done, 6, 2),
                      ("mb", 3, r_e, 1, 1), ("qk0", 3, r_c, 2, 1), ("t2", 1, e_done, 6, 3), ("s0", 0, m_done, 6, 1),
                      ("t3", 1, e_done, 6, 4), ("qk1", 3, r_c, 2, 2), ("t4", 1, e_done, 6, 5), ("s1", 0, m_done, 6, 2)],
            "tp": [("xT", 0, p_xl, 1, 1), ("reT0", 1, q_rte, 2, 1), ("oT0", 2, o_l, 2, 1), ("tq0", 0, p_te, 4, 1),
                   ("oT1", 2, o_l, 2, 2), ("tk0", 0, p_te, 4, 2), ("reT1", 1, q_rte, 2, 2), ("tq1", 0, p_te, 4, 3),
                   ("uT", 4, f_ul, 1, 1), ("tk1", 0, p_te, 4, 4)],
            "proj": [("qk0", 0, p_roped, 2, 1), ("v0", 0, p_vev, 2, 1), ("qk1", 0, p_roped, 2, 2), ("v1", 0, p_vev, 2, 2),
                     ("b0", 5, f_baseread, 2, 1), ("w0", 2, x1_done, 2, 1), ("b1", 5, f_baseread, 2, 2),
                     ("w1", 2, x1_done, 2, 2)],
            "obank": [("o0", 1, n_done, 2, 1), ("o1", 1, n_done, 2, 2)],
            "rbank": [("gT", 5, f_gte, 1, 1), ("h0", 4, r_hn, 2, 1), ("h1", 4, r_hn, 2, 2), ("gates", 3, r_ga, 1, 1),
                      ("aT", 3, r_ac, 1, 1), ("rt", 4, f_lg, 1, 1)],
        }

        def bank_free(pe, bank, name, seqs):
            uses = USES[bank]
            at = [u[0] for u in uses].index(name)
            now = next(s.n + d for d, s in enumerate(seqs) if s is not None)
            for back in range(1, len(uses) + 1):
                _, lag, s, per, count = uses[(at - back) % len(uses)]
                n = now - lag - int(at < back)
                if not isinstance(n, int) or 0 <= n < B:
                    wait(pe, s, n * per + count)
                    return

        def experts_of(seqs, count):
            first = EB * (seqs[0].n - 1) if seqs[0] and isinstance(seqs[0].n, int) else count
            return [k for k in range(first, first + EB) if 0 <= k < count]

        block = stack.enter_context(nc.Block())

        x_v = x.rearrange("b (t p) c -> b p t c", p=128)
        ctx_v = ctx.rearrange("b (t p) c -> b p t c", p=128)
        out_v = out.rearrange("b (t p) c -> b p t c", p=128)
        EXPERTS = NE + NS

        @block.sync
        def _(sp):
            sp.dma_start(xin[0][:], x_v[0]).then_inc(x_in[0], 16)
            sp.dma_start(wstage[:], w_qkv.rearrange("(c p) n -> p c n", p=128)).then_inc(w_in, 16)
            sp.dma_start(cos_t[:], rope_cos).then_inc(w_in, 16)
            sp.dma_start(sin_t[:], rope_sin).then_inc(w_in, 16)
            sp.dma_start(wostage[:], w_out.rearrange("(c p) n -> p c n", p=128)).then_inc(w_in, 16)
            sp.dma_start(gstage[:, 0], igk.rearrange("(c p) n -> p c n", p=128)).then_inc(w_in, 16)
            sp.dma_start(gstage[:, 1], fgk.rearrange("(c p) n -> p c n", p=128)).then_inc(w_in, 16)
            sp.dma_start(cent32[:], centT.rearrange("(c p) n -> p c n", p=128)).then_inc(w_in, 16)
            sp.wait_ge(zeros_in, 1)
            sp.dma_start(gbias[0:NHX, :], igb.rearrange("(h a) -> h a", a=1)).then_inc(misc_in, 16)
            sp.dma_start(gbias[32:32 + NHX, :], fgb.rearrange("(h a) -> h a", a=1)).then_inc(misc_in, 16)
            sp.dma_start(onorm_bc[:], onorm.partition_broadcast(128)).then_inc(misc_in, 16)
            sp.dma_start(ebias_bc[:], ebias.partition_broadcast(128)).then_inc(misc_in, 16)
            sp.dma_start(ball[0:NE, :], br).then_inc(misc_in, 16)
            sp.dma_start(ball[NE:NE + NS, :], bs).then_inc(misc_in, 16)

            def expert(k):
                if k >= EB:
                    sp.wait_ge(e_lo, k - EB + 1)
                src = WrT[:, k] if k < NE else WsT[:, k - NE]
                sp.dma_start(estage[:, k % EB], src.rearrange("(c p) o -> p c o", p=128)).then_inc(e_in[k % EB], 16)

            def body(seqs):
                b = seqs[7]
                if b:
                    sp.wait_ge(f_fin, 2 * b.n + 2)
                    sp.dma_start(out_v[b.n], fin[b.par][:]).then_inc(out_sent[b.par], 16)
                b = seqs[0]
                if b and not (isinstance(b.n, int) and b.n == 0):
                    wait(sp, p_xn, b.n - 1)
                    sp.dma_start(xin[b.par][:], x_v[b.n]).then_inc(x_in[b.par], 16)
                b = seqs[2]
                if b:
                    wait(sp, x1_done, 2 * (b.n - 1))
                    sp.dma_start(xres[b.par][:], x_v[b.n]).then_inc(xres_in[b.par], 16)
                b = seqs[3]
                if b:
                    wait(sp, r_tr, b.n - 1)
                    wait(sp, c_cp, b.n - 1)
                    sp.dma_start(ctx_t[b.par][:], ctx_v[b.n]).then_inc(ctx_in[b.par], 16)
                for k in experts_of(seqs, EXPERTS):
                    expert(k)

            pipeline(body, nc.sync, lags=8, peel=8)
            for i in range(2):
                sp.wait_ge(out_sent[i], 16 * (B // 2))

        @block.gpsimd
        def _(pool):
            g = nc.gpsimd
            chain = {}

            def link(ins, s, seq, per, key):
                chain[key] = chain.get(key, 0) % per + 1
                ins.then_inc(s, 1)
                pool.wait_ge(s, seq.n * per + chain[key])

            g.memset(ident[:], 0.0)
            g.memset(gsum[:], 0.0)
            g.memset(gbias[:], 0.0).then_inc(zeros_in, 1)
            pool.wait_ge(zeros_in, 1)
            g.affine_select(out=ident[:], in_=ident[:], compare_op=ALU.not_equal, fill=1.0, base=0,
                            pattern=[[-1, 128]], channel_multiplier=1).then_inc(zeros_in, 1)
            g.memset(causal[:], 0.0)
            g.memset(headsel[:], 0.0)
            g.memset(cmax3[:], 0.0)
            g.memset(mhalf[:], -0.5)
            g.memset(am[:], 0.0)
            g.memset(zero_row[:], 0.0)
            g.memset(gate[:], 0.5)
            g.memset(kst[:], 0.0)
            for i in range(2):
                g.memset(qst[i][:], 0.0)
                g.memset(v17_h[i][:], WS)
                g.memset(v17_l[i][:], 0.0)
                g.memset(ctx65[i][:], 1.0)
            g.iota(iota16[:], pattern=[[1, NE]], base=0, channel_multiplier=0,
                   allow_small_or_imprecise_dtypes=True).then_inc(zeros_in, 1)
            pool.wait_ge(zeros_in, 3)
            g.memset(kst[:, :, :, 3 * DA:3 * DA + 1], 1.0)
            g.tensor_copy(ident16[:], ident[:])
            g.tensor_copy(identb[:], ident[:])
            g.affine_select(out=causal[:], in_=causal[:], compare_op=ALU.is_ge, fill=NEG, base=0,
                            pattern=[[0, 2], [-1, 128]], channel_multiplier=1)
            for piece in range(3):
                if piece:
                    pool.wait_ge(pool_ready, piece)
                g.affine_select(out=headsel[:], in_=headsel[:], compare_op=ALU.not_equal, fill=1.0, base=-32 * piece,
                                pattern=[[-1, NHX], [0, 128]], channel_multiplier=1).then_inc(pool_ready, 1)

            def rstd(dst, ve, var, n, eps, ready, value, linked, done):
                pool.wait_ge(ready, value)
                held(pool, pool_held)
                linked(g.tensor_scalar(ve, var, eps, None, ALU.add))
                g.tensor_tensor(dst, ve, mhalf[:, 0:n], ALU.pow).then_inc(done, 1)

            def p_rstd_step(b):
                rstd(p_rs[:], p_ve[:], p_mv[:, :, 1], NT, 1e-5, p_var, b.n + 1,
                     lambda i: link(i, pool_p, b, 1, "p"), p_rstd)

            def r_rstd_step(b):
                rstd(r_rs[:], r_ve[:], r_mv[:, :, 1], NT, 1e-5, r_var, b.n + 1,
                     lambda i: link(i, pool_g, b, 1, "g"), r_rstd)

            def mask_probs(b, j):
                pool.wait_ge(e_done, JOBS * b.n + j + 1)
                held(pool, pool_held)
                if j < 2:
                    view = probs[j % 2][:, :].rearrange("p (a q) -> p a q", q=128)
                    pattern = [[0, 8], [1, 128]]
                else:
                    view = probs[j % 2][:, :].rearrange("p (a k q) -> p a k q", k=2, q=128)[:, :, 1, :]
                    pattern = [[0, 4], [1, 128]]
                g.affine_select(out=view, in_=view, compare_op=ALU.is_ge, fill=0.0, base=0, pattern=pattern,
                                channel_multiplier=-1).then_inc(k_done, 1)

            def probs_low(b, j):
                pool.wait_ge(ph_done, JOBS * b.n + j + 1)
                g.tensor_tensor(probs_l[j % PB][:], probs[j % 2][:], probs_h[j % PB][:], ALU.subtract).then_inc(pl_done, 1)

            def ctx_copy(b):
                pool.wait_ge(ctx_in[b.par], 16 * (b.half + 1))
                wait(pool, r_h, 2 * (b.n - 1))
                held(pool, pool_held)
                for t in range(NT):
                    last = g.tensor_copy(ctx65[b.par][:, t, :, 0:DX], ctx_t[b.par][:, t].rearrange("p (h d) -> p h d", h=NHX))
                last.then_inc(c_cp, 1)

            def mask_E(b):
                pool.wait_ge(r_e, b.n + 1)
                held(pool, pool_held)
                for k in (0, 2):
                    view = E_t[:, :, bass.ts(k, 128)]
                    last = g.affine_select(out=view, in_=view, compare_op=ALU.is_ge, fill=0.0, base=0,
                                           pattern=[[0, NHX], [1, 128]], channel_multiplier=-1)
                last.then_inc(r_em, 1)

            def h_rstd_step(b):
                rstd(h_rs[:], h_ve[:], h_mv[:, :, 1], NT * NHX, 1e-5, r_gv, b.n + 1,
                     lambda i: link(i, pool_r, b, 2, "r"), r_gr)

            def finish_r(b):
                pool.wait_ge(r_n, b.n + 1)
                link(g.tensor_tensor(hs[:], hn[:].rearrange("p (t h) d -> p t (h d)", t=NT),
                                     onorm_bc[:].unsqueeze(1).broadcast_to([128, NT, C]), ALU.mult), pool_r, b, 2, "r")
                wait(pool, f_xu, b.n)
                g.tensor_tensor(x2[:], hs[:], x1[b.par][:], ALU.add).then_inc(x2_done, 1)

            def f_rstd_step(b):
                rstd(f_rs[:], f_ve[:], f_mv[:, :, 1], NT, 1e-5, f_var, b.n + 1,
                     lambda i: link(i, pool_f, b, 1, "f"), f_rstd)

            def f_sum(b):
                pool.wait_ge(f_u, b.n + 1)
                wait(pool, f_fin, 2 * (b.n - 1))
                g.tensor_tensor(xu[b.par][:], u_t[:], x2[:], ALU.add).then_inc(f_xu, 1)

            pool.wait_ge(misc_in, 96)

            def body(seqs):
                l0, l1, l2, l3, l4, l5 = seqs
                if l0: p_rstd_step(l0)
                if l3: r_rstd_step(l3)
                if l3: ctx_copy(l3)
                if l2: mask_probs(l2, 5)
                if l2: probs_low(l2, 5)
                if l1: mask_probs(l1, 0)
                if l4: h_rstd_step(l4)
                if l1: probs_low(l1, 0)
                if l4: finish_r(l4)
                if l3: mask_E(l3)
                if l4: f_rstd_step(l4)
                if l1: mask_probs(l1, 1)
                if l1: mask_probs(l1, 2)
                if l1: probs_low(l1, 1)
                if l1: probs_low(l1, 2)
                if l1: mask_probs(l1, 3)
                if l4: f_sum(l4)
                if l1: probs_low(l1, 3)
                if l1: mask_probs(l1, 4)
                if l1: probs_low(l1, 4)

            pipeline(body, nc.gpsimd)

        @block.scalar
        def _(act):
            a = nc.scalar
            a.preload_act_table_set("natural_log_exp_and_others")
            chain = {}

            def link(ins, seq):
                chain["r"] = chain.get("r", 0) % 3 + 1
                ins.then_inc(act_r, 1)
                act.wait_ge(act_r, 3 * seq.n + chain["r"])

            act.wait_ge(w_in, 112)
            act.wait_ge(g_sum, 2)
            for c in range(CH):
                a.activation(wqkv_h[:, c], wstage[:, c], ACT.Copy, scale=WS)
            a.activation(wo_h[:], wostage[:], ACT.Copy, scale=WS)
            a.activation(gw_h[:], gsum[:], ACT.Copy, scale=WS)
            a.activation(cent_h[:], cent32[:], ACT.Copy, scale=WS).then_inc(w_hi, 1)

            def expert_hi(seqs, place):
                for k in experts_of(seqs, NE + 1)[place:place + 1]:
                    if k < NE:
                        act.wait_ge(e_in[k % EB], 16 * (k // EB + 1))
                    else:
                        act.wait_ge(e_sum, 1)
                    a.activation(ew_h[:, :, k], estage[:, k % EB], ACT.Copy, scale=WS).then_inc(e_hi, 1)

            def xT_hi(b):
                act.wait_ge(p_xT, b.n + 1)
                wait(act, p_vp, 2 * b.n)
                a.activation(xT_h[:].rearrange("p c q -> p (c q)"), tp[:], ACT.Copy).then_inc(p_xh, 1)

            def high_parts(b, t):
                act.wait_ge(p_rot, 2 * b.n + t + 1)
                wait(act, q_rt, 2 * (b.n - 2) + t + 1)
                wait(act, p_tr, 4 * (b.n - 1) + 2 * t + 2)
                q_to = qst[b.par][:, t].rearrange("p h (a s) -> p h a s", a=2)[:, :, :, 0:DA]
                k_to = kst[:, t, :, 0:2 * DA].rearrange("p h (a s) -> p h a s", a=2)
                a.activation(q_to, rot[:, 0].unsqueeze(2).broadcast_to([128, NHA, 2, DA]), ACT.Copy)
                a.activation(k_to, rot[:, 1].unsqueeze(2).broadcast_to([128, NHA, 2, DA]), ACT.Copy).then_inc(p_hi, 1)

            def transposed(b, n):
                t, is_k = divmod(n, 2)
                act.wait_ge(p_tr, 4 * b.n + n + 1)
                wait(act, t_done if is_k else s_done, JOBS * (b.n - 1))
                dst = (kT if is_k else qT)[b.par]
                a.activation(dst[:, :, bass.ts(t, 128)], tp16, ACT.Copy).then_inc(p_te, 1)

            def v_out(b, t):
                act.wait_ge(p_vp, 2 * b.n + t + 1)
                wait(act, av_done, JOBS * (b.n - 1))
                a.activation(v17_h[b.par][:, t, :, 0:DA], proj[:, 0:C].rearrange("p (h d) -> p h d", h=NHA),
                             ACT.Copy).then_inc(p_vh, 1)

            def retransposed(b, t):
                act.wait_ge(q_rt, 2 * b.n + t + 1)
                wait(act, t_done, JOBS * (b.n - 1) + (2 if t == 0 else JOBS))
                a.activation(qmT[:, :, bass.ts(t, 128)], tp16, ACT.Copy).then_inc(q_rte, 1)

            def exp_job(b, j):
                act.wait_ge(t_done, JOBS * b.n + j + 1)
                wait(act, pl_done, JOBS * b.n + j - 1)
                a.activation(probs[j % 2][:], ring[1][:], ACT.Exp, scale=DA ** -0.5).then_inc(e_done, 1)

            def probs_high(b, j):
                act.wait_ge(k_done, JOBS * b.n + j + 1)
                wait(act, av_done, JOBS * b.n + j - PB + 1)
                a.activation(probs_h[j % PB][:], probs[j % 2][:], ACT.Copy).then_inc(ph_done, 1)

            def oT_hi(b, t):
                act.wait_ge(o_t, 2 * b.n + t + 1)
                wait(act, w_done, 2 * (b.n - 1) + t + 1)
                a.activation(oT_h[:, t].rearrange("p c q -> p (c q)"), tp[:, 0:C], ACT.Copy).then_inc(o_h, 1)

            def tr_hi(b):
                act.wait_ge(r_tr, b.n + 1)
                wait(act, r_qk, 2 * b.n)
                a.activation(tr_h[:].rearrange("p s c q -> p (s c q)"), ring[1][:], ACT.Copy).then_inc(r_th, 1)

            def gate_acts(b):
                act.wait_ge(r_g, b.n + 1)
                wait(act, r_sc, b.n)
                link(a.activation(fg[:], rbank[32:32 + NHX, 0:T], ACT.Identity, scale=1.0 / WS, bias=gbias[32:32 + NHX, :]), b)
                a.activation(ig[:], rbank[0:NHX, 0:T], ACT.Identity, scale=1.0 / WS, bias=gbias[0:NHX, :])
                link(a.activation(fg_a[:], fg[:], ACT.Abs), b)
                link(a.activation(fg_e[:], fg_a[:], ACT.Exp, scale=-1.0), b)
                a.activation(fg_l[:], fg_e[:], ACT.Ln, bias=1.0).then_inc(r_ga, 1)

            def columns(b):
                act.wait_ge(r_at, b.n + 1)
                cols = rbank[:, 256:256 + NT * 36].rearrange("p (t n) -> p t n", t=NT)
                a.activation(acol[:], cols[:, :, 0:NHX], ACT.Copy)
                a.activation(emd[:], cols[:, :, 32:32 + NHX], ACT.Exp, scale=-1.0).then_inc(r_ac, 1)

            def decay(b):
                act.wait_ge(r_ac, b.n + 1)
                act.wait_ge(r_mb, b.n + 1)
                wait(act, r_c, 2 * b.n)
                mb = ring[1][:].rearrange("p (h q) -> p h q", h=NHX)
                for h in range(NHX):
                    a.activation(E_t[:, h, 0:T], mb[:, h, :], ACT.Exp, scale=-1.0, bias=acol[:, 0, h:h + 1])
                    last = a.activation(E_t[:, h, T:T + 128], mb[:, h, 128:T], ACT.Exp, scale=-1.0, bias=acol[:, 1, h:h + 1])
                last.then_inc(r_e, 1)

            act.wait_ge(misc_in, 96)

            def uT_hi(b):
                act.wait_ge(f_ut, b.n + 1)
                wait(act, f_base, 2 * (b.n - 1))
                a.activation(uT_h[b.par][:].rearrange("p c q -> p (c q)"), tp[:], ACT.Copy).then_inc(f_uh, 1)

            def softmax_exp(b):
                act.wait_ge(f_sh, b.n + 1)
                a.activation(ex[:], lgs[:], ACT.Exp).then_inc(f_ex, 1)

            def gT_out(b):
                act.wait_ge(f_gt, b.n + 1)
                wait(act, f_base, 2 * b.n)
                a.activation(gT[:], rbank[0:NE + NS, 128:128 + T].rearrange("p (t q) -> p t q", t=NT), ACT.Copy).then_inc(f_gte, 1)

            def body(seqs):
                l0, l1, l2, l3, l4, l5 = seqs
                if l5: gT_out(l5)
                if l2: exp_job(l2, 5)
                if l0: xT_hi(l0)
                expert_hi(seqs, 0)
                if l2: probs_high(l2, 5)
                if l3: tr_hi(l3)
                if l1: retransposed(l1, 0)
                if l0: high_parts(l0, 0)
                if l3: gate_acts(l3)
                if l2: oT_hi(l2, 0)
                if l0: v_out(l0, 0)
                expert_hi(seqs, 1)
                if l1: exp_job(l1, 0)
                if l0: transposed(l0, 0)
                if l2: oT_hi(l2, 1)
                if l1: probs_high(l1, 0)
                expert_hi(seqs, 2)
                if l0: transposed(l0, 1)
                if l1: exp_job(l1, 1)
                if l3: columns(l3)
                if l3: decay(l3)
                if l0: high_parts(l0, 1)
                if l1: retransposed(l1, 1)
                if l0: v_out(l0, 1)
                if l0: transposed(l0, 2)
                if l1: exp_job(l1, 2)
                if l4: uT_hi(l4)
                if l1: probs_high(l1, 1)
                if l1: probs_high(l1, 2)
                if l4: softmax_exp(l4)
                if l1: exp_job(l1, 3)
                if l1: probs_high(l1, 3)
                if l1: exp_job(l1, 4)
                expert_hi(seqs, 3)
                if l0: transposed(l0, 3)
                if l1: probs_high(l1, 4)

            pipeline(body, nc.scalar)

        @block.vector
        def _(dve):
            v = nc.vector
            chain = {}

            def link(ins, s, seq, per, key):
                chain[key] = chain.get(key, 0) % per + 1
                ins.then_inc(s, 1)
                dve.wait_ge(s, seq.n * per + chain[key])

            dve.wait_ge(w_in, 112)
            dve.wait_ge(zeros_in, 2)
            for k, col in ((0, 0), (1, 32)):
                v.tensor_copy(gsum[:, 0:CH, col:col + NHX], gstage[:, k, 0:CH])
                v.tensor_tensor(gsum[:, CH:2 * CH, col:col + NHX], gstage[:, k, CH:2 * CH], gstage[:, k, 2 * CH:3 * CH],
                                ALU.add).then_inc(g_sum, 1)
            dve.wait_ge(g_sum, 2)
            dve.wait_ge(w_hi, 1)
            for lo, w, hi in ((wqkv_l, wstage, wqkv_h), (wo_l, wostage, wo_h), (gw_l, gsum, gw_h), (cent_l, cent32, cent_h)):
                last = v.scalar_tensor_tensor(lo[:].rearrange("p c n -> p (c n)"), w[:].rearrange("p c n -> p (c n)"), WS,
                                              hi[:].rearrange("p c n -> p (c n)"), ALU.mult, ALU.subtract)
            last.then_inc(w_lo, 1)
            dve.wait_ge(misc_in, 96)
            v.tensor_scalar(ball[:], ball[:], 2.0 * WS, None, ALU.mult).then_inc(w_lo, 1)

            def ln_stats(src, stats, mv, s, seq, per, key, done):
                for t in range(NT):
                    ins = v.bn_stats(stats[:, t], src[:, t])
                link(ins, s, seq, per, key)
                held(dve, dve_held)
                for t in range(NT):
                    ins = v.bn_aggr(mv[:, t], stats[:, t])
                ins.then_inc(done, 1)

            def expert_lo(seqs, place):
                for k in experts_of(seqs, NE + 1)[place:place + 1]:
                    w = estage[:, k % EB]
                    if k == NE:
                        for i in (k, k + 1):
                            dve.wait_ge(e_in[i % EB], 16 * (i // EB + 1))
                        v.tensor_tensor(w, w, estage[:, (k + 1) % EB], ALU.add).then_inc(e_sum, 1)
                    dve.wait_ge(e_hi, k + 1)
                    v.scalar_tensor_tensor(ew_l[:, :, k], w, WS, ew_h[:, :, k], ALU.mult, ALU.subtract).then_inc(e_lo, 1)

            def normalize(dst, src, mv, rs, done):
                for t in range(NT):
                    last = v.tensor_scalar(dst[:, t], src[:, t], mv[:, t, 0:1], rs[:, t:t + 1], ALU.subtract, ALU.mult)
                last.then_inc(done, 1)

            def p_norm(b):
                dve.wait_ge(p_rstd, b.n + 1)
                wait(dve, p_xT, b.n)
                normalize(p_xn_t, xin[b.par], p_mv, p_rs, p_xn)

            def p_xlo(b):
                dve.wait_ge(p_xh, b.n + 1)
                v.tensor_tensor(xT_l[:].rearrange("p c q -> p (c q)"), tp[:], xT_h[:].rearrange("p c q -> p (c q)"),
                                ALU.subtract).then_inc(p_xl, 1)

            def p_rope(b, t):
                dve.wait_ge(p_qk, 2 * b.n + t + 1)
                qk = proj[:].rearrange("p (h i two) -> p h i two", h=2 * NHA, two=2)

                def table(tab):
                    return tab[:, t].rearrange("p (i two) -> p i two", two=2).unsqueeze(1).broadcast_to([128, 2 * NHA, DA // 2, 2])

                shape = "p (h i two) -> p h i two"
                v.tensor_tensor(rope_a[:].rearrange(shape, h=2 * NHA, two=2), qk, table(cos_t), ALU.mult)
                v.tensor_tensor(rope_b[:].rearrange(shape, h=2 * NHA, two=2), qk[:, :, :, ::-1], table(sin_t),
                                ALU.mult).then_inc(p_roped, 1)
                dve.wait_ge(p_roped, 2 * b.n + t + 1)
                v.tensor_tensor(rot[:].rearrange("p s h d -> p (s h d)"), rope_a[:], rope_b[:], ALU.add).then_inc(p_rot, 1)

            def p_low(b, t):
                dve.wait_ge(p_hi, 2 * b.n + t + 1)
                v.tensor_tensor(qst[b.par][:, t, :, DA:2 * DA], rot[:, 0], qst[b.par][:, t, :, 0:DA], ALU.subtract)
                v.tensor_tensor(kst[:, t, :, 2 * DA:3 * DA], rot[:, 1], kst[:, t, :, 0:DA], ALU.subtract).then_inc(p_lo, 1)

            def v_low(b, t):
                dve.wait_ge(p_vh, 2 * b.n + t + 1)
                v.tensor_tensor(v17_l[b.par][:, t, :, 0:DA], proj[:, 0:C].rearrange("p (h d) -> p h d", h=NHA),
                                v17_h[b.par][:, t, :, 0:DA], ALU.subtract).then_inc(p_vev, 1)

            def max_job(b, j):
                dve.wait_ge(s_done, JOBS * b.n + j + 1)
                src = ring[1]
                if j < 2:
                    t, pairs, keys = 0, slice(4 * j, 4 * j + 4), 128
                else:
                    t, pairs, keys = 1, slice(2 * (j - 2), 2 * (j - 2) + 2), T
                to = qst[b.par][:, t].rearrange("p (k r) s -> p r k s", r=2)[:, :, pairs, 3 * DA]
                v.tensor_reduce(to, src[:].rearrange("p (r k q) -> p r k q", r=2, q=keys), axis=AX.X, op=ALU.max,
                                negate=True).then_inc(m_done, 1)

            def o_norm(b, t):
                dve.wait_ge(av_done, JOBS * b.n + (2 if t == 0 else JOBS))
                wait(dve, o_t, 2 * (b.n - 1) + t + 1)
                o = obank[:, 0:NHA * (DA + 1)].rearrange("p (h d) -> p h d", h=NHA)
                link(v.reciprocal(rec[:, t], o[:, :, DA]), dve_q, b, 2, "q")
                v.tensor_tensor(o_n[:, t].rearrange("p (h d) -> p h d", h=NHA), o[:, :, 0:DA],
                                rec[:, t].unsqueeze(2).broadcast_to([128, NHA, DA]), ALU.mult).then_inc(n_done, 1)

            def oT_lo(b, t):
                dve.wait_ge(o_h, 2 * b.n + t + 1)
                v.tensor_tensor(oT_l[:, t].rearrange("p c q -> p (c q)"), tp[:, 0:C], oT_h[:, t].rearrange("p c q -> p (c q)"),
                                ALU.subtract).then_inc(o_l, 1)

            def residual(b, t):
                if t == 0:
                    dve.wait_ge(xres_in[b.par], 16 * (b.half + 1))
                    wait(dve, x2_done, b.n - 1)
                dve.wait_ge(w_done, 2 * b.n + t + 1)
                v.scalar_tensor_tensor(x1[b.par][:, t], proj[:, 0:C], 1.0 / WS, xres[b.par][:, t], ALU.mult,
                                       ALU.add).then_inc(x1_done, 1)

            def r_stats_step(b):
                dve.wait_ge(x1_done, 2 * b.n + 2)
                ln_stats(x1[b.par], r_stats, r_mv, dve_g, b, KG, "g", r_var)

            def r_norm(b):
                dve.wait_ge(r_rstd, b.n + 1)
                wait(dve, r_tr, b.n)
                normalize(r_xn_t, x1[b.par], r_mv, r_rs, r_xn)

            def tr_lo(b):
                dve.wait_ge(r_th, b.n + 1)
                v.tensor_tensor(tr_l[:].rearrange("p s c q -> p (s c q)"), ring[1][:],
                                tr_h[:].rearrange("p s c q -> p (s c q)"), ALU.subtract).then_inc(r_tl, 1)

            def scans(b):
                dve.wait_ge(r_ga, b.n + 1)
                wait(dve, r_mb, b.n)
                link(v.scalar_tensor_tensor(lsig[:], fg[:], 0.0, fg_l[:], ALU.min, ALU.subtract), dve_g, b, KG, "g")
                link(v.tensor_tensor_scan(cs[:], lsig[:], zero_row[:], 0.0, ALU.add, ALU.add), dve_g, b, KG, "g")
                link(v.tensor_tensor(am[0:NHX, :], ig[:], cs[:], ALU.subtract), dve_g, b, KG, "g")
                link(v.tensor_tensor_scan(cmax[:], am[0:NHX, :], am[0:NHX, :], -3e38, ALU.max, ALU.max), dve_g, b, KG, "g")
                v.tensor_tensor(am[32:32 + NHX, :], cs[:], cmax[:], ALU.add).then_inc(r_sc, 1)
                hi, mid, lo = (cmax3[32 * k:32 * k + NHX, :] for k in range(3))
                link(v.tensor_copy(hi, cmax[:]), dve_g, b, KG, "g")
                link(v.tensor_tensor(cmax_r[:], cmax[:], hi, ALU.subtract), dve_g, b, KG, "g")
                link(v.tensor_copy(mid, cmax_r[:]), dve_g, b, KG, "g")
                v.tensor_tensor(lo, cmax_r[:], mid, ALU.subtract).then_inc(r_c3, 1)

            def weigh(b, c):
                if c == 0:
                    dve.wait_ge(r_em, b.n + 1)
                    wait(dve, r_h, 2 * b.n)
                dve.wait_ge(r_qk, 2 * b.n + c + 1)
                src = ring[1][:].rearrange("p (r q) -> p r q", r=2)[:, :, 0:384]
                v.scalar_tensor_tensor(C_t[:, 2 * c:2 * c + 2], src, DX ** -0.5, E_t[:, 2 * c:2 * c + 2], ALU.mult,
                                       ALU.mult).then_inc(r_c, 1)

            def h_scale(b, t):
                dve.wait_ge(r_h, 2 * b.n + t + 1)
                H = rbank[:, 0:NHX * (DX + 1)].rearrange("p (h d) -> p h d", h=NHX)
                link(v.scalar_tensor_tensor(nre[:, t], H[:, :, DX], -1.0, emd[:, t], ALU.mult, ALU.max), dve_r, b, KR, "h")
                link(v.tensor_tensor(nrm[:, t], H[:, :, DX], nre[:, t], ALU.max), dve_r, b, KR, "h")
                link(v.tensor_scalar(nre[:, t], nrm[:, t], 1e-6, None, ALU.add), dve_r, b, KR, "h")
                link(v.reciprocal(nrr[:, t], nre[:, t]), dve_r, b, KR, "h")
                v.tensor_tensor(hh[:, t], H[:, :, 0:DX], nrr[:, t].unsqueeze(2).broadcast_to([128, NHX, DX]),
                                ALU.mult).then_inc(r_hn, 1)

            def h_stats_step(b):
                dve.wait_ge(r_hn, 2 * b.n + 2)
                for k in range(NT * NHX):
                    ins = v.bn_stats(h_stats[:, k], hh[:, k // NHX, k % NHX])
                link(ins, dve_r, b, KR, "h")
                held(dve, dve_held)
                for k in range(NT * NHX):
                    ins = v.bn_aggr(h_mv[:, k], h_stats[:, k])
                ins.then_inc(r_gv, 1)
                dve.wait_ge(r_gv, b.n + 1)
                wait(dve, x2_done, b.n)
                link(v.tensor_tensor(hc[:], hh[:].rearrange("p t h d -> p (t h) d"),
                                     h_mv[:, :, 0:1].broadcast_to([128, NT * NHX, DX]), ALU.subtract), dve_r, b, KR, "h")

            def h_norm(b):
                dve.wait_ge(r_gr, b.n + 1)
                v.tensor_tensor(hn[:], hc[:], h_rs[:].unsqueeze(2).broadcast_to([128, NT * NHX, DX]), ALU.mult).then_inc(r_n, 1)

            KG = 1 + 7
            KR = 8 + 2

            def p_stats_step(b):
                dve.wait_ge(x_in[b.par], 16 * (b.half + 1))
                ln_stats(xin[b.par], p_stats, p_mv, dve_p, b, 1, "p", p_var)

            def f_stats_step(b):
                dve.wait_ge(x2_done, b.n + 1)
                ln_stats(x2, f_stats, f_mv, dve_f, b, KF, "f", f_var)

            def f_norm(b):
                dve.wait_ge(f_rstd, b.n + 1)
                wait(dve, f_ut, b.n)
                wait(dve, f_xu, b.n)
                normalize(u_t, x2, f_mv, f_rs, f_u)

            def uT_lo(b):
                dve.wait_ge(f_uh, b.n + 1)
                v.tensor_tensor(uT_l[b.par][:].rearrange("p c q -> p (c q)"), tp[:], uT_h[b.par][:].rearrange("p c q -> p (c q)"),
                                ALU.subtract).then_inc(f_ul, 1)

            def flink(ins, b):
                link(ins, dve_f, b, KF, "f")

            def logits(b):
                dve.wait_ge(f_rt, b.n + 1)
                rt = rbank[:, 0:NT * NE].rearrange("p (t e) -> p t e", t=NT)
                v.scalar_tensor_tensor(lg[:], rt, 1.0 / WS, ebias_bc[:].unsqueeze(1).broadcast_to([128, NT, NE]), ALU.mult,
                                       ALU.add).then_inc(f_lg, 1)
                dve.wait_ge(f_lg, b.n + 1)
                held(dve, dve_held)
                for t in range(NT):
                    last = v.max(mx8[:, t], lg[:, t])
                flink(last, b)
                v.tensor_tensor(lgs[:], lg[:], mx8[:, :, 0:1].broadcast_to([128, NT, NE]), ALU.subtract).then_inc(f_sh, 1)

            def top_two(b):
                dve.wait_ge(f_ex, b.n + 1)
                flink(v.tensor_reduce(exsum[:], ex[:], axis=AX.X, op=ALU.add), b)
                flink(v.reciprocal(exrec[:], exsum[:]), b)
                flink(v.tensor_tensor(sm[:], ex[:], exrec[:].unsqueeze(2).broadcast_to([128, NT, NE]), ALU.mult), b)
                held(dve, dve_held)
                for t in range(NT):
                    last = v.max(top8[:, t], sm[:, t])
                flink(last, b)

            def select(b):
                held(dve, dve_held)
                for t in range(NT):
                    last = v.max_index(idx8[:, t], top8[:, t], sm[:, t])
                flink(last, b)
                flink(v.tensor_copy(idxf[:], idx8[:, :, 0:2]), b)
                for t in range(NT):
                    v.tensor_scalar(g1[:, t], iota16[:], idxf[:, t, 0:1], top8[:, t, 0:1], ALU.is_equal, ALU.mult)
                    last = v.tensor_scalar(g2[:, t], iota16[:], idxf[:, t, 1:2], top8[:, t, 1:2], ALU.is_equal, ALU.mult)
                flink(last, b)
                wait(dve, f_gt, b.n)
                flink(v.tensor_tensor(gate[:, :, 0:NE], g1[:], g2[:], ALU.add), b)
                wait(dve, f_fin, 2 * (b.n - 1))
                v.tensor_scalar(gsc[b.par][:], gate[:, :, 0:NE], 1.0 / WS, None, ALU.mult).then_inc(f_g, 1)

            KF = 1 + 1 + 8

            def combine(b, q):
                t, quad = divmod(q, 4)
                if q == 0:
                    dve.wait_ge(f_g, b.n + 1)
                    dve.wait_ge(f_xu, b.n + 1)
                if quad == 0:
                    wait(dve, f_fin, 2 * (b.n - 1) + t + 1)
                dve.wait_ge(f_quad, 8 * b.n + q + 1)
                src = ring[0][:].rearrange("p (e c) -> p e c", e=4)
                for k in range(4):
                    e = 4 * quad + k
                    to, g = acc[:, t, k % 2], gsc[b.par][:, t, e:e + 1]
                    if e == 1:
                        ins = v.tensor_scalar(to, src[:, k], g, None, ALU.mult)
                    else:
                        if t == 1 and e == 12:
                            dve.wait_ge(f_baseread, 2 * b.n + 2)
                        elif e >= 2:
                            dve.wait_ge(f_comb, 32 * b.n + 16 * t + e - 1)
                        ins = v.scalar_tensor_tensor(to, src[:, k], g, xu[b.par][:, t] if e == 0 else to, ALU.mult, ALU.add)
                    ins.then_inc(f_comb, 1)

            def add_base(b, t):
                dve.wait_ge(f_base, 2 * b.n + t + 1)
                dve.wait_ge(f_comb, 32 * b.n + (16 if t == 0 else 28))
                v.scalar_tensor_tensor(acc[:, t, 0], proj[:, 0:C], 0.5 / WS, acc[:, t, 0], ALU.mult, ALU.add).then_inc(f_baseread, 1)

            def close(b, t):
                dve.wait_ge(f_baseread, 2 * b.n + t + 1)
                dve.wait_ge(f_comb, 32 * b.n + 16 * (t + 1))
                if t == 0:
                    wait(dve, out_sent[b.par], 16 * b.half)
                v.tensor_tensor(fin[b.par][:, t], acc[:, t, 0], acc[:, t, 1], ALU.add).then_inc(f_fin, 1)

            def body(seqs):
                l0, l1, l2, l3, l4, l5 = seqs
                if l0: p_stats_step(l0)
                if l1: max_job(l1, 2)
                if l3: r_stats_step(l3)
                if l0: p_norm(l0)
                if l5: combine(l5, 0)
                if l3: r_norm(l3)
                if l4: h_scale(l4, 0)
                if l1: max_job(l1, 3)
                if l0: p_xlo(l0)
                expert_lo(seqs, 0)
                if l5: combine(l5, 1)
                if l4: h_scale(l4, 1)
                if l3: tr_lo(l3)
                if l0: p_rope(l0, 0)
                if l5: combine(l5, 2)
                if l1: max_job(l1, 4)
                if l4: h_stats_step(l4)
                if l0: p_low(l0, 0)
                if l2: o_norm(l2, 1)
                if l2: oT_lo(l2, 0)
                if l0: v_low(l0, 0)
                if l5: combine(l5, 3)
                if l1: max_job(l1, 5)
                if l2: oT_lo(l2, 1)
                if l3: scans(l3)
                if l4: h_norm(l4)
                if l5: combine(l5, 4)
                if l0: p_rope(l0, 1)
                if l4: f_stats_step(l4)
                if l0: p_low(l0, 1)
                if l3: weigh(l3, 0)
                if l0: v_low(l0, 1)
                if l4: f_norm(l4)
                expert_lo(seqs, 1)
                if l5: combine(l5, 5)
                if l5: add_base(l5, 0)
                if l4: uT_lo(l4)
                if l0: max_job(l0, 0)
                if l4: logits(l4)
                if l4: top_two(l4)
                if l2: residual(l2, 0)
                if l5: close(l5, 0)
                if l5: combine(l5, 6)
                if l4: select(l4)
                if l3: weigh(l3, 1)
                if l5: add_base(l5, 1)
                if l1: o_norm(l1, 0)
                expert_lo(seqs, 2)
                expert_lo(seqs, 3)
                if l5: combine(l5, 7)
                if l5: close(l5, 1)
                if l0: max_job(l0, 1)
                if l2: residual(l2, 1)

            pipeline(body, nc.vector)

        @block.tensor
        def _(pe):
            m = nc.tensor

            def split_product(dst, pieces, skip=False):
                for k, (lhsT, rhs) in enumerate(pieces):
                    last = m.matmul(dst, lhsT, rhs, start=k == 0, stop=k == len(pieces) - 1)
                return last

            def xT(b):
                pe.wait_ge(p_xn, b.n + 1)
                for c in range(CH):
                    for t in range(NT):
                        last = m.transpose(tp[:, bass.ds(c * T + t * 128, 128)], p_xn_t[:, t, bass.ts(c, 128)], ident[:])
                last.then_inc(p_xT, 1)

            def project(b, t, cols, done):
                if t == 0:
                    pe.wait_ge(p_xl, b.n + 1)
                q = bass.ts(t, 128)
                pieces = []
                for c in range(CH):
                    pieces += [(xT_h[:, c, q], wqkv_h[:, c, cols]), (xT_h[:, c, q], wqkv_l[:, c, cols]),
                               (xT_l[:, c, q], wqkv_h[:, c, cols])]
                split_product(proj[:, 0:cols.stop - cols.start], pieces).then_inc(done, 1)

            def transpose_heads(src, t, done):
                for k in range(NP):
                    last = m.transpose(tp16[:, k], src[:, t, 2 * k:2 * k + 2].rearrange("p r s -> p (r s)"), ident16[:])
                last.then_inc(done, 1)

            def scores(b, j):
                bank_free(pe, "ring1", f"s{j}", cur[0])
                if j in (0, 2):
                    pe.wait_ge(p_te, 4 * b.n + (2 if j == 0 else 4))
                if j < 2:
                    t, pairs, keys, per = 0, range(4 * j, 4 * j + 4), 128, 4
                else:
                    t, pairs, keys, per = 1, range(2 * (j - 2), 2 * (j - 2) + 2), T, 2
                out4 = ring[1][:].rearrange("p (r k q) -> p r k q", r=2, q=keys)
                for r in range(2):
                    for h2 in range(0, per, 2):
                        m.matmul(out4[:, r, h2:h2 + 2, keys - 128:keys], identb[:], causal[:], start=h2 == 0, stop=False,
                                 skip_group_check=True)
                for k, pair in enumerate(pairs):
                    for r in range(2):
                        rows = slice(64 * r, 64 * r + 3 * DA)
                        last = m.matmul(out4[:, r, k], qT[b.par][rows, pair, bass.ts(t, 128)], kT[b.par][rows, pair, 0:keys],
                                        start=False, stop=True, skip_group_check=True)
                last.then_inc(s_done, 1)

            def reT(b, t):
                pe.wait_ge(m_done, JOBS * b.n + (2 if t == 0 else JOBS))
                transpose_heads(qst[b.par], t, q_rt)

            def scoresT(b, j):
                bank_free(pe, "ring1", f"t{j}", cur[0])
                if j in (0, 2):
                    pe.wait_ge(q_rte, 2 * b.n + (1 if j == 0 else 2))
                if j < 2:
                    out4 = ring[1][:].rearrange("p (r k a q) -> p r k a q", r=2, k=4, a=1)
                    t, pairs = 0, range(4 * j, 4 * j + 4)
                else:
                    out4 = ring[1][:].rearrange("p (r k a q) -> p r k a q", r=2, k=2, a=2)
                    t, pairs = 1, range(2 * (j - 2), 2 * (j - 2) + 2)
                for k, pair in enumerate(pairs):
                    for kt in range(t + 1):
                        for r in range(2):
                            rows = slice(64 * r, 64 * r + 64)
                            last = m.matmul(out4[:, r, k, kt], kT[b.par][rows, pair, bass.ts(kt, 128)],
                                            qmT[rows, pair, bass.ts(t, 128)], start=True, stop=True)
                last.then_inc(t_done, 1)

            def values(b, j):
                if j in (0, 2):
                    bank_free(pe, "obank", "o0" if j == 0 else "o1", cur[0])
                    pe.wait_ge(p_vev, 2 * b.n + (1 if j == 0 else 2))
                pe.wait_ge(pl_done, JOBS * b.n + j + 1)
                o = obank[:, 0:NHA * (DA + 1)].rearrange("p (h d) -> p h d", h=NHA)
                t = 0 if j < 2 else 1
                pairs = range(4 * j, 4 * j + 4) if j < 2 else range(2 * (j - 2), 2 * (j - 2) + 2)
                ph, pl = (x[j % PB][:].rearrange("p (r k a q) -> p r k a q", r=2, k=len(pairs), q=128) for x in (probs_h, probs_l))
                vh, vl = v17_h[b.par], v17_l[b.par]
                for r in range(2):
                    for k, pair in enumerate(pairs):
                        head = 2 * pair + r
                        pieces = []
                        for kt in range(t + 1):
                            hi, lo = ph[:, r, k, kt], pl[:, r, k, kt]
                            pieces += [(hi, vh[:, kt, head]), (hi, vl[:, kt, head]), (lo, vh[:, kt, head])]
                        last = split_product(o[:, head], pieces)
                last.then_inc(av_done, 1)

            def oT(b, t):
                pe.wait_ge(n_done, 2 * b.n + t + 1)
                for c in range(CH):
                    last = m.transpose(tp[:, bass.ts(c, 128)], o_n[:, t, bass.ts(c, 128)], ident[:])
                last.then_inc(o_t, 1)

            def project_out(b, t):
                pe.wait_ge(o_l, 2 * b.n + t + 1)
                pieces = []
                for c in range(CH):
                    pieces += [(oT_h[:, t, c], wo_h[:, c]), (oT_h[:, t, c], wo_l[:, c]), (oT_l[:, t, c], wo_h[:, c])]
                split_product(proj[:, 0:C], pieces).then_inc(w_done, 1)

            def tr(b):
                bank_free(pe, "ring1", "tr", cur[0])
                pe.wait_ge(ctx_in[b.par], 16 * (b.half + 1))
                pe.wait_ge(r_xn, b.n + 1)
                to = ring[1][:].rearrange("p (s c q) -> p s c q", s=2, c=CH)
                for s, src in ((0, ctx_t[b.par]), (1, r_xn_t)):
                    for c in range(CH):
                        for t in range(NT):
                            last = m.transpose(to[:, s, c, bass.ts(t, 128)], src[:, t, bass.ts(c, 128)], ident[:])
                last.then_inc(r_tr, 1)

            def gates(b):
                bank_free(pe, "rbank", "gates", cur[0])
                pe.wait_ge(r_tl, b.n + 1)
                pieces = []
                for s, w0 in ((1, 0), (0, CH)):
                    for c in range(CH):
                        pieces += [(gw_h[:, w0 + c], tr_h[:, s, c]), (gw_h[:, w0 + c], tr_l[:, s, c]), (gw_l[:, w0 + c], tr_h[:, s, c])]
                split_product(rbank[0:36, 0:T], pieces).then_inc(r_g, 1)

            def aT(b):
                bank_free(pe, "rbank", "aT", cur[0])
                pe.wait_ge(r_sc, b.n + 1)
                held(pe, pe_held)
                for t in range(NT):
                    last = m.transpose(rbank[:, 256 + 36 * t:256 + 36 * t + 36], am[:, bass.ts(t, 128)], ident[0:36, 0:36])
                last.then_inc(r_at, 1)

            def mb(b):
                bank_free(pe, "ring1", "mb", cur[0])
                pe.wait_ge(r_c3, b.n + 1)
                to = ring[1][:].rearrange("p (h q) -> p h q", h=NHX)
                for h in range(NHX):
                    last = m.matmul(to[:, h], headsel[:, h], cmax3[:], start=True, stop=True)
                last.then_inc(r_mb, 1)

            def xqk(b, c):
                bank_free(pe, "ring1", f"qk{c}", cur[0])
                to = ring[1][:].rearrange("p (r q) -> p r q", r=2)
                for kt in range(NT):
                    for n, (kp, xp) in enumerate(((tr_h, tr_h), (tr_l, tr_h), (tr_h, tr_l))):
                        for r in range(2):
                            rows = slice(64 * r, 64 * r + 64)
                            dst = to[:, r, 0:T] if kt == 0 else to[:, r, T:T + 128]
                            last = m.matmul(dst, kp[rows, 0, c, bass.ts(kt, 128)], xp[rows, 1, c, kt * 128:T], start=n == 0, stop=n == 2)
                last.then_inc(r_qk, 1)

            def xvalues(b, t):
                bank_free(pe, "rbank", f"h{t}", cur[0])
                if t == 0:
                    pe.wait_ge(r_c, 2 * b.n + 2)
                    pe.wait_ge(c_cp, b.n + 1)
                H = rbank[:, 0:NHX * (DX + 1)].rearrange("p (h d) -> p h d", h=NHX)
                for h in range(NHX):
                    for kt in range(t + 1):
                        cols = slice(128 * t, 128 * t + 128) if kt == 0 else slice(256, 384)
                        last = m.matmul(H[:, h], C_t[:, h, cols], ctx65[b.par][:, kt, h], start=kt == 0, stop=kt == t)
                last.then_inc(r_h, 1)

            cur = [None]
            pe.wait_ge(pool_ready, 3)
            pe.wait_ge(w_lo, 2)

            def tp_use(name, st, fn, *args):
                bank_free(pe, "tp", name, st)
                fn(*args)

            def proj_use(name, st, fn, *args):
                bank_free(pe, "proj", name, st)
                fn(*args)

            def heads_of(b, t, is_k):
                if not is_k:
                    pe.wait_ge(p_lo, 2 * b.n + t + 1)
                transpose_heads(kst if is_k else qst[b.par], t, p_tr)

            QK, V = slice(0, 2 * C), slice(2 * C, 3 * C)

            def uT(b):
                pe.wait_ge(f_u, b.n + 1)
                for c in range(CH):
                    for t in range(NT):
                        last = m.transpose(tp[:, bass.ds(c * T + t * 128, 128)], u_t[:, t, bass.ts(c, 128)], ident[:])
                last.then_inc(f_ut, 1)

            def split_u(b, t, wh, wl):
                h, l, q = uT_h[b.par], uT_l[b.par], bass.ts(t, 128)
                return [x for c in range(CH) for x in ((h[:, c, q], wh(c)), (h[:, c, q], wl(c)), (l[:, c, q], wh(c)))]

            def router(b):
                bank_free(pe, "rbank", "rt", cur[0])
                pe.wait_ge(f_ul, b.n + 1)
                for t in range(NT):
                    last = split_product(rbank[:, bass.ts(t, NE)], split_u(b, t, lambda c: cent_h[:, c], lambda c: cent_l[:, c]))
                last.then_inc(f_rt, 1)

            def gates_T(b):
                bank_free(pe, "rbank", "gT", cur[0])
                pe.wait_ge(f_g, b.n + 1)
                for t in range(NT):
                    last = m.transpose(rbank[0:NE + NS, 128 + 128 * t:256 + 128 * t], gate[:, t], ident[:])
                last.then_inc(f_gt, 1)

            def base(b, t):
                pe.wait_ge(f_gte, b.n + 1)
                if isinstance(b.n, int) and b.n == 0 and t == 0:
                    pe.wait_ge(e_lo, NE + 1)
                pieces = split_u(b, t, lambda c: ew_h[:, c, NE], lambda c: ew_l[:, c, NE])
                split_product(proj[:, 0:C], pieces + [(gT[:, t], ball[:])]).then_inc(f_base, 1)

            def quad(b, q):
                bank_free(pe, "ring0", f"c{q}", cur[0])
                if isinstance(b.n, int) and b.n == 0 and q == 0:
                    pe.wait_ge(e_lo, NE)
                t, k = divmod(q, 4)
                for half in range(2):
                    es = slice(4 * k + 2 * half, 4 * k + 2 * half + 2)
                    last = split_product(ring[0][:, bass.ts(half, 512)],
                                         split_u(b, t, lambda c: ew_h[:, c, es].rearrange("p e o -> p (e o)"),
                                                 lambda c: ew_l[:, c, es].rearrange("p e o -> p (e o)")))
                last.then_inc(f_quad, 1)

            def body(seqs):
                l0, l1, l2, l3, l4, l5 = cur[0] = seqs
                if l1: scores(l1, 2)
                if l5: quad(l5, 0)
                if l5: gates_T(l5)
                if l2: scoresT(l2, 5)
                if l4: xvalues(l4, 0)
                if l1: scores(l1, 3)
                if l0: tp_use("xT", seqs, xT, l0)
                if l5: quad(l5, 1)
                if l4: xvalues(l4, 1)
                if l3: tr(l3)
                if l0: proj_use("qk0", seqs, project, l0, 0, QK, p_qk)
                if l5: quad(l5, 2)
                if l1: tp_use("reT0", seqs, reT, l1, 0)
                if l1: scores(l1, 4)
                if l3: gates(l3)
                if l2: tp_use("oT0", seqs, oT, l2, 0)
                if l0: proj_use("v0", seqs, project, l0, 0, V, p_vp)
                if l2: values(l2, 4)
                if l2: values(l2, 5)
                if l1: scoresT(l1, 0)
                if l5: quad(l5, 3)
                if l0: tp_use("tq0", seqs, heads_of, l0, 0, False)
                if l1: scores(l1, 5)
                if l2: tp_use("oT1", seqs, oT, l2, 1)
                if l0: proj_use("qk1", seqs, project, l0, 1, QK, p_qk)
                if l0: tp_use("tk0", seqs, heads_of, l0, 0, True)
                if l5: quad(l5, 4)
                if l1: scoresT(l1, 1)
                if l1: tp_use("reT1", seqs, reT, l1, 1)
                if l3: aT(l3)
                if l3: mb(l3)
                if l5: quad(l5, 5)
                if l3: xqk(l3, 0)
                if l0: proj_use("v1", seqs, project, l0, 1, V, p_vp)
                if l0: tp_use("tq1", seqs, heads_of, l0, 1, False)
                if l1: values(l1, 0)
                if l1: scoresT(l1, 2)
                if l5: proj_use("b0", seqs, base, l5, 0)
                if l4: tp_use("uT", seqs, uT, l4)
                if l0: scores(l0, 0)
                if l2: proj_use("w0", seqs, project_out, l2, 0)
                if l4: router(l4)
                if l5: quad(l5, 6)
                if l1: scoresT(l1, 3)
                if l1: values(l1, 1)
                if l5: proj_use("b1", seqs, base, l5, 1)
                if l3: xqk(l3, 1)
                if l5: quad(l5, 7)
                if l1: scoresT(l1, 4)
                if l1: values(l1, 2)
                if l0: tp_use("tk1", seqs, heads_of, l0, 1, True)
                if l0: scores(l0, 1)
                if l2: proj_use("w1", seqs, project_out, l2, 1)
                if l1: values(l1, 3)

            pipeline(body, nc.tensor)


def kernel(**inputs):
    import numpy as np
    import concourse.bacc as bacc
    from concourse.bass_utils import run_bass_kernel_spmd as run

    def lay(a):
        return np.ascontiguousarray(a)

    inv = 1.0 / 10000.0 ** (np.arange(0, DA, 2, dtype=np.float32) / DA)
    ang = np.outer(np.arange(T, dtype=np.float32), inv.astype(np.float32)).astype(np.float32)
    cos = np.repeat(np.cos(ang), 2, axis=1) / WS
    sin = np.repeat(np.sin(ang), 2, axis=1) / WS * np.tile([-1.0, 1.0], DA // 2)
    def tiles(a):
        return lay(a.astype(np.float32).reshape(NT, 128, DA).transpose(1, 0, 2))

    arrays = {
        "x": lay(inputs["x"]), "ctx": lay(inputs["ctx_1024"]), "w_qkv": lay(inputs["L0_attn_w_qkv"]),
        "w_out": lay(inputs["L0_attn_w_out"]), "igk": lay(inputs["L0_xattn_igate_kernel"]),
        "igb": lay(inputs["L0_xattn_igate_bias"]), "fgk": lay(inputs["L0_xattn_fgate_kernel"]),
        "fgb": lay(inputs["L0_xattn_fgate_bias"]), "onorm": lay(inputs["L0_xattn_outnorm_scale"]),
        "centT": lay(np.asarray(inputs["L0_ffn_centroids"]).T), "ebias": lay(inputs["L0_ffn_expert_biases"]),
        "WrT": lay(np.asarray(inputs["L0_ffn_Wr"]).transpose(2, 0, 1)), "br": lay(inputs["L0_ffn_br"]),
        "WsT": lay(np.asarray(inputs["L0_ffn_Ws"]).transpose(2, 0, 1)), "bs": lay(inputs["L0_ffn_bs"]),
        "rope_cos": tiles(cos), "rope_sin": tiles(sin),
    }
    nc = bacc.Bacc("TRN2", target_bir_lowering=False, num_devices=1)
    args = [nc.dram_tensor(f"in_{k}", a.shape, mybir.dt.from_np(a.dtype), kind="ExternalInput").ap() for k, a in arrays.items()]
    args.append(nc.dram_tensor("out_y", (B, T, C), mybir.dt.float32, kind="ExternalOutput").ap())
    decoder_layer(nc, *args)
    r = run(nc, [{f"in_{k}": a for k, a in arrays.items()}], core_ids=[0])
    return r.results[0]["out_y"]
```

```python
import concourse.bass as bass
from concourse import mybir
from contextlib import ExitStack
from collections import namedtuple

B, T, C = 16, 256, 256
NT = T // 128
CH = C // 128
NHA, DA = 16, C // 16
NP = NHA // 2
NHX, DX = 4, C // 4
NE, NS = 16, 2
WS = 64.0
NEG = -1e30
PB = 3
JOBS = 6

Seq = namedtuple("Seq", "n half par")
LAGS = 6


def decoder_layer(nc, x, ctx, w_qkv, w_out, igk, igb, fgk, fgb, onorm, centT, ebias, WrT, br, WsT, bs, rope_cos, rope_sin, out):
    f32, f16, bf16, u32 = mybir.dt.float32, mybir.dt.float16, mybir.dt.bfloat16, mybir.dt.uint32
    ALU, ACT, AX = mybir.AluOpType, mybir.ActivationFunctionType, mybir.AxisListType

    stack = ExitStack()
    with stack:
        def sb(name, shape, dt=f32):
            return stack.enter_context(nc.sbuf_tensor(name, shape, dt))

        EB = 4

        def sem(name):
            return stack.enter_context(nc.semaphore(name))

        ident = sb("ident", [128, 128])
        ident16 = sb("ident16", [128, 128], f16)
        identb = sb("identb", [128, 128], bf16)
        causal = sb("causal", [128, 2, 128], bf16)
        zero_row = sb("zero_row", [NHX, T])
        headsel = sb("headsel", [64 + NHX, NHX, 128], bf16)
        mhalf = sb("mhalf", [128, 8])
        zero_ln = sb("zero_ln", [128, NT])
        iota16 = sb("iota16", [128, NE])
        cos_t = sb("cos_t", [128, NT, DA])
        sin_t = sb("sin_t", [128, NT, DA])
        wstage = sb("wstage", [128, CH, 3 * C])
        wostage = sb("wostage", [128, CH, C])
        wqkv_h = sb("wqkv_h", [128, CH, 3 * C], f16)
        wqkv_l = sb("wqkv_l", [128, CH, 3 * C], f16)
        wo_h = sb("wo_h", [128, CH, C], f16)
        wo_l = sb("wo_l", [128, CH, C], f16)
        gstage = sb("gstage", [128, 2, 3 * CH, NHX])
        gsum = sb("gsum", [128, 2 * CH, 36])
        gw_h = sb("gw_h", [128, 2 * CH, 36], f16)
        gw_l = sb("gw_l", [128, 2 * CH, 36], f16)
        gbias = sb("gbias", [36, 1])
        onorm_bc = sb("onorm_bc", [128, C])
        cent32 = sb("cent32", [128, CH, NE])
        cent_h = sb("cent_h", [128, CH, NE], f16)
        cent_l = sb("cent_l", [128, CH, NE], f16)
        ebias_bc = sb("ebias_bc", [128, NE])
        ball = sb("ball", [NE + NS, C])
        estage = sb("estage", [128, EB, CH, C])
        ew_h = sb("ew_h", [128, CH, NE + 1, C], f16)
        ew_l = sb("ew_l", [128, CH, NE + 1, C], f16)

        xin = [sb(f"xin{i}", [128, NT, C]) for i in range(2)]
        p_stats = sb("p_stats", [128, NT, 6])
        p_mv = sb("p_mv", [128, NT, 2])
        p_ve = sb("p_ve", [128, NT])
        p_rs = sb("p_rs", [128, NT])
        p_off = sb("p_off", [128, NT])
        p_xn_t = sb("p_xn_t", [128, NT, C])
        xT_h = sb("xT_h", [128, CH, T], f16)
        xT_l = sb("xT_l", [128, CH, T], f16)
        rope_a = sb("rope_a", [128, 2 * C])
        rope_b = sb("rope_b", [128, 2 * C])
        rot = sb("rot", [128, 2, NHA, DA])
        qst = [sb(f"qst{i}", [128, NT, NHA, 64], f16) for i in range(2)]
        kst = sb("kst", [128, NT, NHA, 64], f16)
        qT = [sb(f"qT{i}", [128, NP, T], f16) for i in range(2)]
        kT = [sb(f"kT{i}", [128, NP, T], f16) for i in range(2)]
        v17_h = [sb(f"v17_h{i}", [128, NT, NHA, DA + 1], f16) for i in range(2)]
        v17_l = [sb(f"v17_l{i}", [128, NT, NHA, DA + 1], f16) for i in range(2)]

        xres = [sb(f"xres{i}", [128, NT, C]) for i in range(2)]
        qmT = sb("qmT", [128, NP, T], f16)
        probs = [sb(f"probs{i}", [128, 1024]) for i in range(2)]
        probs_h = [sb(f"probs_h{i}", [128, 1024], f16) for i in range(PB)]
        probs_l = [sb(f"probs_l{i}", [128, 1024], f16) for i in range(PB)]
        rec = sb("rec", [128, NT, NHA])
        o_n = sb("o_n", [128, NT, C])
        oT_h = sb("oT_h", [128, NT, CH, 128], f16)
        oT_l = sb("oT_l", [128, NT, CH, 128], f16)
        x1 = [sb(f"x1_{i}", [128, NT, C]) for i in range(2)]

        ctx_t = [sb(f"ctx{i}", [128, NT, C]) for i in range(2)]
        ctx65_h = [sb(f"ctx65_h{i}", [128, NT, NHX, DX + 1], f16) for i in range(2)]
        ctx65_l = [sb(f"ctx65_l{i}", [128, NT, NHX, DX + 1], f16) for i in range(2)]
        r_stats = sb("r_stats", [128, NT, 6])
        r_mv = sb("r_mv", [128, NT, 2])
        r_ve = sb("r_ve", [128, NT])
        r_rs = sb("r_rs", [128, NT])
        r_off = sb("r_off", [128, NT])
        r_xn_t = sb("r_xn_t", [128, NT, C])
        tr_h = sb("tr_h", [128, 2, CH, T], f16)
        tr_l = sb("tr_l", [128, 2, CH, T], f16)
        fg = sb("fg", [NHX, T])
        fg_a = sb("fg_a", [NHX, T])
        fg_e = fg_l = fg_a
        ig = sb("ig", [NHX, T])
        lsig = fg
        cs = sb("cs", [NHX, T])
        am = sb("am", [36, T])
        cmax = sb("cmax", [NHX, T])
        cmax_r = sb("cmax_r", [NHX, T])
        cmax3 = sb("cmax3", [64 + NHX, T], bf16)
        acol = sb("acol", [128, NT, NHX])
        emd = sb("emd", [128, NT, NHX])
        E_t = wstage[:].rearrange("p c n -> p (c n)").rearrange("p (h q) -> p h q", h=NHX)
        C_t = sb("C_t", [128, NHX, 3 * 128])
        C_h = sb("C_h", [128, NHX, 3 * 128], f16)
        C_l = sb("C_l", [128, NHX, 3 * 128], f16)
        nrm = sb("nrm", [128, NT, NHX])
        nre = sb("nre", [128, NT, NHX])
        nrr = sb("nrr", [128, NT, NHX])
        hh = sb("hh", [128, NT, NHX, DX])
        h_stats = sb("h_stats", [128, NT * NHX, 6])
        h_mv = sb("h_mv", [128, NT * NHX, 2])
        h_ve = sb("h_ve", [128, NT * NHX])
        h_rs = sb("h_rs", [128, NT * NHX])
        hc = hn = hh[:].rearrange("p t h d -> p (t h) d")
        hs = wostage
        x2 = sb("x2", [128, NT, C])

        f_stats = sb("f_stats", [128, NT, 6])
        f_mv = sb("f_mv", [128, NT, 2])
        f_ve = sb("f_ve", [128, NT])
        f_rs = sb("f_rs", [128, NT])
        f_off = sb("f_off", [128, NT])
        u_t = sb("u_t", [128, NT, C])
        xu = [sb(f"xu{i}", [128, NT, C]) for i in range(2)]
        uT_h = [sb(f"uT_h{i}", [128, CH, T], f16) for i in range(2)]
        uT_l = [sb(f"uT_l{i}", [128, CH, T], f16) for i in range(2)]
        lg = sb("lg", [128, NT, NE])
        lgs = sb("lgs", [128, NT, NE])
        mx8 = sb("mx8", [128, NT, 8])
        ex = sb("ex", [128, NT, NE])
        exsum = sb("exsum", [128, NT])
        exrec = sb("exrec", [128, NT])
        sm = sb("sm", [128, NT, NE])
        top8 = sb("top8", [128, NT, 8])
        idx8 = sb("idx8", [128, NT, 8], u32)
        idxf = sb("idxf", [128, NT, 2])
        g1 = sb("g1", [128, NT, NE])
        g2 = sb("g2", [128, NT, NE])
        gate = sb("gate", [128, NT, NE + NS])
        gsc = [sb(f"gsc{i}", [128, NT, NE]) for i in range(2)]
        gT = sb("gT", [NE + NS, NT, 128])
        acc = sb("acc", [128, NT, 2, C])
        fin = [sb(f"fin{i}", [128, NT, C]) for i in range(2)]

        ring = [stack.enter_context(nc.psum_tensor(f"ring{i}", [128, 1024], f32)) for i in range(2)]
        proj = stack.enter_context(nc.psum_tensor("proj", [128, 512], f32))
        tp = stack.enter_context(nc.psum_tensor("tp", [128, 512], f32))
        obank = stack.enter_context(nc.psum_tensor("obank", [128, 512], f32))
        rbank = stack.enter_context(nc.psum_tensor("rbank", [128, 512], f32))
        tp16 = tp[:, :].bitcast(f16).rearrange("p (a q) -> p a q", a=NP)

        w_in, pool_ready, w_hi, w_lo, g_sum, zeros_in = map(sem, ("w_in", "pool_ready", "w_hi", "w_lo", "g_sum", "zeros_in"))
        misc_in, dve_held, pe_held, pool_held, dve_g, pool_g = map(sem, ("misc_in", "dve_held", "pe_held", "pool_held", "dve_g", "pool_g"))
        x_in, xres_in, ctx_in = ([sem(f"{n}{i}") for i in range(2)] for n in ("x_in", "xres_in", "ctx_in"))
        names = ("p_var p_rstd p_xn p_xT p_xh p_xl p_qk p_roped p_rot p_hi p_lo p_tr p_te p_vp p_vh p_vev dve_p pool_p "
                 "s_done m_done q_rt q_rte t_done e_done k_done ph_done pl_done av_done n_done o_t o_h o_l w_done x1_done dve_q "
                 "c_hi c_cp r_var r_rstd r_xn r_tr r_th r_tl r_g r_ga r_sc r_c3 r_at r_ac r_mb r_e r_em r_qk r_c r_ch r_cl r_h r_hn "
                 "r_gv r_gr r_n x2_done dve_r act_r pool_r").split()
        (p_var, p_rstd, p_xn, p_xT, p_xh, p_xl, p_qk, p_roped, p_rot, p_hi, p_lo, p_tr, p_te, p_vp, p_vh, p_vev, dve_p, pool_p,
         s_done, m_done, q_rt, q_rte, t_done, e_done, k_done, ph_done, pl_done, av_done, n_done, o_t, o_h, o_l, w_done, x1_done, dve_q,
         c_hi, c_cp, r_var, r_rstd, r_xn, r_tr, r_th, r_tl, r_g, r_ga, r_sc, r_c3, r_at, r_ac, r_mb, r_e, r_em, r_qk, r_c, r_ch, r_cl, r_h, r_hn,
         r_gv, r_gr, r_n, x2_done, dve_r, act_r, pool_r) = map(sem, names)
        e_in = [sem(f"e_in{i}") for i in range(EB)]
        e_sum, e_hi, e_lo = map(sem, ("e_sum", "e_hi", "e_lo"))
        (f_var, f_rstd, f_u, f_xu, f_ut, f_uh, f_ul, f_rt, f_lg, f_sh, f_ex, f_g, f_gt, f_gte, f_base, f_quad, f_comb, f_fin,
         f_baseread, dve_f, pool_f) = map(sem, ("f_var f_rstd f_u f_xu f_ut f_uh f_ul f_rt f_lg f_sh f_ex f_g f_gt f_gte "
                                                "f_base f_quad f_comb f_fin f_baseread dve_f pool_f").split())
        out_sent = [sem("out_sent0"), sem("out_sent1")]

        def wait(eng, s, value):
            if not isinstance(value, int) or value > 0:
                eng.wait_ge(s, value)

        def held(eng, s):
            eng.sem_inc(s, 1)

        def pipeline(body, engine, lags=LAGS, peel=8):
            def step(i):
                return [Seq(i - d, (i - d) // 2, (i - d) % 2) if 0 <= i - d < B else None for d in range(lags)]

            for i in range(peel):
                body(step(i))
            with engine.Fori(peel // 2, B // 2) as it:
                for u in range(2):
                    body([Seq(it * 2 + (u - d), it + (u - d) // 2, (u - d) % 2) for d in range(lags)])
            for i in range(B, B + lags - 1):
                body(step(i))

        USES = {
            "ring": [("s3", 1, m_done, 6, 4), ("c1", 5, f_comb, 32, 8), ("tr", 3, r_tl, 1, 1),
                    ("c2", 5, f_comb, 32, 12), ("s4", 1, m_done, 6, 5), ("c3", 5, f_comb, 32, 16),
                    ("t0", 1, e_done, 6, 1), ("s5", 1, m_done, 6, 6), ("t1", 1, e_done, 6, 2),
                    ("c4", 5, f_comb, 32, 20), ("mb", 3, r_e, 1, 1), ("c5", 5, f_comb, 32, 24),
                    ("qk0", 3, r_c, 2, 1), ("t2", 1, e_done, 6, 3), ("s0", 0, m_done, 6, 1),
                    ("t3", 1, e_done, 6, 4), ("qk1", 3, r_c, 2, 2), ("c6", 5, f_comb, 32, 28),
                    ("t4", 1, e_done, 6, 5), ("s1", 0, m_done, 6, 2), ("c7", 5, f_comb, 32, 32),
                    ("s2", 0, m_done, 6, 3), ("c0", 4, f_comb, 32, 4), ("t5", 1, e_done, 6, 6)],
            "tp": [("xT", 0, p_xl, 1, 1), ("reT0", 1, q_rte, 2, 1), ("oT0", 2, o_l, 2, 1),
                  ("tq0", 0, p_te, 4, 1), ("oT1", 2, o_l, 2, 2), ("tk0", 0, p_te, 4, 2),
                  ("reT1", 1, q_rte, 2, 2), ("tq1", 0, p_te, 4, 3), ("uT", 4, f_ul, 1, 1),
                  ("tk1", 0, p_te, 4, 4)],
            "proj": [("qk0", 0, p_roped, 2, 1), ("v0", 0, p_vev, 2, 1), ("qk1", 0, p_roped, 2, 2),
                    ("v1", 0, p_vev, 2, 2), ("b0", 5, f_baseread, 2, 1), ("w0", 2, x1_done, 2, 1),
                    ("b1", 5, f_baseread, 2, 2), ("w1", 2, x1_done, 2, 2)],
            "obank": [("o0", 1, n_done, 2, 1), ("o1", 1, n_done, 2, 2)],
            "rbank": [("h0", 4, r_hn, 2, 1), ("h1", 4, r_hn, 2, 2), ("gates", 3, r_ga, 1, 1),
                     ("aT", 3, r_ac, 1, 1), ("rt", 4, f_lg, 1, 1), ("gT", 4, f_gte, 1, 1)],
        }
        LAG = {u[0]: u[1] for u in USES["ring"]}

        def ring_at(name, step):
            if name[0] == "c":
                return int(name[1:]) % 2 if isinstance(step, int) and step >= B + 3 else 0
            return 0 if isinstance(step, int) and step < 5 and name[0] in "sm" else 1

        def ring_of(b, name):
            return ring[ring_at(name, b.n + LAG[name])]

        def bank_free(pe, bank, name, seqs):
            now = next(s.n + d for d, s in enumerate(seqs) if s is not None)

            def uses(step):
                if bank != "ring":
                    return USES[bank]
                return [u for u in USES["ring"] if ring_at(u[0], step) == ring_at(name, now)]

            here = uses(now)
            at = [u[0] for u in here].index(name)
            before = [(now, u) for u in here[:at][::-1]]
            for back in range(1, LAGS if isinstance(now, int) else 2):
                before += [(now - back, u) for u in uses(now - back)[::-1]]
            for step, (_, lag, s, per, count) in before:
                n = step - lag
                if not isinstance(n, int) or 0 <= n < B:
                    wait(pe, s, n * per + count)
                    return

        def experts_of(seqs, count):
            first = EB * (seqs[0].n - 1) if seqs[0] and isinstance(seqs[0].n, int) else count
            return [k for k in range(first, first + EB) if 0 <= k < count]

        block = stack.enter_context(nc.Block())

        x_v = x.rearrange("b (t p) c -> b p t c", p=128)
        ctx_v = ctx.rearrange("b (t p) c -> b p t c", p=128)
        out_v = out.rearrange("b (t p) c -> b p t c", p=128)
        EXPERTS = NE + NS

        @block.sync
        def _(sp):
            sp.dma_start(xin[0][:], x_v[0]).then_inc(x_in[0], 16)
            sp.dma_start(wstage[:], w_qkv.rearrange("(c p) n -> p c n", p=128)).then_inc(w_in, 16)
            sp.dma_start(cos_t[:], rope_cos).then_inc(w_in, 16)
            sp.dma_start(sin_t[:], rope_sin).then_inc(w_in, 16)
            sp.dma_start(wostage[:], w_out.rearrange("(c p) n -> p c n", p=128)).then_inc(w_in, 16)
            sp.dma_start(gstage[:, 0], igk.rearrange("(c p) n -> p c n", p=128)).then_inc(w_in, 16)
            sp.dma_start(gstage[:, 1], fgk.rearrange("(c p) n -> p c n", p=128)).then_inc(w_in, 16)
            sp.dma_start(cent32[:], centT.rearrange("(c p) n -> p c n", p=128)).then_inc(w_in, 16)
            sp.wait_ge(zeros_in, 1)
            sp.dma_start(gbias[0:NHX, :], igb.rearrange("(h a) -> h a", a=1)).then_inc(misc_in, 16)
            sp.dma_start(gbias[32:32 + NHX, :], fgb.rearrange("(h a) -> h a", a=1)).then_inc(misc_in, 16)
            sp.dma_start(onorm_bc[:], onorm.partition_broadcast(128)).then_inc(misc_in, 16)
            sp.dma_start(ebias_bc[:], ebias.partition_broadcast(128)).then_inc(misc_in, 16)
            sp.dma_start(ball[0:NE, :], br).then_inc(misc_in, 16)
            sp.dma_start(ball[NE:NE + NS, :], bs).then_inc(misc_in, 16)

            def expert(k):
                if k >= EB:
                    sp.wait_ge(e_lo, k - EB + 1)
                src = WrT[:, k] if k < NE else WsT[:, k - NE]
                sp.dma_start(estage[:, k % EB], src.rearrange("(c p) o -> p c o", p=128)).then_inc(e_in[k % EB], 16)

            def body(seqs):
                b = seqs[7]
                if b:
                    sp.wait_ge(f_fin, 2 * b.n + 2)
                    sp.dma_start(out_v[b.n], fin[b.par][:]).then_inc(out_sent[b.par], 16)
                b = seqs[0]
                if b and not (isinstance(b.n, int) and b.n == 0):
                    wait(sp, p_xn, b.n - 1)
                    sp.dma_start(xin[b.par][:], x_v[b.n]).then_inc(x_in[b.par], 16)
                b = seqs[2]
                if b:
                    wait(sp, x1_done, 2 * (b.n - 1))
                    sp.dma_start(xres[b.par][:], x_v[b.n]).then_inc(xres_in[b.par], 16)
                b = seqs[3]
                if b:
                    wait(sp, r_tr, b.n - 1)
                    wait(sp, c_cp, b.n - 1)
                    sp.dma_start(ctx_t[b.par][:], ctx_v[b.n]).then_inc(ctx_in[b.par], 16)
                for k in experts_of(seqs, EXPERTS):
                    expert(k)

            pipeline(body, nc.sync, lags=8, peel=8)
            for i in range(2):
                sp.wait_ge(out_sent[i], 16 * (B // 2))

        @block.gpsimd
        def _(pool):
            g = nc.gpsimd
            chain = {}

            def link(ins, s, seq, per, key):
                chain[key] = chain.get(key, 0) % per + 1
                ins.then_inc(s, 1)
                pool.wait_ge(s, seq.n * per + chain[key])

            g.memset(ident[:], 0.0)
            g.memset(gsum[:], 0.0)
            g.memset(gbias[:], 0.0).then_inc(zeros_in, 1)
            pool.wait_ge(zeros_in, 1)
            g.affine_select(out=ident[:], in_=ident[:], compare_op=ALU.not_equal, fill=1.0, base=0,
                            pattern=[[-1, 128]], channel_multiplier=1).then_inc(zeros_in, 1)
            g.memset(causal[:], 0.0)
            g.memset(headsel[:], 0.0)
            g.memset(cmax3[:], 0.0)
            g.memset(mhalf[:], -0.5)
            g.memset(zero_ln[:], 0.0)
            g.memset(am[:], 0.0)
            g.memset(zero_row[:], 0.0)
            g.memset(gate[:], 0.5)
            g.memset(kst[:], 0.0)
            for i in range(2):
                g.memset(qst[i][:], 0.0)
                g.memset(v17_h[i][:], WS)
                g.memset(v17_l[i][:], 0.0)
                g.memset(ctx65_h[i][:], 1.0)
                g.memset(ctx65_l[i][:], 0.0)
            g.iota(iota16[:], pattern=[[1, NE]], base=0, channel_multiplier=0,
                   allow_small_or_imprecise_dtypes=True).then_inc(zeros_in, 1)
            pool.wait_ge(zeros_in, 3)
            g.memset(kst[:, :, :, 3 * DA:3 * DA + 1], 1.0)
            g.tensor_copy(ident16[:], ident[:])
            g.tensor_copy(identb[:], ident[:])
            g.affine_select(out=causal[:], in_=causal[:], compare_op=ALU.is_ge, fill=NEG, base=0,
                            pattern=[[0, 2], [-1, 128]], channel_multiplier=1)
            for piece in range(3):
                if piece:
                    pool.wait_ge(pool_ready, piece)
                g.affine_select(out=headsel[:], in_=headsel[:], compare_op=ALU.not_equal, fill=1.0, base=-32 * piece,
                                pattern=[[-1, NHX], [0, 128]], channel_multiplier=1).then_inc(pool_ready, 1)

            def rstd(dst, ve, mv, n, eps, ready, value, linked, done, shift=None):
                pool.wait_ge(ready, value)
                held(pool, pool_held)
                linked(g.tensor_scalar(ve, mv[:, :, 1], eps, None, ALU.add))
                last = g.tensor_tensor(dst, ve, mhalf[:, 0:n], ALU.pow)
                if shift is not None:
                    linked(last)
                    linked(g.tensor_tensor(shift, mv[:, :, 0], dst, ALU.mult))
                    last = g.tensor_tensor(shift, zero_ln[:], shift, ALU.subtract)
                last.then_inc(done, 1)

            def p_rstd_step(b):
                rstd(p_rs[:], p_ve[:], p_mv, NT, 1e-5, p_var, b.n + 1,
                     lambda i: link(i, pool_p, b, 3, "p"), p_rstd, p_off[:])

            def r_rstd_step(b):
                rstd(r_rs[:], r_ve[:], r_mv, NT, 1e-5, r_var, b.n + 1,
                     lambda i: link(i, pool_g, b, 3, "g"), r_rstd, r_off[:])

            def rotate(b, t):
                pool.wait_ge(p_roped, 2 * b.n + t + 1)
                wait(pool, p_lo, 2 * b.n + t)
                g.tensor_tensor(rot[:].rearrange("p s h d -> p (s h d)"), rope_a[:], rope_b[:], ALU.add).then_inc(p_rot, 1)

            def mask_probs(b, j):
                pool.wait_ge(e_done, JOBS * b.n + j + 1)
                held(pool, pool_held)
                if j < 2:
                    view = probs[j % 2][:, :].rearrange("p (a q) -> p a q", q=128)
                    pattern = [[0, 8], [1, 128]]
                else:
                    view = probs[j % 2][:, :].rearrange("p (a k q) -> p a k q", k=2, q=128)[:, :, 1, :]
                    pattern = [[0, 4], [1, 128]]
                g.affine_select(out=view, in_=view, compare_op=ALU.is_ge, fill=0.0, base=0, pattern=pattern,
                                channel_multiplier=-1).then_inc(k_done, 1)

            def probs_low(b, j):
                pool.wait_ge(ph_done, JOBS * b.n + j + 1)
                g.tensor_tensor(probs_l[j % PB][:], probs[j % 2][:], probs_h[j % PB][:], ALU.subtract).then_inc(pl_done, 1)

            def ctx_low(b):
                pool.wait_ge(c_hi, b.n + 1)
                for t in range(NT):
                    last = g.tensor_tensor(ctx65_l[b.par][:, t, :, 0:DX], ctx_t[b.par][:, t].rearrange("p (h d) -> p h d", h=NHX),
                                           ctx65_h[b.par][:, t, :, 0:DX], ALU.subtract)
                last.then_inc(c_cp, 1)

            def C_low(b, c):
                pool.wait_ge(r_ch, 2 * b.n + c + 1)
                heads = slice(2 * c, 2 * c + 2)
                g.tensor_tensor(C_l[:, heads], C_t[:, heads], C_h[:, heads], ALU.subtract).then_inc(r_cl, 1)

            def mask_E(b):
                pool.wait_ge(r_e, b.n + 1)
                held(pool, pool_held)
                for k in (0, 2):
                    view = E_t[:, :, bass.ts(k, 128)]
                    last = g.affine_select(out=view, in_=view, compare_op=ALU.is_ge, fill=0.0, base=0,
                                           pattern=[[0, NHX], [1, 128]], channel_multiplier=-1)
                last.then_inc(r_em, 1)

            def h_rstd_step(b):
                rstd(h_rs[:], h_ve[:], h_mv, NT * NHX, 1e-5, r_gv, b.n + 1,
                     lambda i: link(i, pool_r, b, 2, "r"), r_gr)

            def finish_r(b):
                pool.wait_ge(r_n, b.n + 1)
                link(g.tensor_tensor(hs[:], hh[:].rearrange("p t h d -> p t (h d)"),
                                     onorm_bc[:].unsqueeze(1).broadcast_to([128, NT, C]), ALU.mult), pool_r, b, 2, "r")
                wait(pool, f_xu, b.n)
                g.tensor_tensor(x2[:], hs[:], x1[b.par][:], ALU.add).then_inc(x2_done, 1)

            def f_rstd_step(b):
                rstd(f_rs[:], f_ve[:], f_mv, NT, 1e-5, f_var, b.n + 1,
                     lambda i: link(i, pool_f, b, 3, "f"), f_rstd, f_off[:])

            def f_sum(b):
                pool.wait_ge(f_u, b.n + 1)
                wait(pool, f_fin, 2 * (b.n - 1))
                g.tensor_tensor(xu[b.par][:], u_t[:], x2[:], ALU.add).then_inc(f_xu, 1)

            def close(b, t):
                pool.wait_ge(f_baseread, 2 * b.n + t + 1)
                pool.wait_ge(f_comb, 32 * b.n + 16 * (t + 1))
                if t == 0:
                    wait(pool, out_sent[b.par], 16 * b.half)
                g.tensor_tensor(fin[b.par][:, t], acc[:, t, 0], acc[:, t, 1], ALU.add).then_inc(f_fin, 1)

            pool.wait_ge(misc_in, 96)

            def body(seqs):
                l0, l1, l2, l3, l4, l5 = seqs
                if l0: p_rstd_step(l0)
                if l4: C_low(l4, 1)
                if l3: r_rstd_step(l3)
                if l2: probs_low(l2, 4)
                if l2: mask_probs(l2, 5)
                if l2: probs_low(l2, 5)
                if l4: h_rstd_step(l4)
                if l0: rotate(l0, 0)
                if l3: ctx_low(l3)
                if l1: mask_probs(l1, 0)
                if l1: probs_low(l1, 0)
                if l1: mask_probs(l1, 1)
                if l4: finish_r(l4)
                if l0: rotate(l0, 1)
                if l3: mask_E(l3)
                if l4: f_rstd_step(l4)
                if l1: probs_low(l1, 1)
                if l1: mask_probs(l1, 2)
                if l3: C_low(l3, 0)
                if l1: mask_probs(l1, 3)
                if l4: f_sum(l4)
                if l1: probs_low(l1, 2)
                if l1: probs_low(l1, 3)
                if l5: close(l5, 0)
                if l1: mask_probs(l1, 4)
                if l5: close(l5, 1)

            pipeline(body, nc.gpsimd)

        @block.scalar
        def _(act):
            a = nc.scalar
            a.preload_act_table_set("natural_log_exp_and_others")
            chain = {}

            def link(ins, seq):
                chain["r"] = chain.get("r", 0) % 3 + 1
                ins.then_inc(act_r, 1)
                act.wait_ge(act_r, 3 * seq.n + chain["r"])

            act.wait_ge(w_in, 112)
            act.wait_ge(g_sum, 2)
            for c in range(CH):
                a.activation(wqkv_h[:, c], wstage[:, c], ACT.Copy, scale=WS)
            a.activation(wo_h[:], wostage[:], ACT.Copy, scale=WS)
            a.activation(gw_h[:], gsum[:], ACT.Copy, scale=WS)
            a.activation(cent_h[:], cent32[:], ACT.Copy, scale=WS).then_inc(w_hi, 1)

            def expert_hi(seqs, place):
                for k in experts_of(seqs, NE + 1)[place:place + 1]:
                    if k < NE:
                        act.wait_ge(e_in[k % EB], 16 * (k // EB + 1))
                    else:
                        act.wait_ge(e_sum, 1)
                    a.activation(ew_h[:, :, k], estage[:, k % EB], ACT.Copy, scale=WS).then_inc(e_hi, 1)

            def normalize(dst, src, rs, shift, done):
                for t in range(NT):
                    last = a.activation(dst[:, t], src[:, t], ACT.Identity, scale=rs[:, t:t + 1], bias=shift[:, t:t + 1])
                last.then_inc(done, 1)

            def p_norm(b):
                act.wait_ge(p_rstd, b.n + 1)
                wait(act, p_xT, b.n)
                normalize(p_xn_t, xin[b.par], p_rs, p_off, p_xn)

            def r_norm(b):
                act.wait_ge(r_rstd, b.n + 1)
                wait(act, r_tr, b.n)
                normalize(r_xn_t, x1[b.par], r_rs, r_off, r_xn)

            def f_norm(b):
                act.wait_ge(f_rstd, b.n + 1)
                wait(act, f_ut, b.n)
                wait(act, f_xu, b.n)
                normalize(u_t, x2, f_rs, f_off, f_u)

            def xT_hi(b):
                act.wait_ge(p_xT, b.n + 1)
                wait(act, p_vp, 2 * b.n)
                a.activation(xT_h[:].rearrange("p c q -> p (c q)"), tp[:], ACT.Copy).then_inc(p_xh, 1)

            def high_parts(b, t):
                act.wait_ge(p_rot, 2 * b.n + t + 1)
                wait(act, q_rt, 2 * (b.n - 2) + t + 1)
                wait(act, p_tr, 4 * (b.n - 1) + 2 * t + 2)
                q_to = qst[b.par][:, t].rearrange("p h (a s) -> p h a s", a=2)[:, :, :, 0:DA]
                k_to = kst[:, t, :, 0:2 * DA].rearrange("p h (a s) -> p h a s", a=2)
                a.activation(q_to, rot[:, 0].unsqueeze(2).broadcast_to([128, NHA, 2, DA]), ACT.Copy)
                a.activation(k_to, rot[:, 1].unsqueeze(2).broadcast_to([128, NHA, 2, DA]), ACT.Copy).then_inc(p_hi, 1)

            def transposed(b, n):
                t, is_k = divmod(n, 2)
                act.wait_ge(p_tr, 4 * b.n + n + 1)
                wait(act, t_done if is_k else s_done, JOBS * (b.n - 1))
                dst = (kT if is_k else qT)[b.par]
                a.activation(dst[:, :, bass.ts(t, 128)], tp16, ACT.Copy).then_inc(p_te, 1)

            def v_out(b, t):
                act.wait_ge(p_vp, 2 * b.n + t + 1)
                wait(act, av_done, JOBS * (b.n - 1))
                a.activation(v17_h[b.par][:, t, :, 0:DA], proj[:, 0:C].rearrange("p (h d) -> p h d", h=NHA),
                             ACT.Copy).then_inc(p_vh, 1)

            def retransposed(b, t):
                act.wait_ge(q_rt, 2 * b.n + t + 1)
                wait(act, t_done, JOBS * (b.n - 1) + (2 if t == 0 else JOBS))
                a.activation(qmT[:, :, bass.ts(t, 128)], tp16, ACT.Copy).then_inc(q_rte, 1)

            def exp_job(b, j):
                act.wait_ge(t_done, JOBS * b.n + j + 1)
                wait(act, pl_done, JOBS * b.n + j - 1)
                a.activation(probs[j % 2][:], ring_of(b, f"t{j}")[:], ACT.Exp, scale=DA ** -0.5).then_inc(e_done, 1)

            def probs_high(b, j):
                act.wait_ge(k_done, JOBS * b.n + j + 1)
                wait(act, av_done, JOBS * b.n + j - PB + 1)
                a.activation(probs_h[j % PB][:], probs[j % 2][:], ACT.Copy).then_inc(ph_done, 1)

            def oT_hi(b, t):
                act.wait_ge(o_t, 2 * b.n + t + 1)
                wait(act, w_done, 2 * (b.n - 1) + t + 1)
                a.activation(oT_h[:, t].rearrange("p c q -> p (c q)"), tp[:, 0:C], ACT.Copy).then_inc(o_h, 1)

            def tr_hi(b):
                act.wait_ge(r_tr, b.n + 1)
                wait(act, r_qk, 2 * b.n)
                a.activation(tr_h[:].rearrange("p s c q -> p (s c q)"), ring_of(b, "tr")[:], ACT.Copy).then_inc(r_th, 1)

            def gate_acts(b):
                act.wait_ge(r_g, b.n + 1)
                wait(act, r_sc, b.n)
                link(a.activation(fg[:], rbank[32:32 + NHX, 0:T], ACT.Identity, scale=1.0 / WS, bias=gbias[32:32 + NHX, :]), b)
                a.activation(ig[:], rbank[0:NHX, 0:T], ACT.Identity, scale=1.0 / WS, bias=gbias[0:NHX, :])
                link(a.activation(fg_a[:], fg[:], ACT.Abs), b)
                link(a.activation(fg_e[:], fg_a[:], ACT.Exp, scale=-1.0), b)
                a.activation(fg_l[:], fg_e[:], ACT.Ln, bias=1.0).then_inc(r_ga, 1)

            def columns(b):
                act.wait_ge(r_at, b.n + 1)
                cols = rbank[:, 256:256 + NT * 36].rearrange("p (t n) -> p t n", t=NT)
                a.activation(acol[:], cols[:, :, 0:NHX], ACT.Copy)
                a.activation(emd[:], cols[:, :, 32:32 + NHX], ACT.Exp, scale=-1.0).then_inc(r_ac, 1)

            def decay(b):
                act.wait_ge(r_ac, b.n + 1)
                act.wait_ge(r_mb, b.n + 1)
                wait(act, r_c, 2 * b.n)
                mb = ring_of(b, "mb")[:].rearrange("p (h q) -> p h q", h=NHX)
                for h in range(NHX):
                    a.activation(E_t[:, h, 0:T], mb[:, h, :], ACT.Exp, scale=-1.0, bias=acol[:, 0, h:h + 1])
                    last = a.activation(E_t[:, h, T:T + 128], mb[:, h, 128:T], ACT.Exp, scale=-1.0, bias=acol[:, 1, h:h + 1])
                last.then_inc(r_e, 1)

            act.wait_ge(misc_in, 96)

            def uT_hi(b):
                act.wait_ge(f_ut, b.n + 1)
                wait(act, f_base, 2 * (b.n - 1))
                a.activation(uT_h[b.par][:].rearrange("p c q -> p (c q)"), tp[:], ACT.Copy).then_inc(f_uh, 1)

            def ctx_high(b):
                act.wait_ge(ctx_in[b.par], 16 * (b.half + 1))
                wait(act, r_h, 2 * (b.n - 1))
                for t in range(NT):
                    last = a.activation(ctx65_h[b.par][:, t, :, 0:DX], ctx_t[b.par][:, t].rearrange("p (h d) -> p h d", h=NHX), ACT.Copy)
                last.then_inc(c_hi, 1)

            def C_high(b, c):
                act.wait_ge(r_c, 2 * b.n + c + 1)
                heads = slice(2 * c, 2 * c + 2)
                if c == 0:
                    wait(act, r_h, 2 * b.n)
                a.activation(C_h[:, heads], C_t[:, heads], ACT.Copy).then_inc(r_ch, 1)

            def softmax_exp(b):
                act.wait_ge(f_sh, b.n + 1)
                a.activation(ex[:], lgs[:], ACT.Exp).then_inc(f_ex, 1)

            def gT_out(b):
                act.wait_ge(f_gt, b.n + 1)
                wait(act, f_base, 2 * b.n)
                a.activation(gT[:], rbank[0:NE + NS, 128:128 + T].rearrange("p (t q) -> p t q", t=NT), ACT.Copy).then_inc(f_gte, 1)

            def body(seqs):
                l0, l1, l2, l3, l4, l5 = seqs
                if l1: transposed(l1, 2)
                if l4: C_high(l4, 0)
                if l5: uT_hi(l5)
                if l2: exp_job(l2, 3)
                if l5: softmax_exp(l5)
                if l2: probs_high(l2, 2)
                if l1: transposed(l1, 3)
                if l2: probs_high(l2, 3)
                if l4: C_high(l4, 1)
                if l2: exp_job(l2, 4)
                expert_hi(seqs, 0)
                if l3: ctx_high(l3)
                expert_hi(seqs, 1)
                if l2: probs_high(l2, 4)
                if l0: p_norm(l0)
                if l5: gT_out(l5)
                if l2: exp_job(l2, 5)
                if l0: xT_hi(l0)
                if l3: r_norm(l3)
                if l3: tr_hi(l3)
                if l2: probs_high(l2, 5)
                expert_hi(seqs, 2)
                if l1: retransposed(l1, 0)
                if l3: gate_acts(l3)
                if l2: oT_hi(l2, 0)
                if l0: high_parts(l0, 0)
                if l1: exp_job(l1, 0)
                if l0: v_out(l0, 0)
                if l1: probs_high(l1, 0)
                if l0: transposed(l0, 0)
                if l1: exp_job(l1, 1)
                if l2: oT_hi(l2, 1)
                if l1: probs_high(l1, 1)
                if l3: columns(l3)
                if l3: decay(l3)
                if l0: transposed(l0, 1)
                if l0: high_parts(l0, 1)
                if l1: retransposed(l1, 1)
                expert_hi(seqs, 3)
                if l0: v_out(l0, 1)
                if l4: f_norm(l4)
                if l1: exp_job(l1, 2)

            pipeline(body, nc.scalar)

        @block.vector
        def _(dve):
            v = nc.vector
            chain = {}

            def link(ins, s, seq, per, key):
                chain[key] = chain.get(key, 0) % per + 1
                ins.then_inc(s, 1)
                dve.wait_ge(s, seq.n * per + chain[key])

            dve.wait_ge(w_in, 112)
            dve.wait_ge(zeros_in, 2)
            for k, col in ((0, 0), (1, 32)):
                v.tensor_copy(gsum[:, 0:CH, col:col + NHX], gstage[:, k, 0:CH])
                v.tensor_tensor(gsum[:, CH:2 * CH, col:col + NHX], gstage[:, k, CH:2 * CH], gstage[:, k, 2 * CH:3 * CH],
                                ALU.add).then_inc(g_sum, 1)
            dve.wait_ge(g_sum, 2)
            dve.wait_ge(w_hi, 1)
            for lo, w, hi in ((wqkv_l, wstage, wqkv_h), (wo_l, wostage, wo_h), (gw_l, gsum, gw_h), (cent_l, cent32, cent_h)):
                last = v.scalar_tensor_tensor(lo[:].rearrange("p c n -> p (c n)"), w[:].rearrange("p c n -> p (c n)"), WS,
                                              hi[:].rearrange("p c n -> p (c n)"), ALU.mult, ALU.subtract)
            last.then_inc(w_lo, 1)
            dve.wait_ge(misc_in, 96)
            v.tensor_scalar(ball[:], ball[:], 2.0 * WS, None, ALU.mult).then_inc(w_lo, 1)

            def ln_stats(src, stats, mv, s, seq, per, key, done):
                for t in range(NT):
                    ins = v.bn_stats(stats[:, t], src[:, t])
                link(ins, s, seq, per, key)
                held(dve, dve_held)
                for t in range(NT):
                    ins = v.bn_aggr(mv[:, t], stats[:, t])
                ins.then_inc(done, 1)

            def expert_lo(seqs, place):
                for k in experts_of(seqs, NE + 1)[place:place + 1]:
                    w = estage[:, k % EB]
                    if k == NE:
                        for i in (k, k + 1):
                            dve.wait_ge(e_in[i % EB], 16 * (i // EB + 1))
                        v.tensor_tensor(w, w, estage[:, (k + 1) % EB], ALU.add).then_inc(e_sum, 1)
                    dve.wait_ge(e_hi, k + 1)
                    v.scalar_tensor_tensor(ew_l[:, :, k], w, WS, ew_h[:, :, k], ALU.mult, ALU.subtract).then_inc(e_lo, 1)

            def p_xlo(b):
                dve.wait_ge(p_xh, b.n + 1)
                v.tensor_tensor(xT_l[:].rearrange("p c q -> p (c q)"), tp[:], xT_h[:].rearrange("p c q -> p (c q)"),
                                ALU.subtract).then_inc(p_xl, 1)

            def p_rope(b, t):
                dve.wait_ge(p_qk, 2 * b.n + t + 1)
                qk = proj[:].rearrange("p (h i two) -> p h i two", h=2 * NHA, two=2)

                def table(tab):
                    return tab[:, t].rearrange("p (i two) -> p i two", two=2).unsqueeze(1).broadcast_to([128, 2 * NHA, DA // 2, 2])

                wait(dve, p_rot, 2 * b.n + t)
                shape = "p (h i two) -> p h i two"
                v.tensor_tensor(rope_a[:].rearrange(shape, h=2 * NHA, two=2), qk, table(cos_t), ALU.mult)
                v.tensor_tensor(rope_b[:].rearrange(shape, h=2 * NHA, two=2), qk[:, :, :, ::-1], table(sin_t),
                                ALU.mult).then_inc(p_roped, 1)

            def p_low(b, t):
                dve.wait_ge(p_hi, 2 * b.n + t + 1)
                v.tensor_tensor(qst[b.par][:, t, :, DA:2 * DA], rot[:, 0], qst[b.par][:, t, :, 0:DA], ALU.subtract)
                v.tensor_tensor(kst[:, t, :, 2 * DA:3 * DA], rot[:, 1], kst[:, t, :, 0:DA], ALU.subtract).then_inc(p_lo, 1)

            def v_low(b, t):
                dve.wait_ge(p_vh, 2 * b.n + t + 1)
                v.tensor_tensor(v17_l[b.par][:, t, :, 0:DA], proj[:, 0:C].rearrange("p (h d) -> p h d", h=NHA),
                                v17_h[b.par][:, t, :, 0:DA], ALU.subtract).then_inc(p_vev, 1)

            def max_job(b, j):
                dve.wait_ge(s_done, JOBS * b.n + j + 1)
                src = ring_of(b, f"s{j}")
                if j < 2:
                    t, pairs, keys = 0, slice(4 * j, 4 * j + 4), 128
                else:
                    t, pairs, keys = 1, slice(2 * (j - 2), 2 * (j - 2) + 2), T
                to = qst[b.par][:, t].rearrange("p (k r) s -> p r k s", r=2)[:, :, pairs, 3 * DA]
                v.tensor_reduce(to, src[:].rearrange("p (r k q) -> p r k q", r=2, q=keys), axis=AX.X, op=ALU.max,
                                negate=True).then_inc(m_done, 1)

            def o_norm(b, t):
                dve.wait_ge(av_done, JOBS * b.n + (2 if t == 0 else JOBS))
                wait(dve, o_t, 2 * (b.n - 1) + t + 1)
                o = obank[:, 0:NHA * (DA + 1)].rearrange("p (h d) -> p h d", h=NHA)
                link(v.reciprocal(rec[:, t], o[:, :, DA]), dve_q, b, 2, "q")
                v.tensor_tensor(o_n[:, t].rearrange("p (h d) -> p h d", h=NHA), o[:, :, 0:DA],
                                rec[:, t].unsqueeze(2).broadcast_to([128, NHA, DA]), ALU.mult).then_inc(n_done, 1)

            def oT_lo(b, t):
                dve.wait_ge(o_h, 2 * b.n + t + 1)
                v.tensor_tensor(oT_l[:, t].rearrange("p c q -> p (c q)"), tp[:, 0:C], oT_h[:, t].rearrange("p c q -> p (c q)"),
                                ALU.subtract).then_inc(o_l, 1)

            def residual(b, t):
                if t == 0:
                    dve.wait_ge(xres_in[b.par], 16 * (b.half + 1))
                    wait(dve, x2_done, b.n - 1)
                dve.wait_ge(w_done, 2 * b.n + t + 1)
                v.scalar_tensor_tensor(x1[b.par][:, t], proj[:, 0:C], 1.0 / WS, xres[b.par][:, t], ALU.mult,
                                       ALU.add).then_inc(x1_done, 1)

            def r_stats_step(b):
                dve.wait_ge(x1_done, 2 * b.n + 2)
                ln_stats(x1[b.par], r_stats, r_mv, dve_g, b, KG, "g", r_var)

            def tr_lo(b):
                dve.wait_ge(r_th, b.n + 1)
                v.tensor_tensor(tr_l[:].rearrange("p s c q -> p (s c q)"), ring_of(b, "tr")[:],
                                tr_h[:].rearrange("p s c q -> p (s c q)"), ALU.subtract).then_inc(r_tl, 1)

            def scans(b):
                dve.wait_ge(r_ga, b.n + 1)
                wait(dve, r_mb, b.n)
                link(v.scalar_tensor_tensor(lsig[:], fg[:], 0.0, fg_l[:], ALU.min, ALU.subtract), dve_g, b, KG, "g")
                link(v.tensor_tensor_scan(cs[:], lsig[:], zero_row[:], 0.0, ALU.add, ALU.add), dve_g, b, KG, "g")
                link(v.tensor_tensor(am[0:NHX, :], ig[:], cs[:], ALU.subtract), dve_g, b, KG, "g")
                link(v.tensor_tensor_scan(cmax[:], am[0:NHX, :], am[0:NHX, :], -3e38, ALU.max, ALU.max), dve_g, b, KG, "g")
                v.tensor_tensor(am[32:32 + NHX, :], cs[:], cmax[:], ALU.add).then_inc(r_sc, 1)
                hi, mid, lo = (cmax3[32 * k:32 * k + NHX, :] for k in range(3))
                link(v.tensor_copy(hi, cmax[:]), dve_g, b, KG, "g")
                link(v.tensor_tensor(cmax_r[:], cmax[:], hi, ALU.subtract), dve_g, b, KG, "g")
                link(v.tensor_copy(mid, cmax_r[:]), dve_g, b, KG, "g")
                v.tensor_tensor(lo, cmax_r[:], mid, ALU.subtract).then_inc(r_c3, 1)

            def weigh(b, c):
                if c == 0:
                    dve.wait_ge(r_em, b.n + 1)
                    wait(dve, r_cl, 2 * b.n)
                dve.wait_ge(r_qk, 2 * b.n + c + 1)
                src = ring_of(b, f"qk{c}")[:].rearrange("p (r q) -> p r q", r=2)[:, :, 0:384]
                v.scalar_tensor_tensor(C_t[:, 2 * c:2 * c + 2], src, DX ** -0.5, E_t[:, 2 * c:2 * c + 2], ALU.mult,
                                       ALU.mult).then_inc(r_c, 1)

            def h_scale(b, t):
                dve.wait_ge(r_h, 2 * b.n + t + 1)
                if t == 0:
                    wait(dve, x2_done, b.n)
                H = rbank[:, 0:NHX * (DX + 1)].rearrange("p (h d) -> p h d", h=NHX)
                link(v.scalar_tensor_tensor(nre[:, t], H[:, :, DX], -1.0, emd[:, t], ALU.mult, ALU.max), dve_r, b, KR, "h")
                link(v.tensor_tensor(nrm[:, t], H[:, :, DX], nre[:, t], ALU.max), dve_r, b, KR, "h")
                link(v.tensor_scalar(nre[:, t], nrm[:, t], 1e-6, None, ALU.add), dve_r, b, KR, "h")
                link(v.reciprocal(nrr[:, t], nre[:, t]), dve_r, b, KR, "h")
                v.tensor_tensor(hh[:, t], H[:, :, 0:DX], nrr[:, t].unsqueeze(2).broadcast_to([128, NHX, DX]),
                                ALU.mult).then_inc(r_hn, 1)

            def h_stats_step(b):
                dve.wait_ge(r_hn, 2 * b.n + 2)
                for k in range(NT * NHX):
                    ins = v.bn_stats(h_stats[:, k], hc[:, k])
                link(ins, dve_r, b, KR, "h")
                held(dve, dve_held)
                for k in range(NT * NHX):
                    ins = v.bn_aggr(h_mv[:, k], h_stats[:, k])
                ins.then_inc(r_gv, 1)
                dve.wait_ge(r_gv, b.n + 1)
                link(v.tensor_tensor(hc, hc,
                                     h_mv[:, :, 0:1].broadcast_to([128, NT * NHX, DX]), ALU.subtract), dve_r, b, KR, "h")

            def h_norm(b):
                dve.wait_ge(r_gr, b.n + 1)
                v.tensor_tensor(hn, hc, h_rs[:].unsqueeze(2).broadcast_to([128, NT * NHX, DX]), ALU.mult).then_inc(r_n, 1)

            KG = 1 + 7
            KR = 8 + 2

            def p_stats_step(b):
                dve.wait_ge(x_in[b.par], 16 * (b.half + 1))
                ln_stats(xin[b.par], p_stats, p_mv, dve_p, b, 1, "p", p_var)

            def f_stats_step(b):
                dve.wait_ge(x2_done, b.n + 1)
                ln_stats(x2, f_stats, f_mv, dve_f, b, KF, "f", f_var)

            def uT_lo(b):
                dve.wait_ge(f_uh, b.n + 1)
                v.tensor_tensor(uT_l[b.par][:].rearrange("p c q -> p (c q)"), tp[:], uT_h[b.par][:].rearrange("p c q -> p (c q)"),
                                ALU.subtract).then_inc(f_ul, 1)

            def flink(ins, b):
                link(ins, dve_f, b, KF, "f")

            def logits(b):
                dve.wait_ge(f_rt, b.n + 1)
                rt = rbank[:, 0:NT * NE].rearrange("p (t e) -> p t e", t=NT)
                v.scalar_tensor_tensor(lg[:], rt, 1.0 / WS, ebias_bc[:].unsqueeze(1).broadcast_to([128, NT, NE]), ALU.mult,
                                       ALU.add).then_inc(f_lg, 1)
                dve.wait_ge(f_lg, b.n + 1)
                held(dve, dve_held)
                for t in range(NT):
                    last = v.max(mx8[:, t], lg[:, t])
                flink(last, b)
                v.tensor_tensor(lgs[:], lg[:], mx8[:, :, 0:1].broadcast_to([128, NT, NE]), ALU.subtract).then_inc(f_sh, 1)

            def top_two(b):
                dve.wait_ge(f_ex, b.n + 1)
                flink(v.tensor_reduce(exsum[:], ex[:], axis=AX.X, op=ALU.add), b)
                flink(v.reciprocal(exrec[:], exsum[:]), b)
                flink(v.tensor_tensor(sm[:], ex[:], exrec[:].unsqueeze(2).broadcast_to([128, NT, NE]), ALU.mult), b)
                held(dve, dve_held)
                for t in range(NT):
                    last = v.max(top8[:, t], sm[:, t])
                flink(last, b)

            def select(b):
                held(dve, dve_held)
                for t in range(NT):
                    last = v.max_index(idx8[:, t], top8[:, t], sm[:, t])
                flink(last, b)
                flink(v.tensor_copy(idxf[:], idx8[:, :, 0:2]), b)
                for t in range(NT):
                    v.tensor_scalar(g1[:, t], iota16[:], idxf[:, t, 0:1], top8[:, t, 0:1], ALU.is_equal, ALU.mult)
                    last = v.tensor_scalar(g2[:, t], iota16[:], idxf[:, t, 1:2], top8[:, t, 1:2], ALU.is_equal, ALU.mult)
                flink(last, b)
                wait(dve, f_gt, b.n)
                flink(v.tensor_tensor(gate[:, :, 0:NE], g1[:], g2[:], ALU.add), b)
                wait(dve, f_fin, 2 * (b.n - 1))
                v.tensor_scalar(gsc[b.par][:], gate[:, :, 0:NE], 1.0 / WS, None, ALU.mult).then_inc(f_g, 1)

            KF = 1 + 1 + 8

            def combine(b, q):
                t, quad = divmod(q, 4)
                if q == 0:
                    dve.wait_ge(f_g, b.n + 1)
                    dve.wait_ge(f_xu, b.n + 1)
                if quad == 0:
                    wait(dve, f_fin, 2 * (b.n - 1) + t + 1)
                dve.wait_ge(f_quad, 8 * b.n + q + 1)
                src = ring_of(b, f"c{q}")[:].rearrange("p (e c) -> p e c", e=4)
                for k in range(4):
                    e = 4 * quad + k
                    to, g = acc[:, t, k % 2], gsc[b.par][:, t, e:e + 1]
                    if e == 1:
                        ins = v.tensor_scalar(to, src[:, k], g, None, ALU.mult)
                    else:
                        if t == 1 and e == 12:
                            dve.wait_ge(f_baseread, 2 * b.n + 2)
                        elif e >= 2:
                            dve.wait_ge(f_comb, 32 * b.n + 16 * t + e - 1)
                        ins = v.scalar_tensor_tensor(to, src[:, k], g, xu[b.par][:, t] if e == 0 else to, ALU.mult, ALU.add)
                    ins.then_inc(f_comb, 1)

            def add_base(b, t):
                dve.wait_ge(f_base, 2 * b.n + t + 1)
                dve.wait_ge(f_comb, 32 * b.n + (16 if t == 0 else 28))
                v.scalar_tensor_tensor(acc[:, t, 0], proj[:, 0:C], 0.5 / WS, acc[:, t, 0], ALU.mult, ALU.add).then_inc(f_baseread, 1)

            def body(seqs):
                l0, l1, l2, l3, l4, l5 = seqs
                if l0: p_stats_step(l0)
                if l1: max_job(l1, 2)
                if l3: residual(l3, 1)
                if l3: r_stats_step(l3)
                expert_lo(seqs, 0)
                if l5: combine(l5, 0)
                if l4: h_scale(l4, 0)
                if l0: p_xlo(l0)
                if l1: max_job(l1, 3)
                if l5: combine(l5, 1)
                if l4: h_scale(l4, 1)
                if l3: tr_lo(l3)
                if l4: h_stats_step(l4)
                if l5: combine(l5, 2)
                if l0: p_rope(l0, 0)
                if l4: h_norm(l4)
                if l1: max_job(l1, 4)
                if l2: o_norm(l2, 1)
                if l2: oT_lo(l2, 0)
                if l0: p_low(l0, 0)
                if l5: combine(l5, 3)
                if l0: v_low(l0, 0)
                if l1: max_job(l1, 5)
                if l3: scans(l3)
                expert_lo(seqs, 1)
                if l2: oT_lo(l2, 1)
                if l5: combine(l5, 4)
                if l0: p_rope(l0, 1)
                if l4: f_stats_step(l4)
                if l0: p_low(l0, 1)
                if l3: weigh(l3, 0)
                if l0: v_low(l0, 1)
                if l5: combine(l5, 5)
                expert_lo(seqs, 2)
                if l0: max_job(l0, 0)
                expert_lo(seqs, 3)
                if l5: add_base(l5, 0)
                if l4: uT_lo(l4)
                if l1: o_norm(l1, 0)
                if l4: logits(l4)
                if l2: residual(l2, 0)
                if l4: top_two(l4)
                if l3: weigh(l3, 1)
                if l5: combine(l5, 6)
                if l4: select(l4)
                if l5: add_base(l5, 1)
                if l0: max_job(l0, 1)
                if l5: combine(l5, 7)

            pipeline(body, nc.vector)

        @block.tensor
        def _(pe):
            m = nc.tensor

            def split_product(dst, pieces, skip=False):
                for k, (lhsT, rhs) in enumerate(pieces):
                    last = m.matmul(dst, lhsT, rhs, start=k == 0, stop=k == len(pieces) - 1)
                return last

            def xT(b):
                pe.wait_ge(p_xn, b.n + 1)
                for c in range(CH):
                    for t in range(NT):
                        last = m.transpose(tp[:, bass.ds(c * T + t * 128, 128)], p_xn_t[:, t, bass.ts(c, 128)], ident[:])
                last.then_inc(p_xT, 1)

            def project(b, t, cols, done):
                if t == 0:
                    pe.wait_ge(p_xl, b.n + 1)
                q = bass.ts(t, 128)
                pieces = []
                for c in range(CH):
                    pieces += [(xT_h[:, c, q], wqkv_h[:, c, cols]), (xT_h[:, c, q], wqkv_l[:, c, cols]),
                               (xT_l[:, c, q], wqkv_h[:, c, cols])]
                split_product(proj[:, 0:cols.stop - cols.start], pieces).then_inc(done, 1)

            def transpose_heads(src, t, done):
                for k in range(NP):
                    last = m.transpose(tp16[:, k], src[:, t, 2 * k:2 * k + 2].rearrange("p r s -> p (r s)"), ident16[:])
                last.then_inc(done, 1)

            def scores(b, j):
                bank_free(pe, "ring", f"s{j}", cur[0])
                if j in (0, 2):
                    pe.wait_ge(p_te, 4 * b.n + (2 if j == 0 else 4))
                if j < 2:
                    t, pairs, keys, per = 0, range(4 * j, 4 * j + 4), 128, 4
                else:
                    t, pairs, keys, per = 1, range(2 * (j - 2), 2 * (j - 2) + 2), T, 2
                out4 = ring_of(b, f"s{j}")[:].rearrange("p (r k q) -> p r k q", r=2, q=keys)
                for r in range(2):
                    for h2 in range(0, per, 2):
                        m.matmul(out4[:, r, h2:h2 + 2, keys - 128:keys], identb[:], causal[:], start=h2 == 0, stop=False,
                                 skip_group_check=True)
                for k, pair in enumerate(pairs):
                    for r in range(2):
                        rows = slice(64 * r, 64 * r + 3 * DA)
                        last = m.matmul(out4[:, r, k], qT[b.par][rows, pair, bass.ts(t, 128)], kT[b.par][rows, pair, 0:keys],
                                        start=False, stop=True, skip_group_check=True)
                last.then_inc(s_done, 1)

            def reT(b, t):
                pe.wait_ge(m_done, JOBS * b.n + (2 if t == 0 else JOBS))
                transpose_heads(qst[b.par], t, q_rt)

            def scoresT(b, j):
                bank_free(pe, "ring", f"t{j}", cur[0])
                if j in (0, 2):
                    pe.wait_ge(q_rte, 2 * b.n + (1 if j == 0 else 2))
                if j < 2:
                    out4 = ring_of(b, f"t{j}")[:].rearrange("p (r k a q) -> p r k a q", r=2, k=4, a=1)
                    t, pairs = 0, range(4 * j, 4 * j + 4)
                else:
                    out4 = ring_of(b, f"t{j}")[:].rearrange("p (r k a q) -> p r k a q", r=2, k=2, a=2)
                    t, pairs = 1, range(2 * (j - 2), 2 * (j - 2) + 2)
                for k, pair in enumerate(pairs):
                    for kt in range(t + 1):
                        for r in range(2):
                            rows = slice(64 * r, 64 * r + 64)
                            last = m.matmul(out4[:, r, k, kt], kT[b.par][rows, pair, bass.ts(kt, 128)],
                                            qmT[rows, pair, bass.ts(t, 128)], start=True, stop=True)
                last.then_inc(t_done, 1)

            def values(b, j):
                if j in (0, 2):
                    bank_free(pe, "obank", "o0" if j == 0 else "o1", cur[0])
                    pe.wait_ge(p_vev, 2 * b.n + (1 if j == 0 else 2))
                pe.wait_ge(pl_done, JOBS * b.n + j + 1)
                o = obank[:, 0:NHA * (DA + 1)].rearrange("p (h d) -> p h d", h=NHA)
                t = 0 if j < 2 else 1
                pairs = range(4 * j, 4 * j + 4) if j < 2 else range(2 * (j - 2), 2 * (j - 2) + 2)
                ph, pl = (x[j % PB][:].rearrange("p (r k a q) -> p r k a q", r=2, k=len(pairs), q=128) for x in (probs_h, probs_l))
                vh, vl = v17_h[b.par], v17_l[b.par]
                for r in range(2):
                    for k, pair in enumerate(pairs):
                        head = 2 * pair + r
                        pieces = []
                        for kt in range(t + 1):
                            hi, lo = ph[:, r, k, kt], pl[:, r, k, kt]
                            pieces += [(hi, vh[:, kt, head]), (hi, vl[:, kt, head]), (lo, vh[:, kt, head])]
                        last = split_product(o[:, head], pieces)
                last.then_inc(av_done, 1)

            def oT(b, t):
                pe.wait_ge(n_done, 2 * b.n + t + 1)
                for c in range(CH):
                    last = m.transpose(tp[:, bass.ts(c, 128)], o_n[:, t, bass.ts(c, 128)], ident[:])
                last.then_inc(o_t, 1)

            def project_out(b, t):
                pe.wait_ge(o_l, 2 * b.n + t + 1)
                pieces = []
                for c in range(CH):
                    pieces += [(oT_h[:, t, c], wo_h[:, c]), (oT_h[:, t, c], wo_l[:, c]), (oT_l[:, t, c], wo_h[:, c])]
                split_product(proj[:, 0:C], pieces).then_inc(w_done, 1)

            def tr(b):
                bank_free(pe, "ring", "tr", cur[0])
                pe.wait_ge(ctx_in[b.par], 16 * (b.half + 1))
                pe.wait_ge(r_xn, b.n + 1)
                to = ring_of(b, "tr")[:].rearrange("p (s c q) -> p s c q", s=2, c=CH)
                for s, src in ((0, ctx_t[b.par]), (1, r_xn_t)):
                    for c in range(CH):
                        for t in range(NT):
                            last = m.transpose(to[:, s, c, bass.ts(t, 128)], src[:, t, bass.ts(c, 128)], ident[:])
                last.then_inc(r_tr, 1)

            def gates(b):
                bank_free(pe, "rbank", "gates", cur[0])
                pe.wait_ge(r_tl, b.n + 1)
                pieces = []
                for s, w0 in ((1, 0), (0, CH)):
                    for c in range(CH):
                        pieces += [(gw_h[:, w0 + c], tr_h[:, s, c]), (gw_h[:, w0 + c], tr_l[:, s, c]), (gw_l[:, w0 + c], tr_h[:, s, c])]
                split_product(rbank[0:36, 0:T], pieces).then_inc(r_g, 1)

            def aT(b):
                bank_free(pe, "rbank", "aT", cur[0])
                pe.wait_ge(r_sc, b.n + 1)
                held(pe, pe_held)
                for t in range(NT):
                    last = m.transpose(rbank[:, 256 + 36 * t:256 + 36 * t + 36], am[:, bass.ts(t, 128)], ident[0:36, 0:36])
                last.then_inc(r_at, 1)

            def mb(b):
                bank_free(pe, "ring", "mb", cur[0])
                pe.wait_ge(r_c3, b.n + 1)
                to = ring_of(b, "mb")[:].rearrange("p (h q) -> p h q", h=NHX)
                for h in range(NHX):
                    last = m.matmul(to[:, h], headsel[:, h], cmax3[:], start=True, stop=True)
                last.then_inc(r_mb, 1)

            def xqk(b, c):
                bank_free(pe, "ring", f"qk{c}", cur[0])
                to = ring_of(b, f"qk{c}")[:].rearrange("p (r q) -> p r q", r=2)
                for kt in range(NT):
                    for n, (kp, xp) in enumerate(((tr_h, tr_h), (tr_l, tr_h), (tr_h, tr_l))):
                        for r in range(2):
                            rows = slice(64 * r, 64 * r + 64)
                            dst = to[:, r, 0:T] if kt == 0 else to[:, r, T:T + 128]
                            last = m.matmul(dst, kp[rows, 0, c, bass.ts(kt, 128)], xp[rows, 1, c, kt * 128:T], start=n == 0, stop=n == 2)
                last.then_inc(r_qk, 1)

            def xvalues(b, t):
                bank_free(pe, "rbank", f"h{t}", cur[0])
                if t == 0:
                    pe.wait_ge(r_cl, 2 * b.n + 2)
                    pe.wait_ge(c_cp, b.n + 1)
                H = rbank[:, 0:NHX * (DX + 1)].rearrange("p (h d) -> p h d", h=NHX)
                for h in range(NHX):
                    pieces = []
                    for kt in range(t + 1):
                        cols = slice(128 * t, 128 * t + 128) if kt == 0 else slice(256, 384)
                        hi, lo, ch, cl = C_h[:, h, cols], C_l[:, h, cols], ctx65_h[b.par][:, kt, h], ctx65_l[b.par][:, kt, h]
                        pieces += [(hi, ch), (hi, cl), (lo, ch)]
                    last = split_product(H[:, h], pieces)
                last.then_inc(r_h, 1)

            cur = [None]
            pe.wait_ge(pool_ready, 3)
            pe.wait_ge(w_lo, 2)

            def tp_use(name, st, fn, *args):
                bank_free(pe, "tp", name, st)
                fn(*args)

            def proj_use(name, st, fn, *args):
                bank_free(pe, "proj", name, st)
                fn(*args)

            def heads_of(b, t, is_k):
                if not is_k:
                    pe.wait_ge(p_lo, 2 * b.n + t + 1)
                transpose_heads(kst if is_k else qst[b.par], t, p_tr)

            QK, V = slice(0, 2 * C), slice(2 * C, 3 * C)

            def uT(b):
                pe.wait_ge(f_u, b.n + 1)
                for c in range(CH):
                    for t in range(NT):
                        last = m.transpose(tp[:, bass.ds(c * T + t * 128, 128)], u_t[:, t, bass.ts(c, 128)], ident[:])
                last.then_inc(f_ut, 1)

            def split_u(b, t, wh, wl):
                h, l, q = uT_h[b.par], uT_l[b.par], bass.ts(t, 128)
                return [x for c in range(CH) for x in ((h[:, c, q], wh(c)), (h[:, c, q], wl(c)), (l[:, c, q], wh(c)))]

            def router(b):
                bank_free(pe, "rbank", "rt", cur[0])
                pe.wait_ge(f_ul, b.n + 1)
                for t in range(NT):
                    last = split_product(rbank[:, bass.ts(t, NE)], split_u(b, t, lambda c: cent_h[:, c], lambda c: cent_l[:, c]))
                last.then_inc(f_rt, 1)

            def gates_T(b):
                bank_free(pe, "rbank", "gT", cur[0])
                pe.wait_ge(f_g, b.n + 1)
                for t in range(NT):
                    last = m.transpose(rbank[0:NE + NS, 128 + 128 * t:256 + 128 * t], gate[:, t], ident[:])
                last.then_inc(f_gt, 1)

            def base(b, t):
                pe.wait_ge(f_gte, b.n + 1)
                if isinstance(b.n, int) and b.n == 0 and t == 0:
                    pe.wait_ge(e_lo, NE + 1)
                pieces = split_u(b, t, lambda c: ew_h[:, c, NE], lambda c: ew_l[:, c, NE])
                split_product(proj[:, 0:C], pieces + [(gT[:, t], ball[:])]).then_inc(f_base, 1)

            def quad(b, q):
                bank_free(pe, "ring", f"c{q}", cur[0])
                if isinstance(b.n, int) and b.n == 0 and q == 0:
                    pe.wait_ge(e_lo, NE)
                t, k = divmod(q, 4)
                for half in range(2):
                    es = slice(4 * k + 2 * half, 4 * k + 2 * half + 2)
                    last = split_product(ring_of(b, f"c{q}")[:, bass.ts(half, 512)],
                                         split_u(b, t, lambda c: ew_h[:, c, es].rearrange("p e o -> p (e o)"),
                                                 lambda c: ew_l[:, c, es].rearrange("p e o -> p (e o)")))
                last.then_inc(f_quad, 1)

            def body(seqs):
                l0, l1, l2, l3, l4, l5 = cur[0] = seqs
                if l0: tp_use("xT", seqs, xT, l0)
                if l4: xvalues(l4, 0)
                if l1: scores(l1, 3)
                if l5: quad(l5, 1)
                if l4: xvalues(l4, 1)
                if l3: tr(l3)
                if l2: values(l2, 4)
                if l5: quad(l5, 2)
                if l0: proj_use("qk0", seqs, project, l0, 0, QK, p_qk)
                if l1: tp_use("reT0", seqs, reT, l1, 0)
                if l3: gates(l3)
                if l1: scores(l1, 4)
                if l2: tp_use("oT0", seqs, oT, l2, 0)
                if l2: values(l2, 5)
                if l5: quad(l5, 3)
                if l1: scoresT(l1, 0)
                if l0: proj_use("v0", seqs, project, l0, 0, V, p_vp)
                if l1: scores(l1, 5)
                if l0: tp_use("tq0", seqs, heads_of, l0, 0, False)
                if l0: proj_use("qk1", seqs, project, l0, 1, QK, p_qk)
                if l1: scoresT(l1, 1)
                if l2: tp_use("oT1", seqs, oT, l2, 1)
                if l5: quad(l5, 4)
                if l3: aT(l3)
                if l3: mb(l3)
                if l0: tp_use("tk0", seqs, heads_of, l0, 0, True)
                if l1: values(l1, 0)
                if l5: quad(l5, 5)
                if l1: tp_use("reT1", seqs, reT, l1, 1)
                if l3: xqk(l3, 0)
                if l0: proj_use("v1", seqs, project, l0, 1, V, p_vp)
                if l0: tp_use("tq1", seqs, heads_of, l0, 1, False)
                if l1: scoresT(l1, 2)
                if l5: proj_use("b0", seqs, base, l5, 0)
                if l0: scores(l0, 0)
                if l4: tp_use("uT", seqs, uT, l4)
                if l1: values(l1, 1)
                if l1: scoresT(l1, 3)
                if l2: proj_use("w0", seqs, project_out, l2, 0)
                if l4: router(l4)
                if l0: tp_use("tk1", seqs, heads_of, l0, 1, True)
                if l3: xqk(l3, 1)
                if l5: quad(l5, 6)
                if l1: scoresT(l1, 4)
                if l5: proj_use("b1", seqs, base, l5, 1)
                if l0: scores(l0, 1)
                if l5: quad(l5, 7)
                if l0: scores(l0, 2)
                if l2: proj_use("w1", seqs, project_out, l2, 1)
                if l1: values(l1, 2)
                if l4: quad(l4, 0)
                if l4: gates_T(l4)
                if l1: scoresT(l1, 5)
                if l1: values(l1, 3)

            pipeline(body, nc.tensor)


def kernel(**inputs):
    import numpy as np
    import concourse.bacc as bacc
    from concourse.bass_utils import run_bass_kernel_spmd as run

    def lay(a):
        return np.ascontiguousarray(a)

    inv = 1.0 / 10000.0 ** (np.arange(0, DA, 2, dtype=np.float32) / DA)
    ang = np.outer(np.arange(T, dtype=np.float32), inv.astype(np.float32)).astype(np.float32)
    cos = np.repeat(np.cos(ang), 2, axis=1) / WS
    sin = np.repeat(np.sin(ang), 2, axis=1) / WS * np.tile([-1.0, 1.0], DA // 2)
    def tiles(a):
        return lay(a.astype(np.float32).reshape(NT, 128, DA).transpose(1, 0, 2))

    arrays = {
        "x": lay(inputs["x"]), "ctx": lay(inputs["ctx_1024"]), "w_qkv": lay(inputs["L0_attn_w_qkv"]),
        "w_out": lay(inputs["L0_attn_w_out"]), "igk": lay(inputs["L0_xattn_igate_kernel"]),
        "igb": lay(inputs["L0_xattn_igate_bias"]), "fgk": lay(inputs["L0_xattn_fgate_kernel"]),
        "fgb": lay(inputs["L0_xattn_fgate_bias"]), "onorm": lay(inputs["L0_xattn_outnorm_scale"]),
        "centT": lay(np.asarray(inputs["L0_ffn_centroids"]).T), "ebias": lay(inputs["L0_ffn_expert_biases"]),
        "WrT": lay(np.asarray(inputs["L0_ffn_Wr"]).transpose(2, 0, 1)), "br": lay(inputs["L0_ffn_br"]),
        "WsT": lay(np.asarray(inputs["L0_ffn_Ws"]).transpose(2, 0, 1)), "bs": lay(inputs["L0_ffn_bs"]),
        "rope_cos": tiles(cos), "rope_sin": tiles(sin),
    }
    nc = bacc.Bacc("TRN2", target_bir_lowering=False, num_devices=1)
    args = [nc.dram_tensor(f"in_{k}", a.shape, mybir.dt.from_np(a.dtype), kind="ExternalInput").ap() for k, a in arrays.items()]
    args.append(nc.dram_tensor("out_y", (B, T, C), mybir.dt.float32, kind="ExternalOutput").ap())
    decoder_layer(nc, *args)
    r = run(nc, [{f"in_{k}": a for k, a in arrays.items()}], core_ids=[0])
    return r.results[0]["out_y"]
```
